# Optimizing a Trainium2 kernel written in Bass

```python
import numpy as np
import jax
import jax.numpy as jnp

def _softmax(x, axis=-1):
    return jax.nn.softmax(x, axis=axis)

def _gelu(x):
    return jax.nn.gelu(x, approximate=True)

def _silu(x):
    return jax.nn.silu(x)

def _sigmoid(x):
    return jax.nn.sigmoid(x)

def _layernorm(x, axis=-1, eps=1e-05):
    m = jnp.mean(x, axis=axis, keepdims=True)
    v = jnp.var(x, axis=axis, keepdims=True)
    return (x - m) / jnp.sqrt(v + eps)

def _scatter_add(tgt, idx, src, axis=0):
    return tgt.at[idx].add(src)

def _segment_sum(src, seg, n):
    return jax.ops.segment_sum(src, seg, n)
kernel_name = 'mk_vit_tower_d1_tok_img768_r4_ff21cc'

def setup_inputs(seed: int=0):
    np.random.seed(seed)
    _w = jnp.asarray

    def _rec_inputs():
        import jax
        import jax.numpy as jnp
        _rk = jax.random.key(seed)
        x = 7.57192e-06 + 1.00007 * jax.random.normal(jax.random.fold_in(_rk, 1), (32, 3, 96, 96), jnp.float32)
        return x
    x = _rec_inputs()

    def _L0_tok_setup():
        import jax, jax.numpy as jnp
        import numpy as np
        PATCH = 16

        def _shift2d(x, shift):
            l, r, t, b = shift
            H, W = (x.shape[2], x.shape[3])
            xp = jnp.pad(x, ((0, 0), (0, 0), (max(t, 0), max(b, 0)), (max(l, 0), max(r, 0))))
            h0 = max(-t, 0)
            w0 = max(-l, 0)
            return xp[:, :, h0:h0 + H, w0:w0 + W]
        key = jax.random.key(seed)
        k1, k2 = jax.random.split(key)
        B, C, H, W = (64, 3, 224, 224)
        dim = 192
        patch_dim = PATCH * PATCH * 5 * C
        x = jax.random.normal(k1, (B, C, H, W), dtype=jnp.float32)
        ln_weight = jnp.ones((patch_dim,), dtype=jnp.float32)
        ln_bias = jnp.zeros((patch_dim,), dtype=jnp.float32)
        proj_weight = jax.random.normal(k2, (dim, patch_dim), dtype=jnp.float32) * patch_dim ** (-0.5)
        proj_bias = jnp.zeros((dim,), dtype=jnp.float32)
        return {'x': x, 'ln_weight': ln_weight, 'ln_bias': ln_bias, 'proj_weight': proj_weight, 'proj_bias': proj_bias}
    _L0_tok_all = _L0_tok_setup()
    _L0_tok_in = {k: v for k, v in _L0_tok_all.items() if k in ('ln_weight', 'ln_bias', 'proj_weight', 'proj_bias')}
    del _L0_tok_all

    def _L0_attn_setup():
        import jax, jax.numpy as jnp
        import numpy as np
        B, T, C = (16, 512, 192)

        def _wkv(k, v, w, u):
            Bb, Tt, Cc = k.shape

            def step(carry, kv):
                num, den, mx = carry
                kt, vt = kv
                m_out = jnp.maximum(mx, kt + u)
                e1 = jnp.exp(mx - m_out)
                e2 = jnp.exp(kt + u - m_out)
                out = (e1 * num + e2 * vt) / (e1 * den + e2)
                m_new = jnp.maximum(mx + w, kt)
                e1s = jnp.exp(mx + w - m_new)
                e2s = jnp.exp(kt - m_new)
                return ((e1s * num + e2s * vt, e1s * den + e2s, m_new), out)
            init = (jnp.zeros((Bb, Cc), k.dtype), jnp.zeros((Bb, Cc), k.dtype), jnp.full((Bb, Cc), -1e+38, k.dtype))
            _, outs = jax.lax.scan(step, init, (jnp.swapaxes(k, 0, 1), jnp.swapaxes(v, 0, 1)))
            return jnp.swapaxes(outs, 0, 1)
        key = jax.random.key(seed)
        ks = jax.random.split(key, 10)
        s = 0.02
        return {'x': jax.random.normal(ks[0], (B, T, C), dtype=jnp.float32), 'time_decay': jax.random.normal(ks[1], (C,), dtype=jnp.float32) * 0.5, 'time_first': jax.random.normal(ks[2], (C,), dtype=jnp.float32) * 0.5, 'mix_k': jax.random.uniform(ks[3], (C,), dtype=jnp.float32), 'mix_v': jax.random.uniform(ks[4], (C,), dtype=jnp.float32), 'mix_r': jax.random.uniform(ks[5], (C,), dtype=jnp.float32), 'Wk': jax.random.normal(ks[6], (C, C), dtype=jnp.float32) * s, 'Wv': jax.random.normal(ks[7], (C, C), dtype=jnp.float32) * s, 'Wr': jax.random.normal(ks[8], (C, C), dtype=jnp.float32) * s, 'Wo': jax.random.normal(ks[9], (C, C), dtype=jnp.float32) * s}
    _L0_attn_all = _L0_attn_setup()
    _L0_attn_in = {k: v for k, v in _L0_attn_all.items() if k in ('time_decay', 'time_first', 'mix_k', 'mix_v', 'mix_r', 'Wk', 'Wv', 'Wr', 'Wo')}
    del _L0_attn_all

    def _L0_ffn_setup():
        import math
        import jax, jax.numpy as jnp
        import numpy as np
        B, L, D = (8, 1024, 192)
        E = 16
        TOP_K = 2
        F_EXP = 4 * D
        F_SH = F_EXP * 2 // 4
        key = jax.random.key(seed)
        ks = jax.random.split(key, 8)
        s = lambda fan_in: 1.0 / math.sqrt(fan_in)
        return {'hidden_states': jax.random.normal(ks[0], (B, L, D), jnp.float32), 'gate_weight': jax.random.uniform(ks[1], (E, D), jnp.float32, -s(D), s(D)), 'Wg': jax.random.uniform(ks[2], (E, F_EXP, D), jnp.float32, -s(D), s(D)), 'Wu': jax.random.uniform(ks[3], (E, F_EXP, D), jnp.float32, -s(D), s(D)), 'Wd': jax.random.uniform(ks[4], (E, D, F_EXP), jnp.float32, -s(F_EXP), s(F_EXP)), 'Ws_g': jax.random.uniform(ks[5], (F_SH, D), jnp.float32, -s(D), s(D)), 'Ws_u': jax.random.uniform(ks[6], (F_SH, D), jnp.float32, -s(D), s(D)), 'Ws_d': jax.random.uniform(ks[7], (D, F_SH), jnp.float32, -s(F_SH), s(F_SH))}
    _L0_ffn_all = _L0_ffn_setup()
    _L0_ffn_in = {k: v for k, v in _L0_ffn_all.items() if k in ('gate_weight', 'Wg', 'Wu', 'Wd', 'Ws_g', 'Ws_u', 'Ws_d')}
    del _L0_ffn_all
    return {'x': x, 'L0_tok_ln_weight': _L0_tok_in['ln_weight'], 'L0_tok_ln_bias': _L0_tok_in['ln_bias'], 'L0_tok_proj_weight': _L0_tok_in['proj_weight'], 'L0_tok_proj_bias': _L0_tok_in['proj_bias'], 'L0_attn_time_decay': _L0_attn_in['time_decay'], 'L0_attn_time_first': _L0_attn_in['time_first'], 'L0_attn_mix_k': _L0_attn_in['mix_k'], 'L0_attn_mix_v': _L0_attn_in['mix_v'], 'L0_attn_mix_r': _L0_attn_in['mix_r'], 'L0_attn_Wk': _L0_attn_in['Wk'], 'L0_attn_Wv': _L0_attn_in['Wv'], 'L0_attn_Wr': _L0_attn_in['Wr'], 'L0_attn_Wo': _L0_attn_in['Wo'], 'L0_ffn_gate_weight': _L0_ffn_in['gate_weight'], 'L0_ffn_Wg': _L0_ffn_in['Wg'], 'L0_ffn_Wu': _L0_ffn_in['Wu'], 'L0_ffn_Wd': _L0_ffn_in['Wd'], 'L0_ffn_Ws_g': _L0_ffn_in['Ws_g'], 'L0_ffn_Ws_u': _L0_ffn_in['Ws_u'], 'L0_ffn_Ws_d': _L0_ffn_in['Ws_d']}

def reference(x, L0_tok_ln_weight, L0_tok_ln_bias, L0_tok_proj_weight, L0_tok_proj_bias, L0_attn_time_decay, L0_attn_time_first, L0_attn_mix_k, L0_attn_mix_v, L0_attn_mix_r, L0_attn_Wk, L0_attn_Wv, L0_attn_Wr, L0_attn_Wo, L0_ffn_gate_weight, L0_ffn_Wg, L0_ffn_Wu, L0_ffn_Wd, L0_ffn_Ws_g, L0_ffn_Ws_u, L0_ffn_Ws_d):
    import jax
    import jax.numpy as jnp

    def _L0_tok_ref(x, ln_weight, ln_bias, proj_weight, proj_bias):
        import jax, jax.numpy as jnp
        import numpy as np
        PATCH = 16

        def _shift2d(x, shift):
            l, r, t, b = shift
            H, W = (x.shape[2], x.shape[3])
            xp = jnp.pad(x, ((0, 0), (0, 0), (max(t, 0), max(b, 0)), (max(l, 0), max(r, 0))))
            h0 = max(-t, 0)
            w0 = max(-l, 0)
            return xp[:, :, h0:h0 + H, w0:w0 + W]
        shifts = ((1, -1, 0, 0), (-1, 1, 0, 0), (0, 0, 1, -1), (0, 0, -1, 1))
        xc = jnp.concatenate([x] + [_shift2d(x, s) for s in shifts], axis=1)
        B, C5, H, W = xc.shape
        p = PATCH
        h, w = (H // p, W // p)
        t = xc.reshape(B, C5, h, p, w, p)
        t = t.transpose(0, 2, 4, 3, 5, 1).reshape(B, h * w, p * p * C5)
        mu = jnp.mean(t, axis=-1, keepdims=True)
        var = jnp.mean(jnp.square(t - mu), axis=-1, keepdims=True)
        tn = (t - mu) * jax.lax.rsqrt(var + 1e-05) * ln_weight + ln_bias
        return jnp.einsum('bnk,dk->bnd', tn, proj_weight) + proj_bias

    def _L0_attn_ref(x, time_decay, time_first, mix_k, mix_v, mix_r, Wk, Wv, Wr, Wo):
        import jax, jax.numpy as jnp
        import numpy as np
        B, T, C = (16, 512, 192)

        def _wkv(k, v, w, u):
            Bb, Tt, Cc = k.shape

            def step(carry, kv):
                num, den, mx = carry
                kt, vt = kv
                m_out = jnp.maximum(mx, kt + u)
                e1 = jnp.exp(mx - m_out)
                e2 = jnp.exp(kt + u - m_out)
                out = (e1 * num + e2 * vt) / (e1 * den + e2)
                m_new = jnp.maximum(mx + w, kt)
                e1s = jnp.exp(mx + w - m_new)
                e2s = jnp.exp(kt - m_new)
                return ((e1s * num + e2s * vt, e1s * den + e2s, m_new), out)
            init = (jnp.zeros((Bb, Cc), k.dtype), jnp.zeros((Bb, Cc), k.dtype), jnp.full((Bb, Cc), -1e+38, k.dtype))
            _, outs = jax.lax.scan(step, init, (jnp.swapaxes(k, 0, 1), jnp.swapaxes(v, 0, 1)))
            return jnp.swapaxes(outs, 0, 1)
        x_prev = jnp.pad(x, ((0, 0), (1, 0), (0, 0)))[:, :-1]
        k = jnp.einsum('btc,dc->btd', x * mix_k + x_prev * (1.0 - mix_k), Wk)
        v = jnp.einsum('btc,dc->btd', x * mix_v + x_prev * (1.0 - mix_v), Wv)
        r = jax.nn.sigmoid(jnp.einsum('btc,dc->btd', x * mix_r + x_prev * (1.0 - mix_r), Wr))
        w = -jnp.exp(time_decay)
        wkv = _wkv(k, v, w, time_first)
        return jnp.einsum('btc,dc->btd', r * wkv, Wo)

    def _L0_ffn_ref(hidden_states, gate_weight, Wg, Wu, Wd, Ws_g, Ws_u, Ws_d):
        import math
        import jax, jax.numpy as jnp
        import numpy as np
        B, L, D = (8, 1024, 192)
        E = 16
        TOP_K = 2
        F_EXP = 4 * D
        F_SH = F_EXP * 2 // 4
        b, l, d = hidden_states.shape
        n = b * l
        x = hidden_states.reshape(n, d)
        scores = jax.nn.sigmoid(x @ gate_weight.T)
        capacity = math.ceil(n / E * TOP_K)
        topk_score, topk_ids = jax.lax.top_k(scores.T, capacity)
        xg = x[topk_ids]
        gate = jax.nn.silu(jnp.einsum('ecd,efd->ecf', xg, Wg))
        up = jnp.einsum('ecd,efd->ecf', xg, Wu)
        out = jnp.einsum('ecf,edf->ecd', gate * up, Wd)
        out = out * topk_score[..., None]
        y = jnp.zeros((n, d), x.dtype).at[topk_ids.reshape(-1)].add(out.reshape(-1, d))
        y = y.reshape(b, l, d)
        shared = jax.nn.silu(hidden_states @ Ws_g.T) * (hidden_states @ Ws_u.T) @ Ws_d.T
        return y + shared
    h = _L0_tok_ref(x, L0_tok_ln_weight, L0_tok_ln_bias, L0_tok_proj_weight, L0_tok_proj_bias)
    h = h + _L0_attn_ref(_layernorm(h, axis=-1), L0_attn_time_decay, L0_attn_time_first, L0_attn_mix_k, L0_attn_mix_v, L0_attn_mix_r, L0_attn_Wk, L0_attn_Wv, L0_attn_Wr, L0_attn_Wo)
    h = h + _L0_ffn_ref(_layernorm(h, axis=-1), L0_ffn_gate_weight, L0_ffn_Wg, L0_ffn_Wu, L0_ffn_Wd, L0_ffn_Ws_g, L0_ffn_Ws_u, L0_ffn_Ws_d)
    return h

_drawn_inputs = setup_inputs


def setup_inputs(seed=0):
    import zlib

    import numpy as np

    out = dict(_drawn_inputs(seed))
    spreads = {'L0_tok_ln_weight': (1.0, 0.2),
     'L0_tok_ln_bias': (0.0, 0.1),
     'L0_tok_proj_bias': (0.0, 0.1)}
    factors = {'L0_attn_time_decay': 7.82,
     'L0_attn_time_first': 7.973,
     'L0_attn_mix_k': 8.0,
     'L0_attn_mix_v': 6.263,
     'L0_attn_mix_r': 8.0,
     'L0_attn_Wk': 8.0,
     'L0_attn_Wr': 8.0}
    for name, (base, spread) in spreads.items():
        noise = np.random.default_rng([zlib.crc32(name.encode()), seed]).standard_normal(out[name].shape)
        drawn = base * np.exp(spread * noise) if base else spread * noise
        out[name] = jnp.asarray(drawn.astype(out[name].dtype))
    for name, factor in factors.items():
        out[name] = (out[name] * factor).astype(out[name].dtype)
    return out
```

```python
import concourse.bass as bass
from concourse import mybir
from contextlib import ExitStack

B, CH, HW, PATCH = 32, 3, 96, 16
SEG = (HW // PATCH) ** 2
T = B * SEG
C = 192
CB = C - 128
PD = PATCH * PATCH * 5 * CH
WIN = CH * ((PATCH + 2) ** 2 - 4)
KC = 120
NJ = WIN // KC
NT = T // 128
NS = T // SEG + T // SEG // 2
SA = B
HT = T // 2
E, TOPK = 16, 2
CAP = -(-T // E * TOPK)
HC = CAP // 2
F = 4 * C
FM = F // 128
FS = F * 2 // 4
FSM = FS // 128
XR = C + E
WE = 2 * F + F + FM * C
RING = 4
LN_EPS = 1e-5
NEG = -1e38


def vit_tower_kernel(nc, xwin, wshift, kconst, proj_b, chan, wattn, gate_t, wshared, wexp, out):
    fp32 = mybir.dt.float32
    f16 = mybir.dt.float16
    bf16 = mybir.dt.bfloat16
    i32 = mybir.dt.int32
    u32 = mybir.dt.uint32
    ALU = mybir.AluOpType
    ACT = mybir.ActivationFunctionType
    AX = mybir.AxisListType
    ds = bass.ds

    ctx = ExitStack()
    with ctx:
        def sb(name, shape, dt=fp32):
            return ctx.enter_context(nc.sbuf_tensor(name, shape, dt))

        def sem(name):
            return ctx.enter_context(nc.semaphore(name))

        xrows = nc.dram_tensor("xrows", (T, XR), fp32).ap()

        SL = NS * (SEG + 1)
        R1 = sb("R1", [128, NJ * T + NJ * 5 * C])
        R2 = sb("R2", [128, 5 * SL])
        Xs = R1[0:KC, 0:NJ * T].rearrange("p (j t) -> p j t", j=NJ)
        Ws = R1[0:KC, NJ * T:NJ * T + NJ * 5 * C].rearrange("p (j s c) -> p j s c", j=NJ, s=5)
        Wc = sb("Wc", [KC, NJ, C + 1])
        Xq = R2[0:KC, 0:2 * T].rearrange("p (b t) -> p b t", b=2)
        KCN = sb("KCN", [KC, NJ, 11])
        ones = sb("ones", [128, 128])
        pbr = sb("pbr", [1, C])
        csum = sb("csum", [128, 2, C])
        st = sb("st", [128, 8, NT])
        nmu, ex2, musq, rstd0, rstd1, rstd2, half = (st[:, k, :] for k in range(7))
        bst = sb("bst", [128, NT, 6])
        bag = sb("bag", [128, NT, 2])
        h = sb("h", [128, NT, C])
        xn = sb("xn", [128, NT, XR])
        ident = sb("ident", [128, 128])
        chn = sb("chn", [128, 2, 5])
        mix1 = sb("mix1", [128, 2, 3])
        wdec = sb("wdec", [128, 2])
        WA = sb("WA", [128, 8, C])
        WG = sb("WG", [128, 2, E])
        GZ = sb("GZ", [128, 2, 8, 128])
        WS = sb("WS", [128, 3 * FS + FSM * C])
        ring = sb("ring", [128, RING, WE])

        def slot(R, k):
            return R[:, k * SL:(k + 1) * SL].rearrange("p (s t) -> p s t", s=NS)

        def flat(R, k, n=NS * SEG):
            return R[:, k * SL:k * SL + n]
        xt, dx = flat(R2, 0), flat(R2, 1)
        xm = [flat(R2, 2 + m) for m in range(3)]
        kp, wp, mm, cc, aa, bb, vv, bv, er = (slot(R1, k) for k in range(9))
        num, den, e1, e2, nn = (slot(R2, k) for k in range(5))
        tt = cc
        yy = flat(R1, 0)
        yA, yB = yy[:, 0:T], yy[:, T:T + HT]
        yv = yy.rearrange("p (s t) -> p s t", s=NS)
        xt2 = R2[:, 0:2 * T].rearrange("p (k t) -> p k t", k=2)
        o_fs = 2 * T
        sgs = R2[:, o_fs:o_fs + FSM * 384].rearrange("p (m t) -> p m t", m=FSM)
        hsT = R2[:, o_fs + FSM * 384:o_fs + 2 * FSM * 384].rearrange("p (m t) -> p m t", m=FSM)
        o = [0]

        def carve(n, dt=None):
            a = R1[:, o[0]:o[0] + n]
            o[0] += n
            return a if dt is None else a.bitcast(dt)
        sc = carve(CAP)
        scr = carve(CAP)
        gt = carve(CAP)
        eq = carve(CAP)
        cum = carve(CAP)
        zc = carve(CAP)
        slt = carve(CAP)
        af = carve(CAP)
        bf = carve(CAP)
        ai = carve(CAP, i32)
        abT = R1[0:HC, o[0]:o[0] + 256].bitcast(f16).rearrange("p (d h q) -> p d h q", d=2, h=2)
        o[0] += 256
        A1 = R1[0:HC, o[0]:o[0] + 1024].bitcast(f16).rearrange("p (g q) -> p g q", g=16)
        o[0] += 1024
        A0 = R1[0:HC, o[0]:o[0] + 1024].bitcast(f16).rearrange("p (g q) -> p g q", g=16)
        o[0] += 1024
        B1 = R1[0:HC, o[0]:o[0] + 2304].bitcast(f16).rearrange("p (g q) -> p g q", g=16)
        o[0] += 2304
        Ld = carve(E * 18)
        L1 = carve(18)
        Lr = carve(HC)
        xg = R1[0:HC, o[0]:o[0] + 2 * 2 * XR].rearrange("p (b h c) -> p b h c", b=2, h=2)
        o[0] += 4 * XR
        xgT = R1[:, o[0]:o[0] + 4 * CAP].rearrange("p (b k t) -> p b k t", b=2, k=2)
        o[0] += 4 * CAP
        sg = R1[:, o[0]:o[0] + 2 * FM * CAP].rearrange("p (b m t) -> p b m t", b=2, m=FM)
        o[0] += 2 * FM * CAP
        hT = R1[:, o[0]:o[0] + 2 * FM * CAP].rearrange("p (b m t) -> p b m t", b=2, m=FM)
        o[0] += 2 * FM * CAP
        yo = R1[0:HC, o[0]:o[0] + 4 * C].rearrange("p (b h c) -> p b h c", b=2, h=2)
        o[0] += 4 * C
        assert o[0] <= NJ * T + NJ * 5 * C
        small = sb("small", [128, 40])
        cand = sb("cand", [128, 1], i32)
        flip = sb("flip", [128, 1], i32)
        bits = sb("bits", [128, 31], i32)
        bitf = sb("bitf", [128, 31])
        cnt = sb("cnt", [128, 2], bf16)
        same = sb("same", [128, 128], bf16)
        before = sb("before", [128, 128], bf16)
        samef = sb("samef", [128, 2, 128])
        iota8 = sb("iota8", [HC, 8], f16)
        iota18 = sb("iota18", [HC, 18], f16)
        ids = sb("ids", [HC, 16], f16)
        emask = sb("emask", [128, E])
        amask = sb("amask", [128, 4])
        rmask = sb("rmask", [128, E, 2])
        idx = sb("idx", [HC, 2 * E], u32)
        ps = ctx.enter_context(nc.psum_tensor("ps", [128, 8, 512], fp32))

        s_kc = sem("s_kc")
        s_xw = [sem(f"s_xw{j}") for j in range(NJ)]
        s_ws = [sem(f"s_ws{j}") for j in range(NJ)]
        s_pb = sem("s_pb")
        s_ch = sem("s_ch")
        s_wa = sem("s_wa")
        s_wg = sem("s_wg")
        s_wsh = sem("s_wsh")
        s_ring = [sem(f"s_ring{k}") for k in range(RING)]
        s_const = sem("s_const")
        s_ones = sem("s_ones")
        s_acc = sem("s_acc")
        s_wc = sem("s_wc")
        s_xq = sem("s_xq")
        s_sq = sem("s_sq")
        s_tok = sem("s_tok")
        s_b = sem("s_b")
        s_var = [sem(f"s_var{k}") for k in range(3)]
        s_rs = [sem(f"s_rs{k}") for k in range(3)]
        s_pl = sem("s_pl")
        s_xn = [sem(f"s_xn{k}") for k in range(2)]
        s_tp = [sem(f"s_tp{k}") for k in range(2)]
        s_xt = [sem(f"s_xt{k}") for k in range(2)]
        s_mix = sem("s_mix")
        s_w = sem("s_w")
        s_pad = sem("s_pad")
        s_proj = sem("s_proj")
        s_ev = sem("s_ev")
        s_v = sem("s_v")
        s_arg = sem("s_arg")
        s_exp = sem("s_exp")
        s_y = sem("s_y")
        s_at = sem("s_at")
        s_gz = sem("s_gz")
        s_sl = sem("s_sl")
        s_es = sem("s_es")
        s_st = sem("s_st")
        s_est = sem("s_est")
        s_row = sem("s_row")
        s_rowd = sem("s_rowd")
        s_cnt = sem("s_cnt")
        s_tot = sem("s_tot")
        s_r = sem("s_r")
        s_rp = sem("s_rp")
        s_gu = sem("s_gu")
        s_ssg = sem("s_ssg")
        s_sh = sem("s_sh")
        s_dn = sem("s_dn")
        s_ysh = sem("s_ysh")
        s_yd = sem("s_yd")
        s_idx = sem("s_idx")
        s_xg = [sem(f"s_xg{k}") for k in range(2)]
        s_xgt = sem("s_xgt")
        s_xgs = sem("s_xgs")
        s_eg = sem("s_eg")
        s_eu = sem("s_eu")
        s_sg = sem("s_sg")
        s_h = sem("s_h")
        s_ed = sem("s_ed")
        s_yo = sem("s_yo")
        s_add = [sem(f"s_add{k}") for k in range(2)]

        block = ctx.enter_context(nc.Block())

        def tokcol(i):
            return i // 2, 256 * (i % 2)

        @block.sync
        def _(sp):
            sp.dma_start(KCN[:], kconst).then_inc(s_kc, 16)
            for j in range(NJ):
                sp.dma_start(Ws[:, j], wshift[:, j]).then_inc(s_ws[j], 16)
                sp.dma_start(Xs[:, j], xwin[:, j]).then_inc(s_xw[j], 16)
            sp.dma_start(pbr[:], proj_b).then_inc(s_pb, 16)
            sp.dma_start(chn[:], chan).then_inc(s_ch, 16)
            sp.dma_start(WA[:], wattn).then_inc(s_wa, 16)
            sp.dma_start(WG[:], gate_t).then_inc(s_wg, 16)
            sp.dma_start(WS[:], wshared).then_inc(s_wsh, 16)
            for k in range(RING):
                sp.dma_start(ring[:, k], wexp[k]).then_inc(s_ring[k], 16)
            sp.wait_ge(s_row, 1)
            sp.dma_start(xrows.rearrange("(i p) c -> p i c", p=128), xn[:]).then_inc(s_rowd, 16)
            for n in range(3):
                sp.wait_ge(s_ysh, 3 * (n + 1))
                sp.dma_start(out[384 * n:384 * (n + 1), :].rearrange("(i p) c -> p i c", p=128),
                             h[:, 3 * n:3 * n + 3]).then_inc(s_yd, 16)
            wgroup = wexp.rearrange("(g k) p w -> g k p w", k=RING)
            with sp.Fori(1, E // RING) as grp:
                for k in range(RING):
                    sp.wait_ge(s_ed, grp * RING + (k + 1 - RING))
                    sp.dma_start(ring[:, k], wgroup[ds(grp, 1), k].rearrange("a p w -> p (a w)")).then_inc(s_ring[k], 16)

        @block.gpsimd
        def _(pool):
            g = nc.gpsimd
            g.memset(half, -0.5)
            g.memset(ones[:], 1.0).then_inc(s_ones, 1)
            g.memset(ident[:], 1.0).then_inc(s_pl, 1)
            g.memset(samef[:], 1.0).then_inc(s_pl, 1)
            g.memset(emask[:], 1.0).then_inc(s_pl, 1)
            g.memset(rmask[:], 1.0).then_inc(s_pl, 1)
            g.memset(GZ[:], 0.0).then_inc(s_pl, 1)
            pool.wait_ge(s_pl, 5)
            g.affine_select(out=ident[:], in_=ident[:], compare_op=ALU.is_equal, fill=0.0, base=0,
                            pattern=[[-1, 128]], channel_multiplier=1).then_inc(s_const, 1)
            sv = samef[:, 0, :].rearrange("p (e s) -> p e s", e=E)
            g.affine_select(out=sv, in_=sv, compare_op=ALU.is_ge, fill=0.0, base=0,
                            pattern=[[-8, E], [0, 8]], channel_multiplier=1).then_inc(s_pl, 1)
            pool.wait_ge(s_pl, 6)
            g.affine_select(out=sv, in_=sv, compare_op=ALU.is_ge, fill=0.0, base=7,
                            pattern=[[8, E], [0, 8]], channel_multiplier=-1).then_inc(s_pl, 1)
            pool.wait_ge(s_pl, 7)
            g.affine_select(out=samef[:, 1, :], in_=samef[:, 0, :], compare_op=ALU.is_gt, fill=0.0, base=0,
                            pattern=[[1, 128]], channel_multiplier=-1).then_inc(s_pl, 1)
            pool.wait_ge(s_pl, 8)
            g.tensor_copy(same[:], samef[:, 0, :])
            g.tensor_copy(before[:], samef[:, 1, :]).then_inc(s_const, 1)
            g.affine_select(out=emask[:], in_=emask[:], compare_op=ALU.is_ge, fill=0.0, base=0,
                            pattern=[[-8, E]], channel_multiplier=1).then_inc(s_pl, 1)
            pool.wait_ge(s_pl, 9)
            g.affine_select(out=emask[:], in_=emask[:], compare_op=ALU.is_ge, fill=0.0, base=7,
                            pattern=[[8, E]], channel_multiplier=-1).then_inc(s_const, 1)
            g.affine_select(out=rmask[:], in_=rmask[:], compare_op=ALU.is_ge, fill=0.0, base=0,
                            pattern=[[-8, E], [-4, 2]], channel_multiplier=1).then_inc(s_pl, 1)
            pool.wait_ge(s_pl, 10)
            g.affine_select(out=rmask[:], in_=rmask[:], compare_op=ALU.is_ge, fill=0.0, base=3,
                            pattern=[[8, E], [4, 2]], channel_multiplier=-1).then_inc(s_const, 1)
            g.iota(iota8[:], pattern=[[1, 8]], base=0, channel_multiplier=0,
                   allow_small_or_imprecise_dtypes=True)
            g.iota(iota18[:], pattern=[[1, 18]], base=1, channel_multiplier=0,
                   allow_small_or_imprecise_dtypes=True)
            g.iota(ids[:].rearrange("p (h s) -> p h s", h=2), pattern=[[HC, 2], [CAP, 8]], base=0,
                   channel_multiplier=1, allow_small_or_imprecise_dtypes=True).then_inc(s_const, 1)
            pool.wait_ge(s_wg, 16)
            for k, kn in ((0, 128), (1, CB)):
                for s in range(8):
                    last = g.tensor_copy(GZ[0:kn, k, s, :].rearrange("p (e q) -> p e q", e=E)[:, :, s], WG[0:kn, k, :])
            last.then_inc(s_gz, 1)
            for k, (v, r) in enumerate(((ex2, rstd0), (bag[:, :, 1], rstd1), (bag[:, :, 1], rstd2))):
                pool.wait_ge(s_var[k], 1)
                g.tensor_scalar(r, v, LN_EPS, None, ALU.add).then_inc(s_pl, 1)
                pool.wait_ge(s_pl, 11 + k)
                g.tensor_tensor(r, r, half, ALU.pow).then_inc(s_rs[k], 1)
            pool.wait_ge(s_idx, 1)
            pool.wait_ge(s_rowd, 16)

            def gather(e):
                if e >= 2:
                    pool.wait_ge(s_yo, e - 1)
                for hh in range(2):
                    g.indirect_dma_start(xg[:, e % 2, hh, :], None, xrows,
                                         bass.IndirectOffsetOnAxis(idx[:, 2 * e + hh:2 * e + hh + 1], 0)).then_inc(s_xg[e % 2], 16)

            def scatter(e):
                pool.wait_ge(s_yo, e + 1)
                if e:
                    pool.wait_ge(s_add[0], e * 16)
                    pool.wait_ge(s_add[1], e * 16)
                for hh in range(2):
                    g.indirect_dma_start(out, bass.IndirectOffsetOnAxis(idx[:, 2 * e + hh:2 * e + hh + 1], 0),
                                         yo[:, e % 2, hh, :], None, compute_op=ALU.add).then_inc(s_add[hh], 16)

            gather(0)
            gather(1)
            pool.wait_ge(s_yd, 48)
            for e in range(E):
                if e + 2 < E:
                    gather(e + 2)
                scatter(e)
            pool.wait_ge(s_add[0], 16 * E)
            pool.wait_ge(s_add[1], 16 * E)

        @block.scalar
        def _(act):
            a = nc.scalar
            for j in range(NJ):
                act.wait_ge(s_xw[j], 16)
                if j >= 2:
                    act.wait_ge(s_sq, j - 1)
                a.activation(Xq[:, j % 2, :], Xs[:, j, :], ACT.Square).then_inc(s_xq, 1)
            act.wait_ge(s_ch, 16)
            a.activation(wdec[:], chn[:, :, 3], ACT.Exp).then_inc(s_w, 1)
            act.wait_ge(s_tp[0], 1)
            a.copy(xt[:, 0:512], ps[:, 0, :])
            a.copy(xt[:, 512:1024], ps[:, 1, :])
            a.copy(xt[:, 1024:T], ps[:, 2, 0:128])
            a.copy(xt[0:64, T:T + 512], ps[0:64, 3, :])
            a.copy(xt[0:64, T + 512:T + HT], ps[0:64, 4, 0:64])
            a.copy(xt[64:128, T:T + 448], ps[0:64, 4, 64:512])
            a.copy(xt[64:128, T + 448:T + HT], ps[0:64, 5, 0:128]).then_inc(s_xt[0], 1)
            act.wait_ge(s_pad, 1)
            for n in range(18):
                m, q = n // 6, n % 6
                src = ps[:, n % 8, 0:288].rearrange("p (s t) -> p s t", t=SEG)
                act.wait_ge(s_proj, n + 1)
                if m == 0:
                    i = a.copy(kp[:, 8 * q:8 * q + 8, 1:SEG + 1], src)
                elif m == 1:
                    i = a.copy(vv[:, 8 * q:8 * q + 8, 1:SEG + 1], src)
                else:
                    i = a.activation(er[:, 8 * q:8 * q + 8, 1:SEG + 1], src, ACT.Exp, scale=-1.0)
                i.then_inc(s_ev, 1)
            for part, (s0, s1) in enumerate(((0, SA), (SA, NS))):
                for k, x in enumerate((aa, bb, e1, e2)):
                    act.wait_ge(s_arg, 4 * part + k + 1)
                    a.activation(x[:, s0:s1, 1:], x[:, s0:s1, 1:], ACT.Exp).then_inc(s_exp, 1)
            act.wait_ge(s_tp[1], 1)
            a.copy(xt2[:, 0, 0:512], ps[:, 0, :])
            a.copy(xt2[:, 0, 512:1024], ps[:, 1, :])
            a.copy(xt2[:, 0, 1024:T], ps[:, 2, 0:128])
            for p in (0, 64):
                a.copy(xt2[p:p + 64, 1, 0:512], ps[0:64, 3, :])
                a.copy(xt2[p:p + 64, 1, 512:1024], ps[0:64, 4, :])
                last = a.copy(xt2[p:p + 64, 1, 1024:T], ps[0:64, 5, 0:128])
            last.then_inc(s_xt[1], 1)
            act.wait_ge(s_sl, 1)
            a.activation(sc, ps[:, 6, 0:CAP], ACT.Exp, scale=-1.0).then_inc(s_es, 1)
            act.wait_ge(s_st, 1)
            a.activation(xn[:, :, C:XR], ps[:, 7, 0:NT * E].rearrange("p (i e) -> p i e", i=NT), ACT.Exp,
                         scale=-1.0).then_inc(s_est, 1)
            for n in range(3):
                for m in range(FSM):
                    c = FSM * n + m
                    act.wait_ge(s_gu, c + 1)
                    if m == 0 and n:
                        act.wait_ge(s_sh, FSM * n)
                    a.activation(sgs[:, m, :], ps[:, 2 * (c % 2), 0:384], ACT.Silu).then_inc(s_ssg, 1)
            def xg_out(b):
                a.copy(xgT[:, b, 0, :], ps[:, 4, 0:CAP])
                a.copy(xgT[0:64, b, 1, :], ps[0:64, 4, CAP:2 * CAP])
                a.copy(xgT[64:128, b, 1, :], ps[0:64, 4, CAP:2 * CAP]).then_inc(s_xgs, 1)

            def gates(e, b, last=False):
                for q in range(2):
                    act.wait_ge(s_eg, 2 * e + q + 1)
                    a.activation(sg[:, b, 3 * q:3 * q + 3, :].rearrange("p m t -> p (m t)"), ps[:, q, 0:3 * CAP],
                                 ACT.Silu).then_inc(s_sg, 1)
                if not last:
                    act.wait_ge(s_xgt, e + 2)
                    xg_out(1 - b)

            act.wait_ge(s_xgt, 1)
            xg_out(0)
            with act.Fori(0, E // 2 - 1) as pair:
                for b in range(2):
                    gates(pair * 2 + b, b)
            gates(E - 2, 0)
            gates(E - 1, 1, True)

        @block.vector
        def _(dve):
            v = nc.vector
            dve.wait_ge(s_kc, 16)
            v.tensor_copy(Wc[:, :, C], KCN[:, :, 10])
            for j in range(NJ):
                dve.wait_ge(s_ws[j], 16)
                v.tensor_scalar(Wc[:, j, 0:C], Ws[:, j, 0, :], KCN[:, j, 0:1], None, ALU.mult).then_inc(s_acc, 1)
                for s in range(1, 5):
                    dve.wait_ge(s_acc, 4 * j + s)
                    v.scalar_tensor_tensor(Wc[:, j, 0:C], Ws[:, j, s, :], KCN[:, j, s:s + 1], Wc[:, j, 0:C],
                                           ALU.mult, ALU.add).then_inc(s_acc if s < 4 else s_wc, 1)
            for b in range(31):
                v.memset(bits[:, b:b + 1], 1 << (29 - b) if b < 30 else 0)
            last = None
            for b in range(31):
                last = v.memset(bitf[:, b:b + 1], float(1 << (29 - b)) if b < 30 else 0.0)
            v.memset(cand[:], 1 << 29)
            v.memset(small[:], 0.0)
            dve.wait_ge(s_tok, 1)
            v.tensor_scalar(nmu[:, 0:8].rearrange("p (a b) -> p a b", b=2),
                            ps[:, 0:4, :].rearrange("p a (b c) -> p a b c", b=2)[:, :, :, C], -1.0 / PD, None, ALU.mult)
            v.tensor_scalar(nmu[:, 8:9], ps[:, 4, C:C + 1], -1.0 / PD, None, ALU.mult).then_inc(s_b, 1)
            v.tensor_copy(csum[:], ps[:, 5, :].rearrange("p (a c) -> p a c", a=2)[:, :, 0:C]).then_inc(s_b, 1)
            dve.wait_ge(s_b, 2)
            v.tensor_tensor(musq, nmu, nmu, ALU.mult).then_inc(s_b, 1)
            dve.wait_ge(s_b, 3)
            v.scalar_tensor_tensor(ex2, ps[:, 6, 0:NT], 1.0 / PD, musq, ALU.mult, ALU.subtract).then_inc(s_var[0], 1)
            for i in range(NT):
                b, c = tokcol(i)
                v.scalar_tensor_tensor(h[:, i, :], csum[:, 0, :], nmu[:, i:i + 1], ps[:, b, c:c + C],
                                       ALU.mult, ALU.add).then_inc(s_b, 1)
            dve.wait_ge(s_rs[0], 1)
            for i in range(NT):
                dve.wait_ge(s_b, 4 + i)
                v.scalar_tensor_tensor(h[:, i, :], h[:, i, :], rstd0[:, i:i + 1], csum[:, 1, :],
                                       ALU.mult, ALU.add).then_inc(s_b, 1)

            def stats(n0, k):
                for i in range(NT):
                    dve.wait_ge(s_b, n0 - NT + i + 1)
                    v.bn_stats(bst[:, i, :], h[:, i, :]).then_inc(s_b, 1)
                for i in range(NT):
                    dve.wait_ge(s_b, n0 + i + 1)
                    last = v.bn_aggr(bag[:, i, :], bst[:, i, :])
                last.then_inc(s_var[k], 1)

            def normalise(k, r):
                dve.wait_ge(s_rs[k], 1)
                dve.wait_ge(s_var[k], 1)
                for i in range(NT):
                    last = v.tensor_scalar(xn[:, i, 0:C], h[:, i, :], bag[:, i, 0:1], r[:, i:i + 1],
                                           ALU.subtract, ALU.mult)
                    last.then_inc(s_xn[k - 1], 1)

            stats(3 + 2 * NT, 1)
            normalise(1, rstd1)
            v.tensor_scalar(mix1[:], chn[:, :, 0:3], -1.0, None, ALU.add).then_inc(s_mix, 1)
            v.memset(kp[:, :, 0], NEG)
            v.memset(vv[:, :, 0], 0.0)
            v.memset(mm[:, :, 0], NEG)
            v.memset(wp[:, :, 1:], 0.0)
            v.memset(wp[:, :, 0], NEG).then_inc(s_pad, 1)
            dve.wait_ge(s_w, 1)
            dve.wait_ge(s_pad, 1)
            for q, (s0, s1) in enumerate(((0, SA), (SA, NS))):
                v.tensor_scalar(wp[:, s0:s1, 1:], wp[:, s0:s1, 1:], wdec[:, q:q + 1], None, ALU.subtract).then_inc(s_v, 1)
            dve.wait_ge(s_xt[0], 1)
            v.tensor_tensor(dx[:, 1:], xt[:, 1:], xt[:, 0:NS * SEG - 1], ALU.subtract).then_inc(s_mix, 1)
            dve.wait_ge(s_mix, 2)
            v.tensor_copy(dx.rearrange("p (s t) -> p s t", t=SEG)[:, :, 0],
                          xt.rearrange("p (s t) -> p s t", t=SEG)[:, :, 0]).then_inc(s_mix, 1)
            dve.wait_ge(s_mix, 3)
            for m in range(3):
                for q, (c0, c1) in enumerate(((0, T), (T, T + HT))):
                    v.scalar_tensor_tensor(xm[m][:, c0:c1], dx[:, c0:c1], mix1[:, q, m:m + 1], xt[:, c0:c1],
                                           ALU.mult, ALU.add).then_inc(s_mix, 1)
            u = [2]

            def step(ins, s=s_v):
                ins.then_inc(s, 1)
                if s is s_v:
                    u[0] += 1
                    dve.wait_ge(s_v, u[0])
            dve.wait_ge(s_v, 2)
            for q, (s0, s1) in enumerate(((0, SA), (SA, NS))):
                def fl(x):
                    return x[:, s0:s1, :].rearrange("p s t -> p (s t)")

                def cur(x):
                    return x[:, s0:s1, 1:]

                def prev(x):
                    return x[:, s0:s1, 0:SEG]
                dve.wait_ge(s_ev, 4 if q == 0 else 6)
                step(v.tensor_tensor_scan(fl(mm), fl(wp), fl(kp), NEG, ALU.add, ALU.max))
                step(v.scalar_tensor_tensor(cur(cc), prev(mm), wp[:, s0, 1:2], cur(kp), ALU.add, ALU.subtract))
                v.tensor_scalar(cur(aa), cur(cc), 0.0, None, ALU.min).then_inc(s_arg, 1)
                v.tensor_scalar(cur(bb), cur(cc), -1.0, 0.0, ALU.mult, ALU.min).then_inc(s_arg, 1)
                v.memset(aa[:, s0:s1, 0], 0.0)
                v.memset(bv[:, s0:s1, 0], 0.0)
                v.memset(bb[:, s0:s1, 0], 0.0)
                dve.wait_ge(s_arg, 4 * q + 2)
                step(v.scalar_tensor_tensor(cur(cc), cur(kp), chn[:, q, 4:5], prev(mm), ALU.add, ALU.subtract))
                if q == 0:
                    dve.wait_ge(s_proj, 18)
                v.tensor_scalar(cur(e1), cur(cc), -1.0, 0.0, ALU.mult, ALU.min).then_inc(s_arg, 1)
                v.tensor_scalar(cur(e2), cur(cc), 0.0, None, ALU.min).then_inc(s_arg, 1)
                dve.wait_ge(s_ev, 10 if q == 0 else 12)
                dve.wait_ge(s_exp, 4 * q + 2)
                step(v.tensor_tensor(cur(bv), cur(bb), cur(vv), ALU.mult))
                v.tensor_tensor_scan(fl(num), fl(aa), fl(bv), 0.0, ALU.mult, ALU.add)
                step(v.tensor_tensor_scan(fl(den), fl(aa), fl(bb), 0.0, ALU.mult, ALU.add))
                dve.wait_ge(s_exp, 4 * q + 4)
                dve.wait_ge(s_arg, 4 * q + 4)
                v.tensor_tensor(cur(nn), cur(e1), prev(num), ALU.mult)
                step(v.tensor_tensor(cur(tt), cur(e2), cur(vv), ALU.mult))
                step(v.tensor_tensor(cur(nn), cur(nn), cur(tt), ALU.add))
                step(v.tensor_tensor(cur(e1), cur(e1), prev(den), ALU.mult))
                step(v.tensor_tensor(cur(e1), cur(e1), cur(e2), ALU.add))
                dve.wait_ge(s_ev, 16 if q == 0 else 18)
                step(v.scalar_tensor_tensor(cur(e1), cur(er), 1.0, cur(e1), ALU.add, ALU.mult))
                step(v.reciprocal(cur(e1), cur(e1)))
                v.tensor_tensor(yv[:, s0:s1, :], cur(nn), cur(e1), ALU.mult).then_inc(s_y, 1)
            for i in range(NT):
                dve.wait_ge(s_at, min(NT, i // 2 * 2 + 2))
                v.tensor_tensor(h[:, i, :], h[:, i, :], ps[:, i // 2, 256 * (i % 2):256 * (i % 2) + C],
                                ALU.add).then_inc(s_b, 1)
            stats(3 + 4 * NT, 2)
            normalise(2, rstd2)
            r = [0]

            def rs(ins):
                r[0] += 1
                ins.then_inc(s_r, 1)
                dve.wait_ge(s_r, r[0])

            dve.wait_ge(s_es, 1)
            rs(v.tensor_scalar(sc, sc, 1.0, None, ALU.add))
            rs(v.reciprocal(sc, sc))

            def count():
                v.tensor_scalar(scr, sc, cand[:].bitcast(fp32), None, ALU.is_ge, ALU.add,
                                accum_out=cnt[:, 0:1]).then_inc(s_cnt, 1)

            def decide(b):
                dve.wait_ge(s_tot, b + 1)
                rs(v.tensor_scalar(flip[:], ps[:, 7, 256:257], CAP - 0.5, bitf[:, b:b + 1], ALU.is_lt, ALU.mult))
                rs(v.scalar_tensor_tensor(cand[:], cand[:], bits[:, b + 1:b + 2], flip[:], ALU.bitwise_xor, ALU.bitwise_xor))

            def shared_up(c):
                dve.wait_ge(s_ssg, c + 1)
                if c % FSM == 0 and c:
                    dve.wait_ge(s_dn, 3 * (c // FSM))
                v.tensor_tensor(hsT[:, c % FSM, :], sgs[:, c % FSM, :], ps[:, 2 * (c % 2) + 1, 0:384],
                                ALU.mult).then_inc(s_sh, 1)

            def shared_out(i):
                dve.wait_ge(s_dn, i + 1)
                v.tensor_tensor(h[:, i, :], h[:, i, :], ps[:, 4 + i % 2, 0:C], ALU.add).then_inc(s_ysh, 1)

            count()
            b = 0
            for n in range(3):
                for m in range(FSM):
                    decide(b), count()
                    decide(b + 1), count()
                    b += 2
                    shared_up(FSM * n + m)
                    if n == 0 and m == 0:
                        dve.wait_ge(s_est, 1)
                        rs(v.tensor_scalar(xn[:, :, C:XR], xn[:, :, C:XR], 1.0, None, ALU.add))
                        v.reciprocal(xn[:, :, C:XR], xn[:, :, C:XR]).then_inc(s_row, 1)
                for i in range(3):
                    decide(b)
                    if b < 29:
                        count()
                    b += 1
                    shared_out(3 * n + i)
            for b in range(b, 30):
                decide(b)
                if b < 29:
                    count()
            thr = cand[:].bitcast(fp32)
            v.tensor_scalar(gt, sc, thr, None, ALU.is_gt, ALU.add, accum_out=cnt[:, 0:1])
            rs(v.tensor_scalar(eq, sc, thr, None, ALU.is_equal, ALU.add, accum_out=cnt[:, 1:2]))
            v.memset(zc, 1.0).then_inc(s_cnt, 1)
            dve.wait_ge(s_cnt, 31)
            rs(v.tensor_tensor_scan(cum, zc, eq, 0.0, ALU.mult, ALU.add))
            dve.wait_ge(s_rp, 1)
            v.tensor_scalar(small[:, 0:1], ps[:, 7, 258:259], -1.0, float(CAP), ALU.mult, ALU.add)
            rs(v.tensor_copy(small[:, 1:2], ps[:, 7, 259:260]))
            rs(v.tensor_scalar(cum, cum, small[:, 1:2], small[:, 0:1], ALU.add, ALU.is_le))
            rs(v.tensor_tensor(eq, eq, cum, ALU.mult))
            rs(v.tensor_tensor(gt, gt, eq, ALU.add))
            rs(v.tensor_tensor_scan(cum, zc, gt, 0.0, ALU.mult, ALU.add))
            v.tensor_copy(cnt[:, 0:1], cum[:, CAP - 1:CAP]).then_inc(s_cnt, 1)
            dve.wait_ge(s_rp, 2)
            rs(v.tensor_copy(small[:, 2:3], ps[:, 7, 260:261]))
            rs(v.scalar_tensor_tensor(slt, cum, small[:, 2:3], gt, ALU.add, ALU.mult))
            rs(v.tensor_scalar(ai, slt, 1.0 / 18, -9.5 / 18, ALU.mult, ALU.add))
            rs(v.tensor_copy(af, ai))
            v.scalar_tensor_tensor(bf, af, -18.0, slt, ALU.mult, ALU.add).then_inc(s_cnt, 1)
            dve.wait_ge(s_rp, 3)
            rs(v.tensor_copy(abT, ps[0:HC, 6, :].rearrange("p (d h q) -> p d h q", d=2, h=2)))
            dve.wait_ge(s_const, 5)
            for hh in range(2):
                srcA = abT[:, 0, hh, :].rearrange("p (e s) -> p s e", e=E)
                srcB = abT[:, 1, hh, :].rearrange("p (e s) -> p s e", e=E)
                for s in range(8):
                    g_ = 8 * hh + s
                    v.tensor_tensor(A0[:, g_, :].rearrange("p (e a) -> p e a", e=E),
                                    srcA[:, s, :].unsqueeze(2).to_broadcast([HC, E, 8]),
                                    iota8[:].unsqueeze(1).to_broadcast([HC, E, 8]), ALU.is_equal)
                    v.tensor_tensor(B1[:, g_, :].rearrange("p (e a) -> p e a", e=E),
                                    srcB[:, s, :].unsqueeze(2).to_broadcast([HC, E, 18]),
                                    iota18[:].unsqueeze(1).to_broadcast([HC, E, 18]), ALU.is_equal)
            rs(v.memset(small[:, 3:4], 0.0))
            v.tensor_tensor(A1, A0, ids[:].unsqueeze(2).to_broadcast([HC, 16, 128]), ALU.mult).then_inc(s_cnt, 1)
            dve.wait_ge(s_const, 1)
            v.tensor_reduce(amask[:], ident[:].rearrange("p (q a) -> p a q", a=4), AX.X, ALU.add)
            dve.wait_ge(s_rp, 4)
            rs(v.tensor_tensor(Ld.rearrange("p (e b) -> p e b", e=E), ps[:, 6, 0:E * 18].rearrange("p (e b) -> p e b", e=E),
                               emask[:].unsqueeze(2).to_broadcast([128, E, 18]), ALU.mult))
            rs(v.tensor_reduce(L1, Ld.rearrange("p (e b) -> p b e", e=E), AX.X, ALU.add))
            v.tensor_tensor(Lr.rearrange("p (a b) -> p a b", a=4), L1.unsqueeze(1).to_broadcast([128, 4, 18]),
                            amask[:].unsqueeze(2).to_broadcast([128, 4, 18]), ALU.mult).then_inc(s_cnt, 1)
            dve.wait_ge(s_rp, 5)
            v.tensor_copy(idx[:], ps[0:HC, 7, 320:320 + 2 * E]).then_inc(s_idx, 1)
            def expert(e, b, first=False):
                for q in range(2):
                    dve.wait_ge(s_sg, 2 * e + q + 1)
                    dve.wait_ge(s_eu, 2 * e + q + 1)
                    v.tensor_tensor(hT[:, b, 3 * q:3 * q + 3, :].rearrange("p m t -> p (m t)"),
                                    sg[:, b, 3 * q:3 * q + 3, :].rearrange("p m t -> p (m t)"),
                                    ps[:, 2 + q, 0:3 * CAP], ALU.mult).then_inc(s_h, 1)
                dve.wait_ge(s_ed, e + 1)
                if not first:
                    dve.wait_ge(s_add[0], (e - 1) * 16)
                    dve.wait_ge(s_add[1], (e - 1) * 16)
                for hh in range(2):
                    last = v.tensor_scalar(yo[:, b, hh, :], ps[0:HC, 5, 256 * hh:256 * hh + C],
                                           xg[:, b, hh, ds(e + C, 1)], None, ALU.mult)
                last.then_inc(s_yo, 1)

            expert(0, 0, True)
            expert(1, 1, True)
            with dve.Fori(1, E // 2) as pair:
                for b in range(2):
                    expert(pair * 2 + b, b)

        @block.tensor
        def _(pe):
            t = nc.tensor
            pe.wait_ge(s_kc, 16)
            pe.wait_ge(s_ones, 1)
            for j in range(NJ):
                pe.wait_ge(s_ws[j], 16)
                for s in range(5):
                    t.matmul(ps[:, 5, 256:256 + C], KCN[:, j, 5 + s:6 + s].to_broadcast([KC, 128]), Ws[:, j, s, :],
                             start=(j == 0 and s == 0), stop=False, skip_group_check=True)
                pe.wait_ge(s_xw[j], 16)
                pe.wait_ge(s_wc, j + 1)
                t.matmul(ps[:, 5, 0:C], ones[0:KC, :], Wc[:, j, 0:C], start=False, stop=(j == NJ - 1),
                         skip_group_check=True)
                for i in range(NT):
                    b, c = tokcol(i)
                    t.matmul(ps[:, b, c:c + C + 1], Xs[:, j, 128 * i:128 * i + 128], Wc[:, j, :],
                             start=(j == 0 and c == 0), stop=(j == NJ - 1), skip_group_check=True)
                pe.wait_ge(s_xq, j + 1)
                for i in range(NT):
                    last = t.matmul(ps[:, 6, i:i + 1], Xq[:, j % 2, 128 * i:128 * i + 128], Wc[:, j, C:C + 1],
                                    start=(j == 0 and i == 0), stop=(j == NJ - 1), skip_group_check=True)
                last.then_inc(s_sq, 1)
            pe.wait_ge(s_pb, 16)
            t.matmul(ps[:, 5, 256:256 + C], ones[0:1, :], pbr[0:1, :], start=False, stop=True,
                     skip_group_check=True).then_inc(s_tok, 1)

            def transposes(k):
                for i in range(NT):
                    pe.wait_ge(s_xn[k], i + 1)
                    t.transpose(ps[:, i // 4, 128 * (i % 4):128 * (i % 4) + 128], xn[:, i, 0:128], ident[:])
                    last = t.transpose(ps[0:64, 3 + i // 4, 128 * (i % 4):128 * (i % 4) + 128], xn[:, i, 128:C], ident[:])
                last.then_inc(s_tp[k], 1)

            pe.wait_ge(s_const, 1)
            transposes(0)
            pe.wait_ge(s_wa, 16)
            pe.wait_ge(s_xt[0], 1)
            for n in range(18):
                m, q = n // 6, n % 6
                if n >= 8:
                    pe.wait_ge(s_ev, n - 7)
                pe.wait_ge(s_mix, 3 + 2 * (m + 1))
                if q < 4:
                    hf = q // 2
                    o_ = ps[:, n % 8, 0:288]
                    t.matmul(o_, WA[:, m, 0:128], xm[m][:, 288 * q:288 * q + 288], start=True, stop=False)
                    t.matmul(o_, WA[64 * hf:64 * hf + 64, 4 + m, 0:128],
                             xm[m][64 * hf:64 * hf + 64, T + 288 * (q % 2):T + 288 * (q % 2) + 288],
                             start=False, stop=True).then_inc(s_proj, 1)
                else:
                    for hf in range(2):
                        o_ = ps[64 * hf:64 * hf + 64, n % 8, 0:288]
                        c = HT * hf + 288 * (q - 4)
                        t.matmul(o_, WA[:, m, 128:C], xm[m][:, c:c + 288], start=True, stop=False)
                        last = t.matmul(o_, WA[64 * hf:64 * hf + 64, 4 + m, 128:C],
                                        xm[m][64 * hf:64 * hf + 64, T + 288 * (q - 4):T + 288 * (q - 4) + 288],
                                        start=False, stop=True)
                    last.then_inc(s_proj, 1)
            pe.wait_ge(s_ev, 18)
            pe.wait_ge(s_y, 2)
            for i in range(NT):
                b, c = tokcol(i)
                t.matmul(ps[:, b, c:c + C], yA[:, 128 * i:128 * i + 128], WA[:, 3, :], start=(c == 0), stop=False,
                         skip_group_check=True)
                pieces = ([(0, 128, 0, 128 * i)] if i < 4 else [(0, 64, 0, 512), (64, 128, 64, 0)] if i == 4
                          else [(0, 128, 64, 128 * i - HT)])
                for p0, p1, k0, c0 in pieces:
                    last = t.matmul(ps[p0:p1, b, c:c + C], yB[k0:k0 + 64, c0:c0 + p1 - p0], WA[k0:k0 + 64, 7, :],
                                    start=False, stop=True, skip_group_check=True)
                last.then_inc(s_at, 1)
            transposes(1)
            pe.wait_ge(s_xt[1], 1)
            pe.wait_ge(s_gz, 1)
            for s in range(8):
                t.matmul(ps[:, 6, 0:CAP], GZ[:, 0, s, :], xt2[:, 0, CAP * s:CAP * s + CAP], start=(s == 0), stop=False)
                last = t.matmul(ps[:, 6, 0:CAP], GZ[0:64, 1, s, :], xt2[0:64, 1, CAP * s:CAP * s + CAP],
                                start=False, stop=(s == 7))
            last.then_inc(s_sl, 1)
            for i in range(NT):
                t.matmul(ps[:, 7, E * i:E * i + E], xt2[:, 0, 128 * i:128 * i + 128], WG[:, 0, :], start=True, stop=False)
                last = t.matmul(ps[:, 7, E * i:E * i + E], xt2[0:64, 1, 128 * i:128 * i + 128], WG[0:64, 1, :],
                                start=False, stop=True)
            last.then_inc(s_st, 1)
            pe.wait_ge(s_est, 1)
            pe.wait_ge(s_wsh, 16)
            pe.wait_ge(s_const, 2)

            def total(b):
                pe.wait_ge(s_cnt, b + 1)
                t.matmul(ps[:, 7, 256:257], same[:], cnt[:, 0:1], start=True, stop=True).then_inc(s_tot, 1)

            b = 0
            for n in range(3):
                for m in range(FSM):
                    c = FSM * n + m
                    if c >= 2:
                        pe.wait_ge(s_sh, c - 1)
                    for w in range(2):
                        o_ = ps[:, 2 * (c % 2) + w, 0:384]
                        t.matmul(o_, WS[:, FS * w + 128 * m:FS * w + 128 * m + 128], xt2[:, 0, 384 * n:384 * n + 384],
                                 start=True, stop=False)
                        last = t.matmul(o_, WS[64 * w:64 * w + 64, 2 * FS + 128 * m:2 * FS + 128 * m + 128],
                                        xt2[64 * w:64 * w + 64, 1, 384 * n:384 * n + 384], start=False, stop=True)
                        if w == 0:
                            total(b)
                        else:
                            last.then_inc(s_gu, 1)
                            total(b + 1)
                    b += 2
                pe.wait_ge(s_sh, FSM * (n + 1))
                for i in range(3):
                    ti = 3 * n + i
                    if ti >= 2:
                        pe.wait_ge(s_ysh, ti - 1)
                    for m in range(FSM):
                        last = t.matmul(ps[:, 4 + ti % 2, 0:C], hsT[:, m, 128 * i:128 * i + 128],
                                        WS[:, 3 * FS + C * m:3 * FS + C * m + C], start=(m == 0), stop=(m == FSM - 1))
                    last.then_inc(s_dn, 1)
                    total(b)
                    b += 1
            for b in range(b, 30):
                total(b)
            pe.wait_ge(s_cnt, 31)
            t.matmul(ps[:, 7, 258:259], same[:], cnt[:, 0:1], start=True, stop=True)
            t.matmul(ps[:, 7, 259:260], before[:], cnt[:, 1:2], start=True, stop=True).then_inc(s_rp, 1)
            pe.wait_ge(s_cnt, 32)
            t.matmul(ps[:, 7, 260:261], before[:], cnt[:, 0:1], start=True, stop=True).then_inc(s_rp, 1)
            pe.wait_ge(s_cnt, 33)
            for d, x in enumerate((af, bf)):
                for hh in range(2):
                    last = t.transpose(ps[0:HC, 6, 256 * d + 128 * hh:256 * d + 128 * hh + 128],
                                       x[:, HC * hh:HC * hh + HC], ident[:])
            last.then_inc(s_rp, 1)
            pe.wait_ge(s_cnt, 34)
            for g_ in range(16):
                last = t.matmul(ps[:, 6, 0:E * 18], A1[:, g_, :], B1[:, g_, :], start=(g_ == 0), stop=(g_ == 15))
            last.then_inc(s_rp, 1)
            pe.wait_ge(s_cnt, 35)
            pe.wait_ge(s_const, 4)
            t.matmul(ps[0:HC, 7, 320:320 + 2 * E], Lr, rmask[:].rearrange("p e h -> p (e h)"), start=True,
                     stop=True).then_inc(s_rp, 1)

            def xg_in(b):
                for hh in range(2):
                    t.transpose(ps[:, 4, HC * hh:HC * hh + HC], xg[:, b, hh, 0:128], ident[0:HC, 0:HC])
                    last = t.transpose(ps[0:64, 4, CAP + HC * hh:CAP + HC * hh + HC], xg[:, b, hh, 128:C], ident[0:HC, 0:HC])
                last.then_inc(s_xgt, 1)

            pe.wait_ge(s_xg[0], 32)
            xg_in(0)

            def expert(grp, k, last_one=False):
                e = grp * RING + k
                b = k % 2
                W = ring[:, k, :]
                pe.wait_ge(s_ring[k], grp * 16 + 16)
                pe.wait_ge(s_xgs, e + 1)
                for q in range(2):
                    for w in range(2):
                        for m in range(3 * q, 3 * q + 3):
                            o_ = ps[:, 2 * w + q, CAP * (m - 3 * q):CAP * (m - 3 * q) + CAP]
                            t.matmul(o_, W[:, F * w + 128 * m:F * w + 128 * m + 128], xgT[:, b, 0, :],
                                     start=True, stop=False)
                            last = t.matmul(o_, W[64 * w:64 * w + 64, 2 * F + 128 * m:2 * F + 128 * m + 128],
                                            xgT[64 * w:64 * w + 64, b, 1, :], start=False, stop=True)
                        last.then_inc(s_eg if w == 0 else s_eu, 1)
                if not last_one:
                    pe.wait_ge(s_xg[1 - b], grp * (16 * RING) + 32 * ((k + 1) // 2 + 1))
                    xg_in(1 - b)
                pe.wait_ge(s_h, 2 * e + 2)
                for hh in range(2):
                    for m in range(FM):
                        last = t.matmul(ps[0:HC, 5, 256 * hh:256 * hh + C], hT[:, b, m, HC * hh:HC * hh + HC],
                                        W[:, 3 * F + C * m:3 * F + C * m + C], start=(m == 0), stop=(m == FM - 1))
                last.then_inc(s_ed, 1)

            with pe.Fori(0, E // RING - 1) as grp:
                for k in range(RING):
                    expert(grp, k)
            for k in range(RING):
                expert(E // RING - 1, k, k == RING - 1)


def kernel(**inputs):
    import numpy as _np
    import concourse.bacc as _bacc
    from concourse import mybir as _mybir
    from concourse.bass_utils import run_bass_kernel_spmd as _run

    src = {k: _np.asarray(v) for k, v in inputs.items()}
    W2 = PATCH + 2
    pix = [(c, r, s) for c in range(CH) for r in range(W2) for s in range(W2)
           if not (r in (0, W2 - 1) and s in (0, W2 - 1))]
    pc, pr, pw = (_np.array([p[k] for p in pix]) for k in range(3))
    xp = _np.pad(src["x"], ((0, 0), (0, 0), (1, 1), (1, 1)))
    n = HW // PATCH
    rows = pr[None, :] + PATCH * _np.arange(n)[:, None]
    cols = pw[None, :] + PATCH * _np.arange(n)[:, None]
    win = xp[:, pc[None, None, :], rows[:, None, :], cols[None, :, :]]
    xwin = win.reshape(T, NJ, KC).transpose(2, 1, 0)
    places = ((1, 1), (1, 0), (1, 2), (0, 1), (2, 1))

    def in_window(a):
        w = a.reshape(PATCH, PATCH, 5, CH, -1)
        full = _np.zeros((5, CH, W2, W2, w.shape[-1]), a.dtype)
        for s, (r, c) in enumerate(places):
            full[s, :, r:r + PATCH, c:c + PATCH] = w[:, :, s].transpose(2, 0, 1, 3)
        return full[:, pc, pr, pw].reshape(5, NJ, KC, -1).transpose(2, 1, 0, 3)

    wshift = in_window(src["L0_tok_proj_weight"].T)
    lnw = in_window(src["L0_tok_ln_weight"])[..., 0]
    lnb = in_window(src["L0_tok_ln_bias"])[..., 0]
    times = _np.zeros((CH, W2, W2), _np.float32)
    for r, c in places:
        times[:, r:r + PATCH, c:c + PATCH] += 1
    times = times[pc, pr, pw].reshape(NJ, KC).T[:, :, None]
    kconst = _np.concatenate([lnw, lnb, times], axis=2)
    chan = _np.stack([src["L0_attn_" + k] for k in ("mix_k", "mix_v", "mix_r", "time_decay", "time_first")], axis=1)
    chan = _np.stack([chan[:128], _np.concatenate([chan[128:]] * 2)], axis=1)
    wt = [src["L0_attn_W" + k].T for k in "kvro"]
    wattn = _np.stack([w[:128] for w in wt] + [_np.concatenate([w[128:]] * 2) for w in wt], axis=1)
    gt = src["L0_ffn_gate_weight"].T
    gate_t = _np.stack([gt[:128], _np.concatenate([gt[128:]] * 2)], axis=1)

    def ffn(g, u, d):
        g, u, d = (_np.swapaxes(x, -1, -2) for x in (g, u, d))
        d = d.reshape(d.shape[:-2] + (-1, 128, C))
        d = _np.swapaxes(d, -3, -2).reshape(d.shape[:-3] + (128, -1))
        low = _np.concatenate([g[..., 128:, :], u[..., 128:, :]], axis=-2)
        return _np.concatenate([g[..., :128, :], u[..., :128, :], low, d], axis=-1)

    wshared = ffn(*(src["L0_ffn_Ws_" + k] for k in "gud"))
    wexp = ffn(*(src["L0_ffn_W" + k] for k in "gud"))
    given = {"xwin": xwin, "wshift": wshift, "kconst": kconst, "proj_b": src["L0_tok_proj_bias"][None, :],
             "chan": chan, "wattn": wattn, "gate_t": gate_t, "wshared": wshared, "wexp": wexp}
    nc = _bacc.Bacc("TRN2", target_bir_lowering=False, num_devices=1)
    arrays, args = {}, []
    for name, a in given.items():
        a = _np.ascontiguousarray(a)
        arrays[f"in_{name}"] = a
        args.append(nc.dram_tensor(f"in_{name}", a.shape, _mybir.dt.from_np(a.dtype), kind="ExternalInput").ap())
    args.append(nc.dram_tensor("out_h", (T, C), _mybir.dt.float32, kind="ExternalOutput").ap())
    vit_tower_kernel(nc, *args)
    r = _run(nc, [arrays], core_ids=[0])
    return r.results[0]["out_h"].reshape(B, SEG, C)
```

```python
import concourse.bass as bass
from concourse import mybir
from contextlib import ExitStack

B, CH, HW, PATCH = 32, 3, 96, 16
SEG = (HW // PATCH) ** 2
T = B * SEG
C = 192
CB = C - 128
PD = PATCH * PATCH * 5 * CH
WIN = CH * ((PATCH + 2) ** 2 - 4)
KC = 120
NJ = WIN // KC
NT = T // 128
NS = T // SEG + T // SEG // 2
SA = B
HT = T // 2
E, TOPK = 16, 2
CAP = -(-T // E * TOPK)
HC = CAP // 2
F = 4 * C
FM = F // 128
FS = F * 2 // 4
FSM = FS // 128
XSC = 256.0
WSC = 2048.0
XH = 4 * 128 + 2 * E
FD = FM * C
WE = 2 * F + F + FD
WX = 2 * (2 * F + FD) + 2 * F
RING = 4
LN_EPS = 1e-5
NEG = -1e38


def vit_tower_kernel(nc, xwin, wshift, kconst, proj_b, chan, wattn, gate_t, wshared, wexp_gu, wexp_d, wexp_last, out):
    fp32 = mybir.dt.float32
    f16 = mybir.dt.float16
    bf16 = mybir.dt.bfloat16
    i32 = mybir.dt.int32
    u32 = mybir.dt.uint32
    ALU = mybir.AluOpType
    ACT = mybir.ActivationFunctionType
    AX = mybir.AxisListType
    ds = bass.ds

    ctx = ExitStack()
    with ctx:
        def sb(name, shape, dt=fp32):
            return ctx.enter_context(nc.sbuf_tensor(name, shape, dt))

        def sem(name):
            return ctx.enter_context(nc.semaphore(name))

        xrows = nc.dram_tensor("xrows", (T, XH // 2), i32).ap()

        SL = NS * (SEG + 1)
        R1 = sb("R1", [128, NJ * T + NJ * 5 * C])
        R2 = sb("R2", [128, 5 * SL])
        Xs = R1[0:KC, 0:NJ * T].rearrange("p (j t) -> p j t", j=NJ)
        Ws = R1[0:KC, NJ * T:NJ * T + NJ * 5 * C].rearrange("p (j s c) -> p j s c", j=NJ, s=5)
        Xq = R2[0:KC, 0:2 * T].rearrange("p (b t) -> p b t", b=2)
        KCN = sb("KCN", [KC, NJ, 11])
        ones = sb("ones", [128, 128])
        pbr = sb("pbr", [1, C])
        csum = sb("csum", [128, 2, C])
        st = sb("st", [128, 8, NT])
        nmu, ex2, musq, rstd0, rstd1, rstd2, half = (st[:, k, :] for k in range(7))
        bst = sb("bst", [128, NT, 6])
        bag = sb("bag", [128, NT, 2])
        h = sb("h", [128, NT, C])
        xn = sb("xn", [128, NT, C])
        XW = sb("XW", [128, NT * XH // 2], i32)
        Wc = XW[0:KC, 0:NJ * (C + 1)].bitcast(fp32).rearrange("p (j c) -> p j c", j=NJ)
        xr = XW[:].bitcast(f16).rearrange("p (i c) -> p i c", i=NT)
        ident = sb("ident", [128, 128])
        ident16 = sb("ident16", [128, 128], f16)
        chn = sb("chn", [128, 2, 5])
        mix1 = sb("mix1", [128, 2, 3])
        wdec = sb("wdec", [128, 2])
        WA = sb("WA", [128, 8, C])
        WG = sb("WG", [128, 2, E])
        GZ = sb("GZ", [128, 3, 8, 128], f16)
        WGs = sb("WGs", [128, 2, E])
        WGh = sb("WGh", [128, 3, E], f16)
        WS = sb("WS", [128, 2 * (2 * FS + FSM * C) + 2 * FS], f16)
        ring = sb("ring", [128, RING, WX], f16)

        def slot(R, k):
            return R[:, k * SL:(k + 1) * SL].rearrange("p (s t) -> p s t", s=NS)

        def flat(R, k, n=NS * SEG):
            return R[:, k * SL:k * SL + n]
        xt, dx = flat(R2, 0), flat(R2, 1)
        xm = [flat(R2, 2 + m) for m in range(3)]
        kp, wp, mm, cc, aa, bb, vv, bv, er = (slot(R1, k) for k in range(9))
        num, den, e1, e2, nn = (slot(R2, k) for k in range(5))
        tt = cc
        yy = flat(R1, 0)
        yA, yB = yy[:, 0:T], yy[:, T:T + HT]
        yv = yy.rearrange("p (s t) -> p s t", s=NS)
        xt2 = R2[:, 0:2 * T].bitcast(f16).rearrange("p (k t) -> p k t", k=4)
        o_fs = 2 * T
        sgs = R2[:, o_fs:o_fs + FSM * 384].rearrange("p (m t) -> p m t", m=FSM)
        hsf = R2[:, o_fs + FSM * 384:o_fs + 2 * FSM * 384].rearrange("p (m t) -> p m t", m=FSM)
        hsT = R2[:, o_fs + 2 * FSM * 384:o_fs + 3 * FSM * 384].bitcast(f16).rearrange("p (x m t) -> p x m t", x=2, m=FSM)
        o = [0]

        def carve(n, dt=None):
            a = R1[:, o[0]:o[0] + n]
            o[0] += n
            return a if dt is None else a.bitcast(dt)
        sc = carve(CAP)
        scr = carve(CAP)
        gt = carve(CAP)
        eq = carve(CAP)
        cum = carve(CAP)
        zc = carve(CAP)
        slt = carve(CAP)
        af = carve(CAP)
        bf = carve(CAP)
        ai = carve(CAP, i32)
        abT = R1[0:HC, o[0]:o[0] + 256].bitcast(f16).rearrange("p (d h q) -> p d h q", d=2, h=2)
        o[0] += 256
        A1 = R1[0:HC, o[0]:o[0] + 1024].bitcast(f16).rearrange("p (g q) -> p g q", g=16)
        o[0] += 1024
        A0 = R1[0:HC, o[0]:o[0] + 1024].bitcast(f16).rearrange("p (g q) -> p g q", g=16)
        o[0] += 1024
        B1 = R1[0:HC, o[0]:o[0] + 2304].bitcast(f16).rearrange("p (g q) -> p g q", g=16)
        o[0] += 2304
        Ld = carve(E * 18)
        L1 = carve(18)
        Lr = carve(HC)
        o_ex = o[0]
        yo = R1[0:HC, o[0]:o[0] + 4 * C].rearrange("p (b h c) -> p b h c", b=2, h=2)
        o[0] += 4 * C
        xg = R1[0:HC, o[0]:o[0] + 4 * XH].bitcast(f16).rearrange("p (b h c) -> p b h c", b=4, h=2)
        o[0] += 4 * XH
        xgi = xg.bitcast(i32)
        xgT = R1[:, o[0]:o[0] + 4 * CAP].bitcast(f16).rearrange("p (b k t) -> p b k t", b=2, k=4)
        o[0] += 4 * CAP
        raw = R1[:, o[0]:o[0] + 2 * WE].rearrange("p (b w) -> p b w", b=2)
        o[0] += 2 * WE
        assert o[0] <= NJ * T + NJ * 5 * C
        o_hot = 2 * T + 3 * FSM * 384
        sg = R2[:, o_hot:o_hot + FM * CAP].rearrange("p (m t) -> p m t", m=FM)
        hf = R2[:, o_hot + FM * CAP:o_hot + 2 * FM * CAP].rearrange("p (m t) -> p m t", m=FM)
        hT = R2[:, 0:2 * FM * CAP].bitcast(f16).rearrange("p (b x m t) -> p b x m t", b=2, x=2, m=FM)
        assert o_hot + 2 * FM * CAP <= 5 * SL
        small = sb("small", [128, 40])
        cand = sb("cand", [128, 1], i32)
        flip = sb("flip", [128, 1], i32)
        bits = sb("bits", [128, 31], i32)
        bitf = sb("bitf", [128, 31])
        cnt = sb("cnt", [128, 2], bf16)
        same = sb("same", [128, 128], bf16)
        before = sb("before", [128, 128], bf16)
        samef = sb("samef", [128, 2, 128])
        iota8 = sb("iota8", [HC, 8], f16)
        iota18 = sb("iota18", [HC, 18], f16)
        ids = sb("ids", [HC, 16], f16)
        emask = sb("emask", [128, E])
        amask = sb("amask", [128, 4])
        rmask = sb("rmask", [128, E, 2])
        idx = sb("idx", [HC, 2 * E], u32)
        ps = ctx.enter_context(nc.psum_tensor("ps", [128, 8, 512], fp32))

        s_kc = sem("s_kc")
        s_xw = [sem(f"s_xw{j}") for j in range(NJ)]
        s_ws = [sem(f"s_ws{j}") for j in range(NJ)]
        s_pb = sem("s_pb")
        s_ch = sem("s_ch")
        s_wa = sem("s_wa")
        s_wg = sem("s_wg")
        s_rawS = sem("s_rawS")
        s_raw = {x: [sem(f"s_raw{x}{k}") for k in range(2)] for x in "GDR"}
        s_hi = {x: sem(f"s_hi{x}") for x in "GDR"}
        s_lo = {x: sem(f"s_lo{x}") for x in "GDR"}
        s_shi = sem("s_shi")
        s_slo = sem("s_slo")
        s_xhi = sem("s_xhi")
        s_xlo = sem("s_xlo")
        s_gwh = sem("s_gwh")
        s_hs = sem("s_hs")
        s_hhi = sem("s_hhi")
        s_hf = sem("s_hf")
        s_hhi_s = sem("s_hhi_s")
        s_const = sem("s_const")
        s_ones = sem("s_ones")
        s_acc = sem("s_acc")
        s_wc = sem("s_wc")
        s_xq = sem("s_xq")
        s_sq = sem("s_sq")
        s_tok = sem("s_tok")
        s_b = sem("s_b")
        s_var = [sem(f"s_var{k}") for k in range(3)]
        s_rs = [sem(f"s_rs{k}") for k in range(3)]
        s_pl = sem("s_pl")
        s_xn = [sem(f"s_xn{k}") for k in range(2)]
        s_tp = [sem(f"s_tp{k}") for k in range(2)]
        s_xt = [sem(f"s_xt{k}") for k in range(2)]
        s_mix = sem("s_mix")
        s_w = sem("s_w")
        s_pad = sem("s_pad")
        s_proj = sem("s_proj")
        s_ev = sem("s_ev")
        s_v = sem("s_v")
        s_arg = sem("s_arg")
        s_exp = sem("s_exp")
        s_y = sem("s_y")
        s_at = sem("s_at")
        s_gz = sem("s_gz")
        s_sl = sem("s_sl")
        s_es = sem("s_es")
        s_st = sem("s_st")
        s_est = sem("s_est")
        s_row = sem("s_row")
        s_rowd = sem("s_rowd")
        s_cnt = sem("s_cnt")
        s_tot = sem("s_tot")
        s_r = sem("s_r")
        s_rp = sem("s_rp")
        s_gu = sem("s_gu")
        s_ssg = sem("s_ssg")
        s_sh = sem("s_sh")
        s_dn = sem("s_dn")
        s_ysh = sem("s_ysh")
        s_yd = sem("s_yd")
        s_idx = sem("s_idx")
        s_xg = [sem(f"s_xg{k}") for k in range(4)]
        s_xgt = sem("s_xgt")
        s_xgs = sem("s_xgs")
        s_eg = sem("s_eg")
        s_eu = sem("s_eu")
        s_sg = sem("s_sg")
        s_h = sem("s_h")
        s_ed = sem("s_ed")
        s_yo = sem("s_yo")
        s_add = [sem(f"s_add{k}") for k in range(2)]

        block = ctx.enter_context(nc.Block())

        scores = xr[:, :, 512:XH].bitcast(fp32)

        def split_hi(a, w, to, f, d, c0=0, c1=None):
            c1 = 2 * f + d if c1 is None else c1
            return a.activation(to[:, c0:c1], w[:, c0:c1], ACT.Copy, scale=WSC)

        def split_hi_last(a, w, to, f, d, u):
            n, p = 2 * f + d, 64 * u
            return a.activation(to[p:p + 64, 2 * n + f * u:2 * n + f * u + f], w[p:p + 64, n:n + f], ACT.Copy, scale=WSC)

        def split_lo(v, w, to, f, d, c0=0, c1=None):
            n = 2 * f + d
            c1 = n if c1 is None else c1
            return v.scalar_tensor_tensor(to[:, n + c0:n + c1], w[:, c0:c1], WSC, to[:, c0:c1], ALU.mult, ALU.subtract)

        def split_lo_last(v, w, to, f, d, u):
            n, p, q = 2 * f + d, 64 * u, 64 - 64 * u
            c = 2 * n + f * u
            return v.scalar_tensor_tensor(to[q:q + 64, c:c + f], w[p:p + 64, n:n + f], WSC, to[p:p + 64, c:c + f],
                                          ALU.mult, ALU.subtract)

        parts = {"R": (2 * F + FD, WE), "G": (0, 2 * F), "D": (2 * F, 2 * F + FD)}

        def tokcol(i):
            return i // 2, 256 * (i % 2)

        wexp = {"G": wexp_gu, "D": wexp_d, "R": wexp_last}

        @block.sync
        def _(sp):
            sp.dma_start(KCN[:], kconst).then_inc(s_kc, 16)
            for j in range(NJ):
                sp.dma_start(Ws[:, j], wshift[:, j]).then_inc(s_ws[j], 16)
                sp.dma_start(Xs[:, j], xwin[:, j]).then_inc(s_xw[j], 16)
            sp.dma_start(pbr[:], proj_b).then_inc(s_pb, 16)
            sp.dma_start(chn[:], chan).then_inc(s_ch, 16)
            sp.dma_start(WA[:], wattn).then_inc(s_wa, 16)
            sp.dma_start(WG[:], gate_t).then_inc(s_wg, 16)
            sp.wait_ge(s_y, 2)
            sp.dma_start(raw[:, 1, 0:3 * FS + FSM * C], wshared).then_inc(s_rawS, 16)
            for b in range(2):
                if b:
                    sp.wait_ge(s_slo, 1)
                for x, (c0, c1) in parts.items():
                    sp.dma_start(raw[:, b, c0:c1], wexp[x][b]).then_inc(s_raw[x][b], 16)
            sp.wait_ge(s_row, 1)
            sp.dma_start(xrows.rearrange("(i p) c -> p i c", p=128), XW[:].rearrange("p (i c) -> p i c", i=NT)).then_inc(s_rowd, 16)
            for n in range(3):
                sp.wait_ge(s_ysh, 3 * (n + 1))
                sp.dma_start(out[384 * n:384 * (n + 1), :].rearrange("(i p) c -> p i c", p=128),
                             h[:, 3 * n:3 * n + 3]).then_inc(s_yd, 16)
            wpair = {x: w.rearrange("(g b) p w -> g b p w", b=2) for x, w in wexp.items()}
            with sp.Fori(1, E // 2) as pair:
                for b in range(2):
                    for x, (c0, c1) in parts.items():
                        sp.wait_ge(s_lo[x], pair * 2 + (b - 1))
                        sp.dma_start(raw[:, b, c0:c1], wpair[x][ds(pair, 1), b].rearrange("a p w -> p (a w)")).then_inc(s_raw[x][b], 16)

        @block.gpsimd
        def _(pool):
            g = nc.gpsimd
            g.memset(half, -0.5)
            g.memset(ones[:], 1.0).then_inc(s_ones, 1)
            g.memset(ident[:], 1.0).then_inc(s_pl, 1)
            g.memset(samef[:], 1.0).then_inc(s_pl, 1)
            g.memset(emask[:], 1.0).then_inc(s_pl, 1)
            g.memset(rmask[:], 1.0).then_inc(s_pl, 1)
            g.memset(GZ[:], 0.0).then_inc(s_pl, 1)
            pool.wait_ge(s_pl, 5)
            g.affine_select(out=ident[:], in_=ident[:], compare_op=ALU.is_equal, fill=0.0, base=0,
                            pattern=[[-1, 128]], channel_multiplier=1).then_inc(s_const, 1)
            sv = samef[:, 0, :].rearrange("p (e s) -> p e s", e=E)
            g.affine_select(out=sv, in_=sv, compare_op=ALU.is_ge, fill=0.0, base=0,
                            pattern=[[-8, E], [0, 8]], channel_multiplier=1).then_inc(s_pl, 1)
            pool.wait_ge(s_pl, 6)
            g.affine_select(out=sv, in_=sv, compare_op=ALU.is_ge, fill=0.0, base=7,
                            pattern=[[8, E], [0, 8]], channel_multiplier=-1).then_inc(s_pl, 1)
            pool.wait_ge(s_pl, 7)
            g.affine_select(out=samef[:, 1, :], in_=samef[:, 0, :], compare_op=ALU.is_gt, fill=0.0, base=0,
                            pattern=[[1, 128]], channel_multiplier=-1).then_inc(s_pl, 1)
            pool.wait_ge(s_pl, 8)
            g.tensor_copy(same[:], samef[:, 0, :])
            pool.wait_ge(s_const, 1)
            g.tensor_copy(ident16[:], ident[:])
            g.tensor_copy(before[:], samef[:, 1, :]).then_inc(s_const, 1)
            g.affine_select(out=emask[:], in_=emask[:], compare_op=ALU.is_ge, fill=0.0, base=0,
                            pattern=[[-8, E]], channel_multiplier=1).then_inc(s_pl, 1)
            pool.wait_ge(s_pl, 9)
            g.affine_select(out=emask[:], in_=emask[:], compare_op=ALU.is_ge, fill=0.0, base=7,
                            pattern=[[8, E]], channel_multiplier=-1).then_inc(s_const, 1)
            g.affine_select(out=rmask[:], in_=rmask[:], compare_op=ALU.is_ge, fill=0.0, base=0,
                            pattern=[[-8, E], [-4, 2]], channel_multiplier=1).then_inc(s_pl, 1)
            pool.wait_ge(s_pl, 10)
            g.affine_select(out=rmask[:], in_=rmask[:], compare_op=ALU.is_ge, fill=0.0, base=3,
                            pattern=[[8, E], [4, 2]], channel_multiplier=-1).then_inc(s_const, 1)
            g.iota(iota8[:], pattern=[[1, 8]], base=0, channel_multiplier=0,
                   allow_small_or_imprecise_dtypes=True)
            g.iota(iota18[:], pattern=[[1, 18]], base=1, channel_multiplier=0,
                   allow_small_or_imprecise_dtypes=True)
            g.iota(ids[:].rearrange("p (h s) -> p h s", h=2), pattern=[[HC, 2], [CAP, 8]], base=0,
                   channel_multiplier=1, allow_small_or_imprecise_dtypes=True).then_inc(s_const, 1)
            for k, (v, r) in enumerate(((ex2, rstd0), (bag[:, :, 1], rstd1), (bag[:, :, 1], rstd2))):
                if k == 2:
                    pool.wait_ge(s_gwh, 2)
                    for w in range(3):
                        for s in range(8):
                            last = g.tensor_copy(GZ[:, w, s, :].rearrange("p (e q) -> p e q", e=E)[:, :, s], WGh[:, w, :])
                    last.then_inc(s_gz, 1)
                pool.wait_ge(s_var[k], 1)
                g.tensor_scalar(r, v, LN_EPS, None, ALU.add).then_inc(s_pl, 1)
                pool.wait_ge(s_pl, 11 + k)
                g.tensor_tensor(r, r, half, ALU.pow).then_inc(s_rs[k], 1)
            pool.wait_ge(s_idx, 1)
            pool.wait_ge(s_rowd, 16)

            def gather(e):
                if e >= 4:
                    pool.wait_ge(s_yo, e - 3)
                for hh in range(2):
                    g.indirect_dma_start(xgi[:, e % 4, hh, :], None, xrows,
                                         bass.IndirectOffsetOnAxis(idx[:, 2 * e + hh:2 * e + hh + 1], 0)).then_inc(s_xg[e % 4], 16)

            def scatter(e):
                pool.wait_ge(s_yo, e + 1)
                if e:
                    pool.wait_ge(s_add[0], e * 16)
                    pool.wait_ge(s_add[1], e * 16)
                for hh in range(2):
                    g.indirect_dma_start(out, bass.IndirectOffsetOnAxis(idx[:, 2 * e + hh:2 * e + hh + 1], 0),
                                         yo[:, e % 2, hh, :], None, compute_op=ALU.add).then_inc(s_add[hh], 16)

            for e in range(3):
                gather(e)
            pool.wait_ge(s_yd, 48)
            for e in range(E):
                for q in range(2):
                    pool.wait_ge(s_hhi, 2 * e + q + 1)
                    g.tensor_tensor(hT[:, e % 2, 1, 3 * q:3 * q + 3, :], hf[:, 3 * q:3 * q + 3, :],
                                    hT[:, e % 2, 0, 3 * q:3 * q + 3, :], ALU.subtract).then_inc(s_h, 1)
                if e:
                    scatter(e - 1)
                if e + 3 < E:
                    gather(e + 3)
            scatter(E - 1)
            pool.wait_ge(s_add[0], 16 * E)
            pool.wait_ge(s_add[1], 16 * E)

        @block.scalar
        def _(act):
            a = nc.scalar
            for j in range(NJ):
                act.wait_ge(s_xw[j], 16)
                if j >= 2:
                    act.wait_ge(s_sq, j - 1)
                a.activation(Xq[:, j % 2, :], Xs[:, j, :], ACT.Square).then_inc(s_xq, 1)
            act.wait_ge(s_ch, 16)
            a.activation(wdec[:], chn[:, :, 3], ACT.Exp).then_inc(s_w, 1)
            act.wait_ge(s_tp[0], 1)
            a.copy(xt[:, 0:512], ps[:, 0, :])
            a.copy(xt[:, 512:1024], ps[:, 1, :])
            a.copy(xt[:, 1024:T], ps[:, 2, 0:128])
            a.copy(xt[0:64, T:T + 512], ps[0:64, 3, :])
            a.copy(xt[0:64, T + 512:T + HT], ps[0:64, 4, 0:64])
            a.copy(xt[64:128, T:T + 448], ps[0:64, 4, 64:512])
            a.copy(xt[64:128, T + 448:T + HT], ps[0:64, 5, 0:128]).then_inc(s_xt[0], 1)
            act.wait_ge(s_pad, 1)
            for n in range(18):
                m, q = n // 6, n % 6
                src = ps[:, n % 8, 0:288].rearrange("p (s t) -> p s t", t=SEG)
                act.wait_ge(s_proj, n + 1)
                if m == 0:
                    i = a.copy(kp[:, 8 * q:8 * q + 8, 1:SEG + 1], src)
                elif m == 1:
                    i = a.copy(vv[:, 8 * q:8 * q + 8, 1:SEG + 1], src)
                else:
                    i = a.activation(er[:, 8 * q:8 * q + 8, 1:SEG + 1], src, ACT.Exp, scale=-1.0)
                i.then_inc(s_ev, 1)
            for part, (s0, s1) in enumerate(((0, SA), (SA, NS))):
                for k, x in enumerate((aa, bb, e1, e2)):
                    act.wait_ge(s_arg, 4 * part + k + 1)
                    a.activation(x[:, s0:s1, 1:], x[:, s0:s1, 1:], ACT.Exp).then_inc(s_exp, 1)
            for i in range(NT):
                act.wait_ge(s_xn[1], i + 1)
                a.copy(xr[:, i, 0:C], xn[:, i, :])
                a.copy(xr[:, i, C:256], xn[:, i, 128:C]).then_inc(s_xhi, 1)
            act.wait_ge(s_rawS, 16)
            split_hi(a, raw[:, 1, :], WS, FS, FSM * C)
            for u in range(2):
                last = split_hi_last(a, raw[:, 1, :], WS, FS, FSM * C, u)
            last.then_inc(s_shi, 1)

            def expert_hi_all(e):
                for x in "GDR":
                    act.wait_ge(s_raw[x][e], 16)
                for x in "GD":
                    split_hi(a, raw[:, e, :], ring[:, e, :], F, FD, *parts[x]).then_inc(s_hi[x], 1)
                split_hi_last(a, raw[:, e, :], ring[:, e, :], F, FD, 0)
                split_hi_last(a, raw[:, e, :], ring[:, e, :], F, FD, 1).then_inc(s_hi["R"], 1)

            expert_hi_all(0)
            for k in range(4):
                act.wait_ge(s_tp[1], k + 1)
                last = a.copy(xt2[:, k, 0:1024], ps[:, k, :].bitcast(f16))
            for k in range(4):
                last = a.copy(xt2[:, k, 1024:T], ps[:, 4, 64 * k:64 * k + 64].bitcast(f16))
            last.then_inc(s_xt[1], 1)
            act.wait_ge(s_sl, 1)
            a.activation(sc, ps[:, 6, 0:CAP], ACT.Exp, scale=-1.0 / (XSC * WSC)).then_inc(s_es, 1)
            act.wait_ge(s_st, 1)
            a.activation(scores, ps[:, 7, 0:NT * E].rearrange("p (i e) -> p i e", i=NT), ACT.Exp,
                         scale=-1.0 / (XSC * WSC)).then_inc(s_est, 1)
            for n in range(3):
                for m in range(FSM):
                    c = FSM * n + m
                    act.wait_ge(s_gu, c + 1)
                    if n:
                        act.wait_ge(s_hs, c + 1 - FSM)
                    a.activation(sgs[:, m, :], ps[:, 2 * (c % 2), 0:384], ACT.Silu, scale=1.0 / (XSC * WSC)).then_inc(s_ssg, 1)
                    act.wait_ge(s_hs, c + 1)
                    if n and m == 0:
                        act.wait_ge(s_dn, 3 * n)
                    a.copy(hsT[:, 0, m, :], hsf[:, m, :]).then_inc(s_hhi_s, 1)
            def xg_out(b):
                a.copy(xgT[:, b, :, :], ps[:, 4, 0:2 * CAP].bitcast(f16).rearrange("p (k t) -> p k t", k=4)).then_inc(s_xgs, 1)

            expert_hi_all(1)
            act.wait_ge(s_xgt, 1)
            xg_out(0)

            def gates(g4, k):
                e = g4 * 4 + k
                b = k % 2
                static = isinstance(g4, int)
                ahead = not (static and e + 2 >= E)
                landed = 8 * (e - k) + 16 * (k // 2) + 32
                to = ring[:, (k + 2) % RING, :]
                for q in range(2):
                    act.wait_ge(s_eg, 2 * e + q + 1)
                    a.activation(sg[:, 3 * q:3 * q + 3, :], ps[:, q, 0:3 * CAP].rearrange("p (m t) -> p m t", m=3),
                                 ACT.Silu, scale=1.0 / (XSC * WSC)).then_inc(s_sg, 1)
                    if q == 0:
                        if ahead:
                            act.wait_ge(s_raw["R"][b], landed)
                            split_hi_last(a, raw[:, b, :], to, F, FD, 0)
                        if not (static and e < 2):
                            act.wait_ge(s_ed, e - 1)
                    act.wait_ge(s_hf, 2 * e + q + 1)
                    a.copy(hT[:, b, 0, 3 * q:3 * q + 3, :], hf[:, 3 * q:3 * q + 3, :]).then_inc(s_hhi, 1)
                    if q == 0 and ahead:
                        split_hi_last(a, raw[:, b, :], to, F, FD, 1).then_inc(s_hi["R"], 1)
                if not (static and e == E - 1):
                    act.wait_ge(s_xgt, e + 2)
                    xg_out(1 - b)
                if ahead:
                    for x in "GD":
                        act.wait_ge(s_raw[x][b], landed)
                        split_hi(a, raw[:, b, :], to, F, FD, *parts[x]).then_inc(s_hi[x], 1)

            for k in range(4):
                gates(0, k)
            with act.Fori(1, E // 4 - 1) as g4:
                for k in range(4):
                    gates(g4, k)
            for k in range(4):
                gates(E // 4 - 1, k)

        @block.vector
        def _(dve):
            v = nc.vector
            dve.wait_ge(s_kc, 16)
            v.tensor_copy(Wc[:, :, C], KCN[:, :, 10])
            for j in range(NJ):
                dve.wait_ge(s_ws[j], 16)
                v.tensor_scalar(Wc[:, j, 0:C], Ws[:, j, 0, :], KCN[:, j, 0:1], None, ALU.mult).then_inc(s_acc, 1)
                for s in range(1, 5):
                    dve.wait_ge(s_acc, 4 * j + s)
                    v.scalar_tensor_tensor(Wc[:, j, 0:C], Ws[:, j, s, :], KCN[:, j, s:s + 1], Wc[:, j, 0:C],
                                           ALU.mult, ALU.add).then_inc(s_acc if s < 4 else s_wc, 1)
            for b in range(31):
                v.memset(bits[:, b:b + 1], 1 << (29 - b) if b < 30 else 0)
            last = None
            for b in range(31):
                last = v.memset(bitf[:, b:b + 1], float(1 << (29 - b)) if b < 30 else 0.0)
            v.memset(cand[:], 1 << 29)
            v.memset(small[:], 0.0)
            dve.wait_ge(s_tok, 1)
            v.tensor_scalar(nmu[:, 0:8].rearrange("p (a b) -> p a b", b=2),
                            ps[:, 0:4, :].rearrange("p a (b c) -> p a b c", b=2)[:, :, :, C], -1.0 / PD, None, ALU.mult)
            v.tensor_scalar(nmu[:, 8:9], ps[:, 4, C:C + 1], -1.0 / PD, None, ALU.mult).then_inc(s_b, 1)
            v.tensor_copy(csum[:], ps[:, 5, :].rearrange("p (a c) -> p a c", a=2)[:, :, 0:C]).then_inc(s_b, 1)
            dve.wait_ge(s_b, 2)
            v.tensor_tensor(musq, nmu, nmu, ALU.mult).then_inc(s_b, 1)
            dve.wait_ge(s_b, 3)
            v.scalar_tensor_tensor(ex2, ps[:, 6, 0:NT], 1.0 / PD, musq, ALU.mult, ALU.subtract).then_inc(s_var[0], 1)
            for i in range(NT):
                b, c = tokcol(i)
                v.scalar_tensor_tensor(h[:, i, :], csum[:, 0, :], nmu[:, i:i + 1], ps[:, b, c:c + C],
                                       ALU.mult, ALU.add).then_inc(s_b, 1)
            dve.wait_ge(s_rs[0], 1)
            for i in range(NT):
                dve.wait_ge(s_b, 4 + i)
                v.scalar_tensor_tensor(h[:, i, :], h[:, i, :], rstd0[:, i:i + 1], csum[:, 1, :],
                                       ALU.mult, ALU.add).then_inc(s_b, 1)

            def stats(n0, k):
                for i in range(NT):
                    dve.wait_ge(s_b, n0 - NT + i + 1)
                    v.bn_stats(bst[:, i, :], h[:, i, :]).then_inc(s_b, 1)
                for i in range(NT):
                    dve.wait_ge(s_b, n0 + i + 1)
                    last = v.bn_aggr(bag[:, i, :], bst[:, i, :])
                last.then_inc(s_var[k], 1)

            def normalise(k, r):
                dve.wait_ge(s_rs[k], 1)
                dve.wait_ge(s_var[k], 1)
                for i in range(NT):
                    last = v.tensor_scalar(xn[:, i, 0:C], h[:, i, :], bag[:, i, 0:1], r[:, i:i + 1],
                                           ALU.subtract, ALU.mult)
                    last.then_inc(s_xn[k - 1], 1)

            stats(3 + 2 * NT, 1)
            normalise(1, rstd1)
            dve.wait_ge(s_wg, 16)
            v.tensor_scalar(WGs[:], WG[:], WSC, None, ALU.mult).then_inc(s_gwh, 1)
            dve.wait_ge(s_gwh, 1)
            v.tensor_copy(WGh[:, 0, :], WGs[:, 0, :])
            v.tensor_copy(WGh[0:64, 2, :], WGs[0:64, 1, :]).then_inc(s_mix, 1)
            dve.wait_ge(s_mix, 1)
            v.tensor_tensor(WGh[:, 1, :], WGs[:, 0, :], WGh[:, 0, :], ALU.subtract)
            v.tensor_tensor(WGh[64:128, 2, :], WGs[0:64, 1, :], WGh[0:64, 2, :], ALU.subtract).then_inc(s_gwh, 1)
            v.tensor_scalar(mix1[:], chn[:, :, 0:3], -1.0, None, ALU.add).then_inc(s_mix, 1)
            v.memset(kp[:, :, 0], NEG)
            v.memset(vv[:, :, 0], 0.0)
            v.memset(mm[:, :, 0], NEG)
            v.memset(wp[:, :, 1:], 0.0)
            v.memset(wp[:, :, 0], NEG).then_inc(s_pad, 1)
            dve.wait_ge(s_w, 1)
            dve.wait_ge(s_pad, 1)
            for q, (s0, s1) in enumerate(((0, SA), (SA, NS))):
                v.tensor_scalar(wp[:, s0:s1, 1:], wp[:, s0:s1, 1:], wdec[:, q:q + 1], None, ALU.subtract).then_inc(s_v, 1)
            dve.wait_ge(s_xt[0], 1)
            v.tensor_tensor(dx[:, 1:], xt[:, 1:], xt[:, 0:NS * SEG - 1], ALU.subtract).then_inc(s_mix, 1)
            dve.wait_ge(s_mix, 3)
            v.tensor_copy(dx.rearrange("p (s t) -> p s t", t=SEG)[:, :, 0],
                          xt.rearrange("p (s t) -> p s t", t=SEG)[:, :, 0]).then_inc(s_mix, 1)
            dve.wait_ge(s_mix, 4)
            for m in range(3):
                for q, (c0, c1) in enumerate(((0, T), (T, T + HT))):
                    v.scalar_tensor_tensor(xm[m][:, c0:c1], dx[:, c0:c1], mix1[:, q, m:m + 1], xt[:, c0:c1],
                                           ALU.mult, ALU.add).then_inc(s_mix, 1)
            u = [2]

            def step(ins, s=s_v):
                ins.then_inc(s, 1)
                if s is s_v:
                    u[0] += 1
                    dve.wait_ge(s_v, u[0])
            dve.wait_ge(s_v, 2)
            for q, (s0, s1) in enumerate(((0, SA), (SA, NS))):
                def fl(x):
                    return x[:, s0:s1, :].rearrange("p s t -> p (s t)")

                def cur(x):
                    return x[:, s0:s1, 1:]

                def prev(x):
                    return x[:, s0:s1, 0:SEG]
                dve.wait_ge(s_ev, 4 if q == 0 else 6)
                step(v.tensor_tensor_scan(fl(mm), fl(wp), fl(kp), NEG, ALU.add, ALU.max))
                step(v.scalar_tensor_tensor(cur(cc), prev(mm), wp[:, s0, 1:2], cur(kp), ALU.add, ALU.subtract))
                v.tensor_scalar(cur(aa), cur(cc), 0.0, None, ALU.min).then_inc(s_arg, 1)
                v.tensor_scalar(cur(bb), cur(cc), -1.0, 0.0, ALU.mult, ALU.min).then_inc(s_arg, 1)
                v.memset(aa[:, s0:s1, 0], 0.0)
                v.memset(bv[:, s0:s1, 0], 0.0)
                v.memset(bb[:, s0:s1, 0], 0.0)
                dve.wait_ge(s_arg, 4 * q + 2)
                step(v.scalar_tensor_tensor(cur(cc), cur(kp), chn[:, q, 4:5], prev(mm), ALU.add, ALU.subtract))
                if q == 0:
                    dve.wait_ge(s_proj, 18)
                v.tensor_scalar(cur(e1), cur(cc), -1.0, 0.0, ALU.mult, ALU.min).then_inc(s_arg, 1)
                v.tensor_scalar(cur(e2), cur(cc), 0.0, None, ALU.min).then_inc(s_arg, 1)
                dve.wait_ge(s_ev, 10 if q == 0 else 12)
                dve.wait_ge(s_exp, 4 * q + 2)
                step(v.tensor_tensor(cur(bv), cur(bb), cur(vv), ALU.mult))
                v.tensor_tensor_scan(fl(num), fl(aa), fl(bv), 0.0, ALU.mult, ALU.add)
                step(v.tensor_tensor_scan(fl(den), fl(aa), fl(bb), 0.0, ALU.mult, ALU.add))
                dve.wait_ge(s_exp, 4 * q + 4)
                dve.wait_ge(s_arg, 4 * q + 4)
                v.tensor_tensor(cur(nn), cur(e1), prev(num), ALU.mult)
                step(v.tensor_tensor(cur(tt), cur(e2), cur(vv), ALU.mult))
                step(v.tensor_tensor(cur(nn), cur(nn), cur(tt), ALU.add))
                step(v.tensor_tensor(cur(e1), cur(e1), prev(den), ALU.mult))
                step(v.tensor_tensor(cur(e1), cur(e1), cur(e2), ALU.add))
                dve.wait_ge(s_ev, 16 if q == 0 else 18)
                step(v.scalar_tensor_tensor(cur(e1), cur(er), 1.0, cur(e1), ALU.add, ALU.mult))
                step(v.reciprocal(cur(e1), cur(e1)))
                v.tensor_tensor(yv[:, s0:s1, :], cur(nn), cur(e1), ALU.mult).then_inc(s_y, 1)
            for i in range(NT):
                dve.wait_ge(s_at, min(NT, i // 2 * 2 + 2))
                v.tensor_tensor(h[:, i, :], h[:, i, :], ps[:, i // 2, 256 * (i % 2):256 * (i % 2) + C],
                                ALU.add).then_inc(s_b, 1)
            stats(3 + 4 * NT, 2)
            dve.wait_ge(s_rs[2], 1)
            v.tensor_scalar(rstd2, rstd2, XSC, None, ALU.mult).then_inc(s_rs[2], 1)
            dve.wait_ge(s_rs[2], 2)
            normalise(2, rstd2)
            for i in range(NT):
                dve.wait_ge(s_xhi, i + 1)
                v.tensor_tensor(xr[:, i, 256:256 + C], xn[:, i, :], xr[:, i, 0:C], ALU.subtract)
                v.tensor_tensor(xr[:, i, 256 + C:512], xn[:, i, 128:C], xr[:, i, C:256], ALU.subtract).then_inc(s_xlo, 1)
            dve.wait_ge(s_shi, 1)
            split_lo(v, raw[:, 1, :], WS, FS, FSM * C)
            for u in range(2):
                last = split_lo_last(v, raw[:, 1, :], WS, FS, FSM * C, u)
            last.then_inc(s_slo, 1)

            def expert_lo(x, e, slot_, b):
                dve.wait_ge(s_hi[x], e + 1)
                if x == "R":
                    split_lo_last(v, raw[:, b, :], ring[:, slot_, :], F, FD, 0)
                    last = split_lo_last(v, raw[:, b, :], ring[:, slot_, :], F, FD, 1)
                else:
                    last = split_lo(v, raw[:, b, :], ring[:, slot_, :], F, FD, *parts[x])
                last.then_inc(s_lo[x], 1)

            for x in "GDR":
                expert_lo(x, 0, 0, 0)
            r = [0]

            def rs(ins):
                r[0] += 1
                ins.then_inc(s_r, 1)
                dve.wait_ge(s_r, r[0])

            dve.wait_ge(s_es, 1)
            rs(v.tensor_scalar(sc, sc, 1.0, None, ALU.add))
            rs(v.reciprocal(sc, sc))

            def count():
                v.tensor_scalar(scr, sc, cand[:].bitcast(fp32), None, ALU.is_ge, ALU.add,
                                accum_out=cnt[:, 0:1]).then_inc(s_cnt, 1)

            def decide(b):
                dve.wait_ge(s_tot, b + 1)
                rs(v.tensor_scalar(flip[:], ps[:, 7, 256:257], CAP - 0.5, bitf[:, b:b + 1], ALU.is_lt, ALU.mult))
                rs(v.scalar_tensor_tensor(cand[:], cand[:], bits[:, b + 1:b + 2], flip[:], ALU.bitwise_xor, ALU.bitwise_xor))

            def shared_up(c):
                n, m = c // FSM, c % FSM
                dve.wait_ge(s_ssg, c + 1)
                if n:
                    dve.wait_ge(s_sh, c + 1 - FSM)
                v.scalar_tensor_tensor(hsf[:, m, :], ps[:, 2 * (c % 2) + 1, 0:384], 1.0 / WSC, sgs[:, m, :],
                                       ALU.mult, ALU.mult).then_inc(s_hs, 1)

            def shared_lo(c):
                m = c % FSM
                dve.wait_ge(s_hhi_s, c + 1)
                v.tensor_tensor(hsT[:, 1, m, :], hsf[:, m, :], hsT[:, 0, m, :], ALU.subtract).then_inc(s_sh, 1)

            def shared_out(i):
                dve.wait_ge(s_dn, i + 1)
                v.scalar_tensor_tensor(h[:, i, :], ps[:, 4 + i % 2, 0:C], 1.0 / (XSC * WSC), h[:, i, :],
                                       ALU.mult, ALU.add).then_inc(s_ysh, 1)

            count()
            b = 0
            for n in range(3):
                for m in range(FSM):
                    decide(b), count()
                    if m:
                        shared_lo(FSM * n + m - 1)
                    decide(b + 1), count()
                    b += 2
                    shared_up(FSM * n + m)
                    if n == 0 and m == 0:
                        dve.wait_ge(s_est, 1)
                        rs(v.tensor_scalar(scores, scores, 1.0, None, ALU.add))
                        v.reciprocal(scores, scores).then_inc(s_row, 1)
                shared_lo(FSM * n + 2)
                for i in range(3):
                    decide(b)
                    if b < 29:
                        count()
                    b += 1
                    shared_out(3 * n + i)
            for b in range(b, 30):
                decide(b)
                if b < 29:
                    count()
            thr = cand[:].bitcast(fp32)
            v.tensor_scalar(gt, sc, thr, None, ALU.is_gt, ALU.add, accum_out=cnt[:, 0:1])
            rs(v.tensor_scalar(eq, sc, thr, None, ALU.is_equal, ALU.add, accum_out=cnt[:, 1:2]))
            v.memset(zc, 1.0).then_inc(s_cnt, 1)
            dve.wait_ge(s_cnt, 31)
            rs(v.tensor_tensor_scan(cum, zc, eq, 0.0, ALU.mult, ALU.add))
            dve.wait_ge(s_rp, 1)
            v.tensor_scalar(small[:, 0:1], ps[:, 7, 258:259], -1.0, float(CAP), ALU.mult, ALU.add)
            rs(v.tensor_copy(small[:, 1:2], ps[:, 7, 259:260]))
            rs(v.tensor_scalar(cum, cum, small[:, 1:2], small[:, 0:1], ALU.add, ALU.is_le))
            rs(v.tensor_tensor(eq, eq, cum, ALU.mult))
            rs(v.tensor_tensor(gt, gt, eq, ALU.add))
            rs(v.tensor_tensor_scan(cum, zc, gt, 0.0, ALU.mult, ALU.add))
            v.tensor_copy(cnt[:, 0:1], cum[:, CAP - 1:CAP]).then_inc(s_cnt, 1)
            dve.wait_ge(s_rp, 2)
            rs(v.tensor_copy(small[:, 2:3], ps[:, 7, 260:261]))
            rs(v.scalar_tensor_tensor(slt, cum, small[:, 2:3], gt, ALU.add, ALU.mult))
            rs(v.tensor_scalar(ai, slt, 1.0 / 18, -9.5 / 18, ALU.mult, ALU.add))
            rs(v.tensor_copy(af, ai))
            v.scalar_tensor_tensor(bf, af, -18.0, slt, ALU.mult, ALU.add).then_inc(s_cnt, 1)
            dve.wait_ge(s_rp, 3)
            rs(v.tensor_copy(abT, ps[0:HC, 6, :].rearrange("p (d h q) -> p d h q", d=2, h=2)))
            dve.wait_ge(s_const, 5)
            for hh in range(2):
                srcA = abT[:, 0, hh, :].rearrange("p (e s) -> p s e", e=E)
                srcB = abT[:, 1, hh, :].rearrange("p (e s) -> p s e", e=E)
                for s in range(8):
                    g_ = 8 * hh + s
                    v.tensor_tensor(A0[:, g_, :].rearrange("p (e a) -> p e a", e=E),
                                    srcA[:, s, :].unsqueeze(2).to_broadcast([HC, E, 8]),
                                    iota8[:].unsqueeze(1).to_broadcast([HC, E, 8]), ALU.is_equal)
                    v.tensor_tensor(B1[:, g_, :].rearrange("p (e a) -> p e a", e=E),
                                    srcB[:, s, :].unsqueeze(2).to_broadcast([HC, E, 18]),
                                    iota18[:].unsqueeze(1).to_broadcast([HC, E, 18]), ALU.is_equal)
            rs(v.memset(small[:, 3:4], 0.0))
            v.tensor_tensor(A1, A0, ids[:].unsqueeze(2).to_broadcast([HC, 16, 128]), ALU.mult).then_inc(s_cnt, 1)
            dve.wait_ge(s_const, 1)
            v.tensor_reduce(amask[:], ident[:].rearrange("p (q a) -> p a q", a=4), AX.X, ALU.add)
            dve.wait_ge(s_rp, 4)
            rs(v.tensor_tensor(Ld.rearrange("p (e b) -> p e b", e=E), ps[:, 6, 0:E * 18].rearrange("p (e b) -> p e b", e=E),
                               emask[:].unsqueeze(2).to_broadcast([128, E, 18]), ALU.mult))
            rs(v.tensor_reduce(L1, Ld.rearrange("p (e b) -> p b e", e=E), AX.X, ALU.add))
            v.tensor_tensor(Lr.rearrange("p (a b) -> p a b", a=4), L1.unsqueeze(1).to_broadcast([128, 4, 18]),
                            amask[:].unsqueeze(2).to_broadcast([128, 4, 18]), ALU.mult).then_inc(s_cnt, 1)
            dve.wait_ge(s_rp, 5)
            v.tensor_copy(idx[:], ps[0:HC, 7, 320:320 + 2 * E]).then_inc(s_idx, 1)
            def outputs(g4, k):
                e = g4 * 4 + k
                dve.wait_ge(s_ed, e + 1)
                if not (isinstance(g4, int) and e < 2):
                    dve.wait_ge(s_add[0], (e - 1) * 16)
                    dve.wait_ge(s_add[1], (e - 1) * 16)
                for hh in range(2):
                    last = v.tensor_scalar(yo[:, k % 2, hh, :], ps[0:HC, 5 + k % 2, 256 * hh:256 * hh + C],
                                           xg[:, k, hh, 512:XH].bitcast(fp32)[:, ds(e, 1)], 1.0 / (XSC * WSC),
                                           ALU.mult, ALU.mult)
                last.then_inc(s_yo, 1)

            def hidden(g4, k):
                e = g4 * 4 + k
                ahead = not (isinstance(g4, int) and e + 1 >= E)
                nxt = (e + 1, (k + 1) % RING, (k + 1) % 2)
                if ahead:
                    expert_lo("R", *nxt)
                for q in range(2):
                    dve.wait_ge(s_sg, 2 * e + q + 1)
                    dve.wait_ge(s_eu, 2 * e + q + 1)
                    if not (isinstance(g4, int) and e == 0):
                        dve.wait_ge(s_h, 2 * e + q - 1)
                    v.scalar_tensor_tensor(hf[:, 3 * q:3 * q + 3, :], ps[:, 2 + q, 0:3 * CAP].rearrange("p (m t) -> p m t", m=3),
                                           1.0 / WSC, sg[:, 3 * q:3 * q + 3, :], ALU.mult, ALU.mult).then_inc(s_hf, 1)
                    if ahead:
                        expert_lo("GD"[q], *nxt)

            def group(g4):
                for k in range(4):
                    hidden(g4, k)
                    if not (isinstance(g4, int) and g4 == 0 and k == 0):
                        outputs(g4 if k else g4 - 1, (k + 3) % 4)
            group(0)
            with dve.Fori(1, E // 4 - 1) as g4:
                group(g4)
            group(E // 4 - 1)
            outputs(E // 4 - 1, 3)

        @block.tensor
        def _(pe):
            t = nc.tensor
            pe.wait_ge(s_kc, 16)
            pe.wait_ge(s_ones, 1)
            for j in range(NJ):
                pe.wait_ge(s_ws[j], 16)
                for s in range(5):
                    t.matmul(ps[:, 5, 256:256 + C], KCN[:, j, 5 + s:6 + s].to_broadcast([KC, 128]), Ws[:, j, s, :],
                             start=(j == 0 and s == 0), stop=False, skip_group_check=True)
                pe.wait_ge(s_xw[j], 16)
                pe.wait_ge(s_wc, j + 1)
                t.matmul(ps[:, 5, 0:C], ones[0:KC, :], Wc[:, j, 0:C], start=False, stop=(j == NJ - 1),
                         skip_group_check=True)
                for i in range(NT):
                    b, c = tokcol(i)
                    t.matmul(ps[:, b, c:c + C + 1], Xs[:, j, 128 * i:128 * i + 128], Wc[:, j, :],
                             start=(j == 0 and c == 0), stop=(j == NJ - 1), skip_group_check=True)
                pe.wait_ge(s_xq, j + 1)
                for i in range(NT):
                    last = t.matmul(ps[:, 6, i:i + 1], Xq[:, j % 2, 128 * i:128 * i + 128], Wc[:, j, C:C + 1],
                                    start=(j == 0 and i == 0), stop=(j == NJ - 1), skip_group_check=True)
                last.then_inc(s_sq, 1)
            pe.wait_ge(s_pb, 16)
            t.matmul(ps[:, 5, 256:256 + C], ones[0:1, :], pbr[0:1, :], start=False, stop=True,
                     skip_group_check=True).then_inc(s_tok, 1)

            for i in range(NT):
                if i == 0:
                    pe.wait_ge(s_const, 1)
                pe.wait_ge(s_xn[0], i + 1)
                t.transpose(ps[:, i // 4, 128 * (i % 4):128 * (i % 4) + 128], xn[:, i, 0:128], ident[:])
                last = t.transpose(ps[0:64, 3 + i // 4, 128 * (i % 4):128 * (i % 4) + 128], xn[:, i, 128:C], ident[:])
            last.then_inc(s_tp[0], 1)
            pe.wait_ge(s_wa, 16)
            pe.wait_ge(s_xt[0], 1)
            for n in range(18):
                m, q = n // 6, n % 6
                if n >= 8:
                    pe.wait_ge(s_ev, n - 7)
                pe.wait_ge(s_mix, 4 + 2 * (m + 1))
                if q < 4:
                    hf = q // 2
                    o_ = ps[:, n % 8, 0:288]
                    t.matmul(o_, WA[:, m, 0:128], xm[m][:, 288 * q:288 * q + 288], start=True, stop=False)
                    t.matmul(o_, WA[64 * hf:64 * hf + 64, 4 + m, 0:128],
                             xm[m][64 * hf:64 * hf + 64, T + 288 * (q % 2):T + 288 * (q % 2) + 288],
                             start=False, stop=True).then_inc(s_proj, 1)
                else:
                    for hf in range(2):
                        o_ = ps[64 * hf:64 * hf + 64, n % 8, 0:288]
                        c = HT * hf + 288 * (q - 4)
                        t.matmul(o_, WA[:, m, 128:C], xm[m][:, c:c + 288], start=True, stop=False)
                        last = t.matmul(o_, WA[64 * hf:64 * hf + 64, 4 + m, 128:C],
                                        xm[m][64 * hf:64 * hf + 64, T + 288 * (q - 4):T + 288 * (q - 4) + 288],
                                        start=False, stop=True)
                    last.then_inc(s_proj, 1)
            pe.wait_ge(s_ev, 18)
            pe.wait_ge(s_y, 2)
            for i in range(NT):
                b, c = tokcol(i)
                t.matmul(ps[:, b, c:c + C], yA[:, 128 * i:128 * i + 128], WA[:, 3, :], start=(c == 0), stop=False,
                         skip_group_check=True)
                pieces = ([(0, 128, 0, 128 * i)] if i < 4 else [(0, 64, 0, 512), (64, 128, 64, 0)] if i == 4
                          else [(0, 128, 64, 128 * i - HT)])
                for p0, p1, k0, c0 in pieces:
                    last = t.matmul(ps[p0:p1, b, c:c + C], yB[k0:k0 + 64, c0:c0 + p1 - p0], WA[k0:k0 + 64, 7, :],
                                    start=False, stop=True, skip_group_check=True)
                last.then_inc(s_at, 1)
            pe.wait_ge(s_const, 2)
            for k in range(4):
                for i in range(NT):
                    pe.wait_ge(s_xhi if k < 2 else s_xlo, i + 1)
                    to = ps[:, k, 64 * i:64 * i + 64] if i < 8 else ps[:, 4, 64 * k:64 * k + 64]
                    last = t.transpose(to.bitcast(f16), xr[:, i, 128 * k:128 * k + 128], ident16[:])
                last.then_inc(s_tp[1], 1)
            pe.wait_ge(s_xt[1], 1)
            pe.wait_ge(s_gz, 1)
            terms = ((0, 0), (1, 0), (0, 2), (2, 1), (2, 3))
            for s in range(8):
                for x, (w, k) in enumerate(terms):
                    last = t.matmul(ps[:, 6, 0:CAP], GZ[:, w, s, :], xt2[:, k, CAP * s:CAP * s + CAP],
                                    start=(s == 0 and x == 0), stop=(s == 7 and x == 4))
            last.then_inc(s_sl, 1)
            for i in range(NT):
                for x, (w, k) in enumerate(terms):
                    last = t.matmul(ps[:, 7, E * i:E * i + E], xt2[:, k, 128 * i:128 * i + 128], WGh[:, w, :],
                                    start=(x == 0), stop=(x == 4))
            last.then_inc(s_st, 1)
            pe.wait_ge(s_est, 1)
            pe.wait_ge(s_slo, 1)

            def split_product(o_, W, f, d, w, m, x):
                n = 2 * f + d
                hi = f * w + 128 * m
                last_ch = 2 * n + f * w + 128 * m
                for y, (c, k) in enumerate(((hi, 0), (n + hi, 0), (hi, 2), (last_ch, 1), (last_ch, 3))):
                    last = t.matmul(o_, W[:, c:c + 128], x[k], start=(y == 0), stop=(y == 4))
                return last

            def total(b):
                pe.wait_ge(s_cnt, b + 1)
                t.matmul(ps[:, 7, 256:257], same[:], cnt[:, 0:1], start=True, stop=True).then_inc(s_tot, 1)

            b = 0
            for n in range(3):
                for m in range(FSM):
                    c = FSM * n + m
                    if c >= 2:
                        pe.wait_ge(s_sh, c - 1)
                    for w in range(2):
                        o_ = ps[:, 2 * (c % 2) + w, 0:384]
                        last = split_product(o_, WS, FS, FSM * C, w, m, [xt2[:, k, 384 * n:384 * n + 384] for k in range(4)])
                        if w == 0:
                            total(b)
                        else:
                            last.then_inc(s_gu, 1)
                            total(b + 1)
                    b += 2
                pe.wait_ge(s_sh, FSM * (n + 1))
                for i in range(3):
                    ti = 3 * n + i
                    if ti >= 2:
                        pe.wait_ge(s_ysh, ti - 1)
                    for m in range(FSM):
                        for y, (x, w) in enumerate(((0, 0), (0, 1), (1, 0))):
                            c = (2 * FS + FSM * C) * w + 2 * FS + C * m
                            last = t.matmul(ps[:, 4 + ti % 2, 0:C], hsT[:, x, m, 128 * i:128 * i + 128], WS[:, c:c + C],
                                            start=(m == 0 and y == 0), stop=(m == FSM - 1 and y == 2))
                    last.then_inc(s_dn, 1)
                    total(b)
                    b += 1
            for b in range(b, 30):
                total(b)
            pe.wait_ge(s_cnt, 31)
            t.matmul(ps[:, 7, 258:259], same[:], cnt[:, 0:1], start=True, stop=True)
            t.matmul(ps[:, 7, 259:260], before[:], cnt[:, 1:2], start=True, stop=True).then_inc(s_rp, 1)
            pe.wait_ge(s_cnt, 32)
            t.matmul(ps[:, 7, 260:261], before[:], cnt[:, 0:1], start=True, stop=True).then_inc(s_rp, 1)
            pe.wait_ge(s_cnt, 33)
            for d, x in enumerate((af, bf)):
                for hh in range(2):
                    last = t.transpose(ps[0:HC, 6, 256 * d + 128 * hh:256 * d + 128 * hh + 128],
                                       x[:, HC * hh:HC * hh + HC], ident[:])
            last.then_inc(s_rp, 1)
            pe.wait_ge(s_cnt, 34)
            for g_ in range(16):
                last = t.matmul(ps[:, 6, 0:E * 18], A1[:, g_, :], B1[:, g_, :], start=(g_ == 0), stop=(g_ == 15))
            last.then_inc(s_rp, 1)
            pe.wait_ge(s_cnt, 35)
            pe.wait_ge(s_const, 4)
            t.matmul(ps[0:HC, 7, 320:320 + 2 * E], Lr, rmask[:].rearrange("p e h -> p (e h)"), start=True,
                     stop=True).then_inc(s_rp, 1)

            def xg_in(k):
                for hh in range(2):
                    for x in range(4):
                        o_ = ps[:, 4, HC * x + HC // 2 * hh:HC * x + HC // 2 * hh + HC // 2]
                        last = t.transpose(o_.bitcast(f16), xg[:, k, hh, 128 * x:128 * x + 128], ident16[0:HC, 0:HC])
                last.then_inc(s_xgt, 1)

            def up(g4, k):
                e = g4 * 4 + k
                b = k % 2
                pe.wait_ge(s_lo["G"], e + 1)
                pe.wait_ge(s_lo["R"], e + 1)
                pe.wait_ge(s_xgs, e + 1)
                for q in range(2):
                    if not (isinstance(g4, int) and e == 0):
                        pe.wait_ge(s_hf, 2 * e + q - 1)
                    for w in range(2):
                        for m in range(3 * q, 3 * q + 3):
                            o_ = ps[:, 2 * w + q, CAP * (m - 3 * q):CAP * (m - 3 * q) + CAP]
                            last = split_product(o_, ring[:, k, :], F, FD, w, m, [xgT[:, b, x, :] for x in range(4)])
                        last.then_inc(s_eg if w == 0 else s_eu, 1)
                if not (isinstance(g4, int) and e == E - 1):
                    pe.wait_ge(s_xg[(k + 1) % 4], g4 * 32 + 32 * ((k + 1) // 4 + 1))
                    xg_in((k + 1) % 4)

            def down(g4, k):
                e = g4 * 4 + k
                pe.wait_ge(s_h, 2 * e + 2)
                pe.wait_ge(s_lo["D"], e + 1)
                if not (isinstance(g4, int) and e < 2):
                    pe.wait_ge(s_yo, e - 1)
                for hh in range(2):
                    for m in range(FM):
                        for y, (x, w) in enumerate(((0, 0), (0, 1), (1, 0))):
                            c = (2 * F + FD) * w + 2 * F + C * m
                            last = t.matmul(ps[0:HC, 5 + k % 2, 256 * hh:256 * hh + C],
                                            hT[:, k % 2, x, m, HC * hh:HC * hh + HC], ring[:, k, c:c + C],
                                            start=(m == 0 and y == 0), stop=(m == FM - 1 and y == 2))
                last.then_inc(s_ed, 1)

            def group(g4):
                for k in range(4):
                    up(g4, k)
                    if not (isinstance(g4, int) and g4 == 0 and k == 0):
                        down(g4 if k else g4 - 1, (k + 3) % 4)

            pe.wait_ge(s_xg[0], 32)
            xg_in(0)
            group(0)
            with pe.Fori(1, E // 4 - 1) as g4:
                group(g4)
            group(E // 4 - 1)
            down(E // 4 - 1, 3)


def kernel(**inputs):
    import numpy as _np
    import concourse.bacc as _bacc
    from concourse import mybir as _mybir
    from concourse.bass_utils import run_bass_kernel_spmd as _run

    src = {k: _np.asarray(v) for k, v in inputs.items()}
    W2 = PATCH + 2
    pix = [(c, r, s) for c in range(CH) for r in range(W2) for s in range(W2)
           if not (r in (0, W2 - 1) and s in (0, W2 - 1))]
    pc, pr, pw = (_np.array([p[k] for p in pix]) for k in range(3))
    xp = _np.pad(src["x"], ((0, 0), (0, 0), (1, 1), (1, 1)))
    n = HW // PATCH
    rows = pr[None, :] + PATCH * _np.arange(n)[:, None]
    cols = pw[None, :] + PATCH * _np.arange(n)[:, None]
    win = xp[:, pc[None, None, :], rows[:, None, :], cols[None, :, :]]
    xwin = win.reshape(T, NJ, KC).transpose(2, 1, 0)
    places = ((1, 1), (1, 0), (1, 2), (0, 1), (2, 1))

    def in_window(a):
        w = a.reshape(PATCH, PATCH, 5, CH, -1)
        full = _np.zeros((5, CH, W2, W2, w.shape[-1]), a.dtype)
        for s, (r, c) in enumerate(places):
            full[s, :, r:r + PATCH, c:c + PATCH] = w[:, :, s].transpose(2, 0, 1, 3)
        return full[:, pc, pr, pw].reshape(5, NJ, KC, -1).transpose(2, 1, 0, 3)

    wshift = in_window(src["L0_tok_proj_weight"].T)
    lnw = in_window(src["L0_tok_ln_weight"])[..., 0]
    lnb = in_window(src["L0_tok_ln_bias"])[..., 0]
    times = _np.zeros((CH, W2, W2), _np.float32)
    for r, c in places:
        times[:, r:r + PATCH, c:c + PATCH] += 1
    times = times[pc, pr, pw].reshape(NJ, KC).T[:, :, None]
    kconst = _np.concatenate([lnw, lnb, times], axis=2)
    chan = _np.stack([src["L0_attn_" + k] for k in ("mix_k", "mix_v", "mix_r", "time_decay", "time_first")], axis=1)
    chan = _np.stack([chan[:128], _np.concatenate([chan[128:]] * 2)], axis=1)
    wt = [src["L0_attn_W" + k].T for k in "kvro"]
    wattn = _np.stack([w[:128] for w in wt] + [_np.concatenate([w[128:]] * 2) for w in wt], axis=1)
    gt = src["L0_ffn_gate_weight"].T
    gate_t = _np.stack([gt[:128], _np.concatenate([gt[128:]] * 2)], axis=1)

    def ffn(g, u, d):
        g, u, d = (_np.swapaxes(x, -1, -2) for x in (g, u, d))
        d = d.reshape(d.shape[:-2] + (-1, 128, C))
        d = _np.swapaxes(d, -3, -2).reshape(d.shape[:-3] + (128, -1))
        low = _np.concatenate([g[..., 128:, :], u[..., 128:, :]], axis=-2)
        return _np.concatenate([g[..., :128, :], u[..., :128, :], d, low], axis=-1)

    wshared = ffn(*(src["L0_ffn_Ws_" + k] for k in "gud"))
    wexp = ffn(*(src["L0_ffn_W" + k] for k in "gud"))
    given = {"xwin": xwin, "wshift": wshift, "kconst": kconst, "proj_b": src["L0_tok_proj_bias"][None, :],
             "chan": chan, "wattn": wattn, "gate_t": gate_t, "wshared": wshared,
             "wexp_gu": wexp[..., :2 * F], "wexp_d": wexp[..., 2 * F:-F], "wexp_last": wexp[..., -F:]}
    nc = _bacc.Bacc("TRN2", target_bir_lowering=False, num_devices=1)
    arrays, args = {}, []
    for name, a in given.items():
        a = _np.ascontiguousarray(a)
        arrays[f"in_{name}"] = a
        args.append(nc.dram_tensor(f"in_{name}", a.shape, _mybir.dt.from_np(a.dtype), kind="ExternalInput").ap())
    args.append(nc.dram_tensor("out_h", (T, C), _mybir.dt.float32, kind="ExternalOutput").ap())
    vit_tower_kernel(nc, *args)
    r = _run(nc, [arrays], core_ids=[0])
    return r.results[0]["out_h"].reshape(B, SEG, C)
```

```python
import concourse.bass as bass
from concourse import mybir
from contextlib import ExitStack

B, CH, HW, PATCH = 32, 3, 96, 16
SEG = (HW // PATCH) ** 2
T = B * SEG
C = 192
CB = C - 128
PD = PATCH * PATCH * 5 * CH
WIN = CH * ((PATCH + 2) ** 2 - 4)
KC = 120
NJ = WIN // KC
NT = T // 128
NS = T // SEG + T // SEG // 2
SA = B
HT = T // 2
E, TOPK = 16, 2
CAP = -(-T // E * TOPK)
HC = CAP // 2
F = 4 * C
FM = F // 128
FS = F * 2 // 4
FSM = FS // 128
XSC = 256.0
WSC = 2048.0
XH = 4 * 128 + 2 * E
FD = FM * C
WE = 2 * F + F + FD
WX = 2 * (2 * F + FD) + 2 * F
RING = 4
ROUNDS = 15
LN_EPS = 1e-5
NEG = -1e38


def vit_tower_kernel(nc, xwin, wshift, kconst, proj_b, chan, wattn, gate_t, wshared, wexp_gu, wexp_d, wexp_last, out):
    fp32 = mybir.dt.float32
    f16 = mybir.dt.float16
    bf16 = mybir.dt.bfloat16
    i32 = mybir.dt.int32
    u32 = mybir.dt.uint32
    ALU = mybir.AluOpType
    ACT = mybir.ActivationFunctionType
    AX = mybir.AxisListType
    ds = bass.ds

    ctx = ExitStack()
    with ctx:
        def sb(name, shape, dt=fp32):
            return ctx.enter_context(nc.sbuf_tensor(name, shape, dt))

        def sem(name):
            return ctx.enter_context(nc.semaphore(name))

        xrows = nc.dram_tensor("xrows", (T, XH // 2), i32).ap()

        SL = NS * (SEG + 1)
        R1 = sb("R1", [128, NJ * T + NJ * 5 * C])
        R2 = sb("R2", [128, 5 * SL])
        Xs = R1[0:KC, 0:NJ * T].rearrange("p (j t) -> p j t", j=NJ)
        Ws = R1[0:KC, NJ * T:NJ * T + NJ * 5 * C].rearrange("p (j s c) -> p j s c", j=NJ, s=5)
        Xq = R2[0:KC, 0:2 * T].rearrange("p (b t) -> p b t", b=2)
        sqs = R2[0:KC, 2 * T:3 * T]
        o_lb = 3 * T
        lbp = R2[0:KC, o_lb:o_lb + 10 * C].rearrange("p (b s c) -> p b s c", b=2, s=5)
        lbs = R2[0:KC, o_lb + 10 * C:o_lb + 15 * C].rearrange("p (s c) -> p s c", s=5)
        KCN = sb("KCN", [KC, NJ, 11])
        ones = sb("ones", [128, 128])
        pbr = sb("pbr", [1, C])
        csum = sb("csum", [128, 2, C])
        st = sb("st", [128, 8, NT])
        nmu, ex2, musq, rstd0, rstd1, rstd2, half = (st[:, k, :] for k in range(7))
        bst = sb("bst", [128, NT, 6])
        bag = sb("bag", [128, NT, 2])
        h = sb("h", [128, NT, C])
        xn = sb("xn", [128, NT, C])
        XW = sb("XW", [128, NT * XH // 2], i32)
        Wc = XW[0:KC, 0:NJ * (C + 1)].bitcast(fp32).rearrange("p (j c) -> p j c", j=NJ)
        xr = XW[:].bitcast(f16).rearrange("p (i c) -> p i c", i=NT)
        ident = sb("ident", [128, 128])
        ident16 = sb("ident16", [128, 128], f16)
        chn = sb("chn", [128, 2, 5])
        mix1 = sb("mix1", [128, 2, 3])
        wdec = sb("wdec", [128, 2])
        early = sb("early", [128, 1])
        WA = sb("WA", [128, 8, C])
        WG = sb("WG", [128, 2, E])
        GZ = sb("GZ", [128, 3, 8, 128], f16)
        WGs = sb("WGs", [128, 2, E])
        WGh = sb("WGh", [128, 3, E], f16)
        WS = sb("WS", [128, 2 * (2 * FS + FSM * C) + 2 * FS], f16)
        ring = sb("ring", [128, RING, WX], f16)

        def slot(R, k):
            return R[:, k * SL:(k + 1) * SL].rearrange("p (s t) -> p s t", s=NS)

        def flat(R, k, n=NS * SEG):
            return R[:, k * SL:k * SL + n]
        xt, dx = flat(R2, 0), flat(R2, 1)
        xm = [flat(R2, 2 + m) for m in range(3)]
        kp, mm, cc, aa, bb, vv, bv, er = (slot(R1, k) for k in range(8))
        rf = ring[:].rearrange("p r w -> p (r w)").bitcast(fp32)
        num, den, e1, e2, nn, wp = (slot(rf, k) for k in range(6))
        tt = cc
        yy = flat(R1, 0)
        yA, yB = yy[:, 0:T], yy[:, T:T + HT]
        yv = yy.rearrange("p (s t) -> p s t", s=NS)
        xt2 = R2[:, 0:2 * T].bitcast(f16).rearrange("p (k t) -> p k t", k=4)
        o_fs = 2 * T
        sgs = R2[:, o_fs:o_fs + FSM * 384].rearrange("p (m t) -> p m t", m=FSM)
        hsf = R2[:, o_fs + FSM * 384:o_fs + 2 * FSM * 384].rearrange("p (m t) -> p m t", m=FSM)
        hsT = R2[:, o_fs + 2 * FSM * 384:o_fs + 3 * FSM * 384].bitcast(f16).rearrange("p (x m t) -> p x m t", x=2, m=FSM)
        o = [0]

        def carve(n, dt=None):
            a = R1[:, o[0]:o[0] + n]
            o[0] += n
            return a if dt is None else a.bitcast(dt)
        sc = carve(CAP)
        scr = carve(CAP)
        gt = carve(CAP)
        eq = carve(CAP)
        cum = carve(CAP)
        zc = carve(CAP)
        slt = carve(CAP)
        af = carve(CAP)
        bf = carve(CAP)
        ai = carve(CAP, i32)
        abT = R1[0:HC, o[0]:o[0] + 256].bitcast(f16).rearrange("p (d h q) -> p d h q", d=2, h=2)
        o[0] += 256
        A1 = R1[0:HC, o[0]:o[0] + 1024].bitcast(f16).rearrange("p (g q) -> p g q", g=16)
        o[0] += 1024
        A0 = R1[0:HC, o[0]:o[0] + 1024].bitcast(f16).rearrange("p (g q) -> p g q", g=16)
        o[0] += 1024
        B1 = R1[0:HC, o[0]:o[0] + 2304].bitcast(f16).rearrange("p (g q) -> p g q", g=16)
        o[0] += 2304
        Ld = carve(E * 18)
        L1 = carve(18)
        Lr = carve(HC)
        yo = R1[0:HC, o[0]:o[0] + 4 * C].rearrange("p (b h c) -> p b h c", b=2, h=2)
        o[0] += 4 * C
        xg = R1[0:HC, o[0]:o[0] + 4 * XH].bitcast(f16).rearrange("p (b h c) -> p b h c", b=4, h=2)
        o[0] += 4 * XH
        xgi = xg.bitcast(i32)
        xgT = R1[:, o[0]:o[0] + 4 * CAP].bitcast(f16).rearrange("p (b k t) -> p b k t", b=2, k=4)
        o[0] += 4 * CAP
        raw = R1[:, o[0]:o[0] + 2 * WE].rearrange("p (b w) -> p b w", b=2)
        o[0] += 2 * WE
        assert o[0] <= NJ * T + NJ * 5 * C
        o_hid = 2 * T + 3 * FSM * 384
        sg = R2[:, o_hid:o_hid + FM * CAP].rearrange("p (m t) -> p m t", m=FM)
        hf = R2[:, o_hid + FM * CAP:o_hid + 2 * FM * CAP].rearrange("p (m t) -> p m t", m=FM)
        hT = R2[:, 0:2 * FM * CAP].bitcast(f16).rearrange("p (b x m t) -> p b x m t", b=2, x=2, m=FM)
        assert o_hid + 2 * FM * CAP <= 5 * SL
        small = sb("small", [128, 40])
        cands = sb("cands", [128, 2, 4], i32)
        flip = sb("flip", [128, 1], i32)
        trial = sb("trial", [128, ROUNDS + 1, 4], i32)
        cnt = sb("cnt", [128, 3], bf16)
        same = sb("same", [128, 128], bf16)
        before = sb("before", [128, 128], bf16)
        samef = sb("samef", [128, 2, 128])
        ids = sb("ids", [HC, 16], f16)
        emask = sb("emask", [128, E])
        amask = sb("amask", [128, 4])
        rmask = sb("rmask", [128, E, 2])
        idx = sb("idx", [HC, 2 * E], u32)
        ps = ctx.enter_context(nc.psum_tensor("ps", [128, 8, 512], fp32))

        s_kc = sem("s_kc")
        s_xw = [sem(f"s_xw{j}") for j in range(NJ)]
        s_ws = [sem(f"s_ws{j}") for j in range(NJ)]
        s_pb = sem("s_pb")
        s_ch = sem("s_ch")
        s_wa = sem("s_wa")
        s_wg = sem("s_wg")
        s_rawS = sem("s_rawS")
        s_raw = {x: [sem(f"s_raw{x}{k}") for k in range(2)] for x in "GDR"}
        s_hi = {x: sem(f"s_hi{x}") for x in "GDR"}
        s_lo = {x: sem(f"s_lo{x}") for x in "GDR"}
        s_shi = sem("s_shi")
        s_slo = sem("s_slo")
        s_xhi = sem("s_xhi")
        s_xlo2 = sem("s_xlo2")
        s_scl = sem("s_scl")
        s_tt = sem("s_tt")
        s_num = sem("s_num")
        s_nn = sem("s_nn")
        s_res = sem("s_res")
        s_bn = sem("s_bn")
        s_cross = sem("s_cross")
        s_mask = sem("s_mask")
        s_ab = sem("s_ab")
        s_a0 = sem("s_a0")
        s_a1 = [sem(f"s_a1{k}") for k in range(4)]
        s_b1 = sem("s_b1")
        s_xt2 = sem("s_xt2")
        s_xlo = sem("s_xlo")
        s_gwh = sem("s_gwh")
        s_hs = sem("s_hs")
        s_hhi = sem("s_hhi")
        s_hf = sem("s_hf")
        s_hhi_s = sem("s_hhi_s")
        s_const = sem("s_const")
        s_ones = sem("s_ones")
        s_acc = sem("s_acc")
        s_wc = sem("s_wc")
        s_xq = sem("s_xq")
        s_sq = sem("s_sq")
        s_lbp = sem("s_lbp")
        s_lb = sem("s_lb")
        s_mixp = sem("s_mixp")
        s_mixr = sem("s_mixr")
        s_tok = sem("s_tok")
        s_b = sem("s_b")
        s_var = [sem(f"s_var{k}") for k in range(3)]
        s_rs = [sem(f"s_rs{k}") for k in range(3)]
        s_pl = sem("s_pl")
        s_xn = [sem(f"s_xn{k}") for k in range(2)]
        s_tp = [sem(f"s_tp{k}") for k in range(2)]
        s_xt = [sem(f"s_xt{k}") for k in range(2)]
        s_mix = sem("s_mix")
        s_w = sem("s_w")
        s_pad = sem("s_pad")
        s_proj = sem("s_proj")
        s_ev = sem("s_ev")
        s_v = sem("s_v")
        s_arg = sem("s_arg")
        s_exp = sem("s_exp")
        s_y = sem("s_y")
        s_at = sem("s_at")
        s_gz = sem("s_gz")
        s_sl = sem("s_sl")
        s_es = sem("s_es")
        s_st = sem("s_st")
        s_est = sem("s_est")
        s_row = sem("s_row")
        s_rowd = sem("s_rowd")
        s_cnt = sem("s_cnt")
        s_tot = sem("s_tot")
        s_r = sem("s_r")
        s_rp = sem("s_rp")
        s_gu = sem("s_gu")
        s_ssg = sem("s_ssg")
        s_sh = sem("s_sh")
        s_dn = sem("s_dn")
        s_ysh = sem("s_ysh")
        s_yd = sem("s_yd")
        s_idx = sem("s_idx")
        s_xg = [sem(f"s_xg{k}") for k in range(4)]
        s_xgt = sem("s_xgt")
        s_xgs = sem("s_xgs")
        s_eg = sem("s_eg")
        s_eu = sem("s_eu")
        s_sg = sem("s_sg")
        s_h = sem("s_h")
        s_ed = sem("s_ed")
        s_yo = sem("s_yo")
        s_add = [sem(f"s_add{k}") for k in range(2)]

        block = ctx.enter_context(nc.Block())

        scores = xr[:, :, 512:XH].bitcast(fp32)

        def split_hi(a, w, to, f, d, c0=0, c1=None):
            c1 = 2 * f + d if c1 is None else c1
            return a.activation(to[:, c0:c1], w[:, c0:c1], ACT.Copy, scale=WSC)

        def split_hi_last(a, w, to, f, d, u):
            n, p = 2 * f + d, 64 * u
            return a.activation(to[p:p + 64, 2 * n + f * u:2 * n + f * u + f], w[p:p + 64, n:n + f], ACT.Copy, scale=WSC)

        def split_lo(v, w, to, f, d, c0=0, c1=None):
            n = 2 * f + d
            c1 = n if c1 is None else c1
            return v.scalar_tensor_tensor(to[:, n + c0:n + c1], w[:, c0:c1], WSC, to[:, c0:c1], ALU.mult, ALU.subtract)

        def split_lo_last(v, w, to, f, d, u):
            n, p, q = 2 * f + d, 64 * u, 64 - 64 * u
            c = 2 * n + f * u
            return v.scalar_tensor_tensor(to[q:q + 64, c:c + f], w[p:p + 64, n:n + f], WSC, to[p:p + 64, c:c + f],
                                          ALU.mult, ALU.subtract)

        shared_work = [("hidden", c) for c in range(3)]
        for n in range(1, 4):
            shared_work += [("hidden", 3 * n)] * (n < 3) + [("out", 3 * n - 3 + k) for k in range(3)]
            shared_work += [("hidden", 3 * n + k) for k in (1, 2)] * (n < 3)

        parts = {"R": (2 * F + FD, WE), "G": (0, 2 * F), "D": (2 * F, 2 * F + FD)}

        def tokcol(i):
            return i // 2, 256 * (i % 2)

        wexp = {"G": wexp_gu, "D": wexp_d, "R": wexp_last}
        ln_parts = ((0, 4), (4, NT))
        groups = ((0, 0, SA // 2), (0, SA // 2, SA), (1, SA, NS))
        second = (0, 2, 1)

        def transposed_out(copy, j):
            return copy(xt2[:, 2 * (j % 2):2 * (j % 2) + 2, 512 * (j // 2):512 * (j // 2) + 512],
                        ps[:, j, :].bitcast(f16).rearrange("p (k t) -> p k t", k=2))

        def views(s0, s1):
            return (lambda x: x[:, s0:s1, :].rearrange("p s t -> p (s t)"), lambda x: x[:, s0:s1, 1:],
                    lambda x: x[:, s0:s1, 0:SEG])

        def times_ids(eng, k):
            g4 = slice(4 * k, 4 * k + 4)
            eng.tensor_tensor(A1[:, g4, :], A0[:, g4, :], ids[:, g4].unsqueeze(2).to_broadcast([HC, 4, 128]),
                              ALU.mult).then_inc(s_a1[k], 1)

        @block.sync
        def _(sp):
            sp.dma_start(KCN[:], kconst).then_inc(s_kc, 16)
            sp.dma_start(chn[:], chan).then_inc(s_ch, 16)
            for j in range(NJ):
                sp.dma_start(Ws[:, j], wshift[:, j]).then_inc(s_ws[j], 16)
                sp.dma_start(Xs[:, j], xwin[:, j]).then_inc(s_xw[j], 16)
            sp.dma_start(pbr[:], proj_b).then_inc(s_pb, 16)
            sp.dma_start(WA[:], wattn).then_inc(s_wa, 16)
            sp.dma_start(WG[:], gate_t).then_inc(s_wg, 16)
            sp.wait_ge(s_y, 3)
            sp.dma_start(raw[:, 1, 0:3 * FS + FSM * C], wshared).then_inc(s_rawS, 16)
            for b in range(2):
                if b:
                    sp.wait_ge(s_slo, 1)
                for x, (c0, c1) in parts.items():
                    sp.dma_start(raw[:, b, c0:c1], wexp[x][b]).then_inc(s_raw[x][b], 16)
            sp.wait_ge(s_row, 1)
            sp.dma_start(xrows.rearrange("(i p) c -> p i c", p=128), XW[:].rearrange("p (i c) -> p i c", i=NT)).then_inc(s_rowd, 16)
            for n in range(3):
                sp.wait_ge(s_ysh, 3 * (n + 1))
                sp.dma_start(out[384 * n:384 * (n + 1), :].rearrange("(i p) c -> p i c", p=128),
                             h[:, 3 * n:3 * n + 3]).then_inc(s_yd, 16)
            wpair = {x: w.rearrange("(g b) p w -> g b p w", b=2) for x, w in wexp.items()}
            with sp.Fori(1, E // 2) as pair:
                for b in range(2):
                    for x, (c0, c1) in parts.items():
                        sp.wait_ge(s_lo[x], pair * 2 + (b - 1))
                        sp.dma_start(raw[:, b, c0:c1], wpair[x][ds(pair, 1), b].rearrange("a p w -> p (a w)")).then_inc(s_raw[x][b], 16)

        @block.gpsimd
        def _(pool):
            g = nc.gpsimd
            g.memset(half, -0.5)
            g.memset(ones[:], 1.0).then_inc(s_ones, 1)
            g.memset(ident[:], 1.0).then_inc(s_pl, 1)
            g.memset(samef[:], 1.0).then_inc(s_pl, 1)
            g.memset(GZ[:], 0.0).then_inc(s_pl, 1)
            pool.wait_ge(s_pl, 3)
            g.affine_select(out=ident[:], in_=ident[:], compare_op=ALU.is_equal, fill=0.0, base=0,
                            pattern=[[-1, 128]], channel_multiplier=1).then_inc(s_const, 1)
            sv = samef[:, 0, :].rearrange("p (e s) -> p e s", e=E)
            g.affine_select(out=sv, in_=sv, compare_op=ALU.is_ge, fill=0.0, base=0,
                            pattern=[[-8, E], [0, 8]], channel_multiplier=1).then_inc(s_pl, 1)
            pool.wait_ge(s_pl, 4)
            g.affine_select(out=sv, in_=sv, compare_op=ALU.is_ge, fill=0.0, base=7,
                            pattern=[[8, E], [0, 8]], channel_multiplier=-1).then_inc(s_pl, 1)
            pool.wait_ge(s_pl, 5)
            g.affine_select(out=samef[:, 1, :], in_=samef[:, 0, :], compare_op=ALU.is_gt, fill=0.0, base=0,
                            pattern=[[1, 128]], channel_multiplier=-1).then_inc(s_pl, 1)
            pool.wait_ge(s_pl, 6)
            g.tensor_copy(same[:], samef[:, 0, :])
            pool.wait_ge(s_const, 1)
            g.tensor_copy(ident16[:], ident[:])
            g.tensor_copy(before[:], samef[:, 1, :]).then_inc(s_const, 1)
            g.iota(ids[:].rearrange("p (h s) -> p h s", h=2), pattern=[[HC, 2], [CAP, 8]], base=0,
                   channel_multiplier=1, allow_small_or_imprecise_dtypes=True).then_inc(s_const, 1)
            g.memset(trial[:], 0).then_inc(s_const, 1)
            pool.wait_ge(s_const, 4)
            for b in range(ROUNDS):
                for c in range(1, 4):
                    last = g.memset(trial[:, b, c:c + 1], c << (2 * (ROUNDS - 1 - b)))
            last.then_inc(s_const, 1)
            for j in range(NJ):
                pool.wait_ge(s_lbp, j + 1)
                if j == 0:
                    g.tensor_copy(lbs, lbp[:, 0]).then_inc(s_lb, 1)
                else:
                    pool.wait_ge(s_lb, j)
                    g.tensor_tensor(lbs, lbs, lbp[:, j % 2], ALU.add).then_inc(s_lb, 1)
            g.memset(wp[:, :, 1:], 0.0)
            g.memset(wp[:, :, 0], NEG).then_inc(s_pad, 1)
            for k, (v, r) in enumerate(((ex2, rstd0), (bag[:, :, 1], rstd1), (bag[:, :, 1], rstd2))):
                if k == 2:
                    pool.wait_ge(s_gwh, 2)
                    for w in range(3):
                        for s in range(8):
                            last = g.tensor_copy(GZ[:, w, s, :].rearrange("p (e q) -> p e q", e=E)[:, :, s], WGh[:, w, :])
                    last.then_inc(s_gz, 1)
                    for n, k_ in enumerate(second):
                        q, s0, s1 = groups[k_]
                        fl, cur, prev = views(s0, s1)
                        pool.wait_ge(s_ev, 8 + 2 * k_)
                        pool.wait_ge(s_exp, 4 * n + 4)
                        g.tensor_tensor(cur(tt), cur(e2), cur(vv), ALU.mult).then_inc(s_tt, 1)
                        pool.wait_ge(s_num, n + 1)
                        g.tensor_tensor(cur(nn), cur(e1), prev(num), ALU.mult).then_inc(s_nn, 1)
                        pool.wait_ge(s_nn, 3 * n + 1)
                        pool.wait_ge(s_tt, n + 1)
                        g.tensor_tensor(cur(nn), cur(nn), cur(tt), ALU.add).then_inc(s_nn, 1)
                        pool.wait_ge(s_nn, 3 * n + 2)
                        pool.wait_ge(s_ev, 14 + 2 * k_)
                        g.tensor_tensor(cur(nn), cur(nn), cur(er), ALU.mult).then_inc(s_nn, 1)
                for j, (i0, i1) in enumerate(ln_parts):
                    pool.wait_ge(s_var[k], j + 1 if k else 1)
                    g.tensor_scalar(r[:, i0:i1], v[:, i0:i1], LN_EPS, 1.0 if k < 2 else XSC ** -2, ALU.add,
                                    ALU.mult).then_inc(s_pl, 1)
                    pool.wait_ge(s_pl, 7 + 2 * k + j)
                    g.tensor_tensor(r[:, i0:i1], r[:, i0:i1], half[:, i0:i1], ALU.pow).then_inc(s_rs[k], 1)
                if k == 0:
                    g.memset(kp[:, :, 0], NEG)
                    g.memset(mm[:, :, 0], NEG)
                    for x in (vv, aa, bv, bb):
                        last = g.memset(x[:, :, 0], 0.0)
                    last.then_inc(s_pad, 1)
                    pool.wait_ge(s_pad, 1)
                    pool.wait_ge(s_w, 1)
                    for q, (s0, s1) in enumerate(((0, SA), (SA, NS))):
                        g.tensor_scalar(wp[:, s0:s1, 1:], wp[:, s0:s1, 1:], wdec[:, q:q + 1], None,
                                        ALU.subtract).then_inc(s_pad, 1)
                if k == 1:
                    for q, (c0, c1) in enumerate(((0, T), (T, T + HT))):
                        pool.wait_ge(s_mixp, q + 1)
                        g.tensor_tensor(xm[2][:, c0:c1], xm[2][:, c0:c1], xt[:, c0:c1], ALU.add).then_inc(s_mixr, 1)
            for i in range(NT):
                pool.wait_ge(s_xhi, i + 1)
                pool.wait_ge(s_xn[1], i + 1)
                g.tensor_tensor(xr[:, i, 256 + C:512], xn[:, i, 128:C], xr[:, i, C:256], ALU.subtract).then_inc(s_xlo2, 1)

            def first_lo(x):
                pool.wait_ge(s_hi[x], 1)
                w, to, n = raw[:, 0, :], ring[:, 0, :], 2 * F + FD
                if x == "R":
                    for u in range(2):
                        p, q, c = 64 * u, 64 - 64 * u, 2 * n + F * u
                        if u:
                            pool.wait_ge(s_cross, 1)
                        last = g.tensor_tensor(to[q:q + 64, c:c + F], w[p:p + 64, n:n + F], to[p:p + 64, c:c + F],
                                               ALU.subtract)
                        if u == 0:
                            last.then_inc(s_cross, 1)
                else:
                    c0, c1 = parts[x]
                    last = g.tensor_tensor(to[:, n + c0:n + c1], w[:, c0:c1], to[:, c0:c1], ALU.subtract)
                last.then_inc(s_lo[x], 1)
                if x == "R":
                    pool.wait_ge(s_lo[x], 1)

            for c in range(3 * FSM):
                pool.wait_ge(s_hhi_s, c + 1)
                m = c % FSM
                g.tensor_tensor(hsT[:, 1, m, :], hsf[:, m, :], hsT[:, 0, m, :], ALU.subtract).then_inc(s_sh, 1)
            pool.wait_ge(s_sh, 3 * FSM)
            first_lo("R")
            first_lo("G")
            pool.wait_ge(s_a0, 1)
            for k in range(1, 4):
                times_ids(g, k)
            first_lo("D")
            pool.wait_ge(s_idx, 1)
            pool.wait_ge(s_rowd, 16)

            def gather(e):
                if e >= 4:
                    pool.wait_ge(s_yo, e - 3)
                for hh in range(2):
                    g.indirect_dma_start(xgi[:, e % 4, hh, :], None, xrows,
                                         bass.IndirectOffsetOnAxis(idx[:, 2 * e + hh:2 * e + hh + 1], 0)).then_inc(s_xg[e % 4], 16)

            def scatter(e):
                pool.wait_ge(s_yo, e + 1)
                if e:
                    pool.wait_ge(s_add[0], e * 16)
                    pool.wait_ge(s_add[1], e * 16)
                for hh in range(2):
                    g.indirect_dma_start(out, bass.IndirectOffsetOnAxis(idx[:, 2 * e + hh:2 * e + hh + 1], 0),
                                         yo[:, e % 2, hh, :], None, compute_op=ALU.add).then_inc(s_add[hh], 16)

            for e in range(3):
                gather(e)
            pool.wait_ge(s_yd, 48)
            for e in range(E):
                for q in range(2):
                    pool.wait_ge(s_hhi, 2 * e + q + 1)
                    g.tensor_tensor(hT[:, e % 2, 1, 3 * q:3 * q + 3, :], hf[:, 3 * q:3 * q + 3, :],
                                    hT[:, e % 2, 0, 3 * q:3 * q + 3, :], ALU.subtract).then_inc(s_h, 1)
                if e:
                    scatter(e - 1)
                if e + 3 < E:
                    gather(e + 3)
            scatter(E - 1)
            pool.wait_ge(s_add[0], 16 * E)
            pool.wait_ge(s_add[1], 16 * E)

        @block.scalar
        def _(act):
            a = nc.scalar
            for j in range(NJ):
                act.wait_ge(s_xw[j], 16)
                if j >= 2:
                    act.wait_ge(s_sq, j - 1)
                a.activation(Xq[:, j % 2, :], Xs[:, j, :], ACT.Square).then_inc(s_xq, 1)
                if j == 0:
                    act.wait_ge(s_kc, 16)
                act.wait_ge(s_ws[j], 16)
                if j >= 2:
                    act.wait_ge(s_lb, j - 1)
                for s in range(5):
                    last = a.activation(lbp[:, j % 2, s, :], Ws[:, j, s, :], ACT.Copy, scale=KCN[:, j, 5 + s:6 + s])
                last.then_inc(s_lbp, 1)
            act.wait_ge(s_ch, 16)
            a.activation(wdec[:], chn[:, :, 3], ACT.Exp).then_inc(s_w, 1)
            act.wait_ge(s_tp[0], 4)
            a.copy(xt[:, 0:512], ps[:, 0, :])
            a.copy(xt[0:64, T:T + 512], ps[0:64, 3, :])
            act.wait_ge(s_tp[0], 8)
            a.copy(xt[:, 512:1024], ps[:, 1, :])
            a.copy(xt[0:64, T + 512:T + HT], ps[0:64, 4, 0:64])
            a.copy(xt[64:128, T:T + 448], ps[0:64, 4, 64:512])
            act.wait_ge(s_tp[0], 9)
            a.copy(xt[:, 1024:T], ps[:, 2, 0:128]).then_inc(s_xt[0], 1)
            a.copy(xt[64:128, T + 448:T + HT], ps[0:64, 5, 0:128]).then_inc(s_xt[0], 1)
            act.wait_ge(s_mix, 5)
            for q, (c0, c1) in enumerate(((0, T), (T, T + HT))):
                a.activation(xm[2][:, c0:c1], dx[:, c0:c1], ACT.Copy, scale=mix1[:, q, 2:3]).then_inc(s_mixp, 1)
            act.wait_ge(s_pad, 4)

            def region(n):
                return ps[:, n % 8, 0:288].rearrange("p (s t) -> p s t", t=SEG)

            def keys_or_values(x, n0):
                for n in range(n0, n0 + 6):
                    q = n % 6
                    act.wait_ge(s_proj, n + 1)
                    a.copy(x[:, 8 * q:8 * q + 8, 1:SEG + 1], region(n)).then_inc(s_ev, 1)

            def exponentials(k_):
                q, s0, s1 = groups[k_]
                for k, x in enumerate((aa, bb, e1, e2)):
                    act.wait_ge(s_arg, 4 * k_ + k + 1)
                    a.activation(x[:, s0:s1, 1:], x[:, s0:s1, 1:], ACT.Exp).then_inc(s_exp, 1)

            keys_or_values(kp, 0)
            exponentials(second[0])
            keys_or_values(vv, 6)
            exponentials(second[1])
            exponentials(second[2])
            for n in range(12, 18):
                q = n % 6
                act.wait_ge(s_proj, n + 1)
                a.activation(er[:, 8 * q:8 * q + 8, 1:SEG + 1], region(n), ACT.Sigmoid).then_inc(s_ev, 1)
            a.activation(early[:], chn[:, 0, 3:4], ACT.Exp)
            for i in range(NT):
                act.wait_ge(s_xn[1], i + 1)
                a.copy(xr[:, i, 0:C], xn[:, i, :])
                a.copy(xr[:, i, C:256], xn[:, i, 128:C]).then_inc(s_xhi, 1)
            for j in (0, 2):
                act.wait_ge(s_tp[1], 4 * (j // 2 + 1))
                transposed_out(a.copy, j).then_inc(s_xt[1], 1)
            act.wait_ge(s_tp[1], NT)
            a.copy(xt2[:, :, 1024:T], ps[:, 4, 0:256].bitcast(f16).rearrange("p (k t) -> p k t", k=4)).then_inc(s_xt[1], 1)
            act.wait_ge(s_rawS, 16)
            split_hi(a, raw[:, 1, :], WS, FS, FSM * C)
            for u in range(2):
                last = split_hi_last(a, raw[:, 1, :], WS, FS, FSM * C, u)
            last.then_inc(s_shi, 1)

            def first_hi(x):
                c0, c1 = parts[x]
                act.wait_ge(s_raw[x][0], 16)
                a.activation(raw[:, 0, c0:c1], raw[:, 0, c0:c1], ACT.Copy, scale=WSC).then_inc(s_scl, 1)
                act.wait_ge(s_scl, 1 + "RGD".index(x))
                if x == "R":
                    for u in range(2):
                        p, n = 64 * u, 2 * F + FD
                        last = a.copy(ring[p:p + 64, 0, 2 * n + F * u:2 * n + F * u + F], raw[p:p + 64, 0, n:n + F])
                else:
                    last = a.copy(ring[:, 0, c0:c1], raw[:, 0, c0:c1])
                last.then_inc(s_hi[x], 1)

            act.wait_ge(s_sl, 1)
            a.activation(sc, ps[:, 6, 0:CAP], ACT.Exp, scale=-1.0 / (XSC * WSC)).then_inc(s_es, 1)
            act.wait_ge(s_st, 1)
            a.activation(scores, ps[:, 7, 0:NT * E].rearrange("p (i e) -> p i e", i=NT), ACT.Exp,
                         scale=-1.0 / (XSC * WSC)).then_inc(s_est, 1)
            for c in range(3 * FSM):
                n, m = c // FSM, c % FSM
                act.wait_ge(s_gu, c + 1)
                if n:
                    act.wait_ge(s_hs, c + 1 - FSM)
                a.activation(sgs[:, m, :], ps[:, 2 * (c % 2), 0:384], ACT.Silu, scale=1.0 / (XSC * WSC)).then_inc(s_ssg, 1)
                act.wait_ge(s_hs, c + 1)
                if n and m == 0:
                    act.wait_ge(s_dn, 3 * n)
                a.copy(hsT[:, 0, m, :], hsf[:, m, :]).then_inc(s_hhi_s, 1)
            def xg_out(b):
                a.copy(xgT[:, b, :, :], ps[:, 4, 0:2 * CAP].bitcast(f16).rearrange("p (k t) -> p k t", k=4)).then_inc(s_xgs, 1)

            for x in "RGD":
                first_hi(x)
            for x in "GDR":
                act.wait_ge(s_raw[x][1], 16)
            for x in "GD":
                split_hi(a, raw[:, 1, :], ring[:, 1, :], F, FD, *parts[x]).then_inc(s_hi[x], 1)
            split_hi_last(a, raw[:, 1, :], ring[:, 1, :], F, FD, 0)
            split_hi_last(a, raw[:, 1, :], ring[:, 1, :], F, FD, 1).then_inc(s_hi["R"], 1)
            act.wait_ge(s_xgt, 1)
            xg_out(0)

            def gates(g4, k):
                e = g4 * 4 + k
                b = k % 2
                static = isinstance(g4, int)
                ahead = not (static and e + 2 >= E)
                landed = 8 * (e - k) + 16 * (k // 2) + 32
                to = ring[:, (k + 2) % RING, :]
                for q in range(2):
                    act.wait_ge(s_eg, 2 * e + q + 1)
                    a.activation(sg[:, 3 * q:3 * q + 3, :], ps[:, q, 0:3 * CAP].rearrange("p (m t) -> p m t", m=3),
                                 ACT.Silu, scale=1.0 / (XSC * WSC)).then_inc(s_sg, 1)
                    if q == 0:
                        if ahead:
                            act.wait_ge(s_raw["R"][b], landed)
                            split_hi_last(a, raw[:, b, :], to, F, FD, 0)
                        if not (static and e < 2):
                            act.wait_ge(s_ed, e - 1)
                    act.wait_ge(s_hf, 2 * e + q + 1)
                    a.copy(hT[:, b, 0, 3 * q:3 * q + 3, :], hf[:, 3 * q:3 * q + 3, :]).then_inc(s_hhi, 1)
                    if q == 0 and ahead:
                        split_hi_last(a, raw[:, b, :], to, F, FD, 1).then_inc(s_hi["R"], 1)
                if not (static and e == E - 1):
                    act.wait_ge(s_xgt, e + 2)
                    xg_out(1 - b)
                if ahead:
                    for x in "GD":
                        act.wait_ge(s_raw[x][b], landed)
                        split_hi(a, raw[:, b, :], to, F, FD, *parts[x]).then_inc(s_hi[x], 1)

            for k in range(4):
                gates(0, k)
            with act.Fori(1, E // 4 - 1) as g4:
                for k in range(4):
                    gates(g4, k)
            for k in range(4):
                gates(E // 4 - 1, k)

        @block.vector
        def _(dve):
            v = nc.vector
            dve.wait_ge(s_kc, 16)
            v.tensor_copy(Wc[:, :, C], KCN[:, :, 10])
            for j in range(NJ):
                dve.wait_ge(s_ws[j], 16)
                v.tensor_scalar(Wc[:, j, 0:C], Ws[:, j, 0, :], KCN[:, j, 0:1], None, ALU.mult).then_inc(s_acc, 1)
                for s in range(1, 5):
                    dve.wait_ge(s_acc, 4 * j + s)
                    v.scalar_tensor_tensor(Wc[:, j, 0:C], Ws[:, j, s, :], KCN[:, j, s:s + 1], Wc[:, j, 0:C],
                                           ALU.mult, ALU.add).then_inc(s_acc if s < 4 else s_wc, 1)
                dve.wait_ge(s_xq, j + 1)
                if j == 0:
                    v.tensor_scalar(sqs, Xq[:, 0, :], KCN[:, 0, 10:11], None, ALU.mult).then_inc(s_sq, 1)
                else:
                    dve.wait_ge(s_sq, j)
                    v.scalar_tensor_tensor(sqs, Xq[:, j % 2, :], KCN[:, j, 10:11], sqs, ALU.mult,
                                           ALU.add).then_inc(s_sq, 1)
            v.memset(small[:], 0.0)
            dve.wait_ge(s_const, 1)
            v.tensor_reduce(emask[:], ident[:].rearrange("p (a e) -> p e a", e=E), AX.X, ALU.add)
            v.tensor_reduce(rmask[:], ident[:].rearrange("p (h a e) -> p e h a", h=2, a=4), AX.X, ALU.add)
            v.tensor_reduce(amask[:], ident[:].rearrange("p (h a e) -> p a h e", h=2, a=4), AX.XY, ALU.add).then_inc(s_mask, 1)
            dve.wait_ge(s_tok, 1)
            v.tensor_scalar(nmu[:, 0:8].rearrange("p (a b) -> p a b", b=2),
                            ps[:, 0:4, :].rearrange("p a (b c) -> p a b c", b=2)[:, :, :, C], -1.0 / PD, None, ALU.mult)
            v.tensor_scalar(nmu[:, 8:9], ps[:, 4, C:C + 1], -1.0 / PD, None, ALU.mult).then_inc(s_b, 1)
            v.tensor_copy(csum[:, 0, :], ps[:, 5, 0:C]).then_inc(s_b, 1)
            dve.wait_ge(s_b, 2)
            v.tensor_tensor(musq, nmu, nmu, ALU.mult).then_inc(s_b, 1)
            for i in range(NT):
                b, c = tokcol(i)
                if i == 5:
                    dve.wait_ge(s_tok, 2)
                    dve.wait_ge(s_b, 3)
                    v.scalar_tensor_tensor(ex2, ps[:, 6, 0:NT], 1.0 / PD, musq, ALU.mult, ALU.subtract).then_inc(s_var[0], 1)
                v.scalar_tensor_tensor(h[:, i, :], csum[:, 0, :], nmu[:, i:i + 1], ps[:, b, c:c + C],
                                       ALU.mult, ALU.add).then_inc(s_b, 1)
            dve.wait_ge(s_tok, 3)
            v.tensor_copy(csum[:, 1, :], ps[:, 7, 0:C]).then_inc(s_b, 1)
            dve.wait_ge(s_b, 4 + NT)

            def tile_stats(k, i):
                v.bn_stats(bst[:, i, :], h[:, i, :]).then_inc(s_bn, 1)

            def aggregate(k, i0, i1):
                for i in range(i0, i1):
                    dve.wait_ge(s_bn, NT * (k - 1) + i + 1)
                    last = v.bn_aggr(bag[:, i, :], bst[:, i, :])
                last.then_inc(s_var[k], 1)

            def normalise(k, r, j):
                dve.wait_ge(s_rs[k], j + 1)
                dve.wait_ge(s_var[k], j + 1)
                for i in range(*ln_parts[j]):
                    v.tensor_scalar(xn[:, i, 0:C], h[:, i, :], bag[:, i, 0:1], r[:, i:i + 1],
                                    ALU.subtract, ALU.mult).then_inc(s_xn[k - 1], 1)

            for j, (i0, i1) in enumerate(ln_parts):
                dve.wait_ge(s_rs[0], j + 1)
                for i in range(i0, i1):
                    v.scalar_tensor_tensor(h[:, i, :], h[:, i, :], rstd0[:, i:i + 1], csum[:, 1, :],
                                           ALU.mult, ALU.add).then_inc(s_b, 1)
                for i in range(i0, i1):
                    dve.wait_ge(s_b, 5 + NT + i)
                    tile_stats(1, i)
                aggregate(1, i0, i1)
            dve.wait_ge(s_wg, 16)
            v.tensor_scalar(WGs[:], WG[:], WSC, None, ALU.mult).then_inc(s_gwh, 1)
            dve.wait_ge(s_gwh, 1)
            v.tensor_copy(WGh[:, 0, :], WGs[:, 0, :])
            v.tensor_copy(WGh[0:64, 2, :], WGs[0:64, 1, :]).then_inc(s_mix, 1)
            dve.wait_ge(s_mix, 1)
            v.tensor_tensor(WGh[:, 1, :], WGs[:, 0, :], WGh[:, 0, :], ALU.subtract)
            v.tensor_tensor(WGh[64:128, 2, :], WGs[0:64, 1, :], WGh[0:64, 2, :], ALU.subtract).then_inc(s_gwh, 1)
            v.tensor_scalar(mix1[:], chn[:, :, 0:3], -1.0, None, ALU.add).then_inc(s_mix, 1)
            for j in range(2):
                normalise(1, rstd1, j)
            dve.wait_ge(s_xt[0], 1)
            v.tensor_tensor(dx[:, 1:T], xt[:, 1:T], xt[:, 0:T - 1], ALU.subtract).then_inc(s_mix, 1)
            dve.wait_ge(s_xt[0], 2)
            v.tensor_tensor(dx[:, T + 1:], xt[:, T + 1:], xt[:, T:NS * SEG - 1], ALU.subtract).then_inc(s_mix, 1)
            dve.wait_ge(s_mix, 4)
            v.tensor_copy(dx.rearrange("p (s t) -> p s t", t=SEG)[:, :, 0],
                          xt.rearrange("p (s t) -> p s t", t=SEG)[:, :, 0]).then_inc(s_mix, 1)
            dve.wait_ge(s_mix, 5)
            for m in range(2):
                for q, (c0, c1) in enumerate(((0, T), (T, T + HT))):
                    v.scalar_tensor_tensor(xm[m][:, c0:c1], dx[:, c0:c1], mix1[:, q, m:m + 1], xt[:, c0:c1],
                                           ALU.mult, ALU.add).then_inc(s_mix, 1)
            u = [0]

            def step(ins):
                u[0] += 1
                ins.then_inc(s_v, 1)
                dve.wait_ge(s_v, u[0])

            dve.wait_ge(s_pad, 4)
            for n, (q, s0, s1) in enumerate(groups):
                fl, cur, prev = views(s0, s1)
                dve.wait_ge(s_ev, 2 * n + 2)
                step(v.tensor_tensor_scan(fl(mm), fl(wp), fl(kp), NEG, ALU.add, ALU.max))
                v.scalar_tensor_tensor(cur(cc), prev(mm), wp[:, s0, 1:2], cur(kp), ALU.add, ALU.subtract)
                step(v.scalar_tensor_tensor(cur(nn), cur(kp), chn[:, q, 4:5], prev(mm), ALU.add, ALU.subtract))
                v.tensor_scalar(cur(aa), cur(cc), 0.0, None, ALU.min).then_inc(s_arg, 1)
                v.tensor_scalar(cur(bb), cur(cc), -1.0, 0.0, ALU.mult, ALU.min).then_inc(s_arg, 1)
                v.tensor_scalar(cur(e1), cur(nn), -1.0, 0.0, ALU.mult, ALU.min).then_inc(s_arg, 1)
                v.tensor_scalar(cur(e2), cur(nn), 0.0, None, ALU.min).then_inc(s_arg, 1)
            for n, k_ in enumerate(second):
                q, s0, s1 = groups[k_]
                fl, cur, prev = views(s0, s1)
                dve.wait_ge(s_ev, 8 + 2 * k_)
                dve.wait_ge(s_exp, 4 * n + 2)
                v.tensor_tensor(cur(bv), cur(bb), cur(vv), ALU.mult).then_inc(s_v, 1)
                step(v.tensor_tensor_scan(fl(den), fl(aa), fl(bb), 0.0, ALU.mult, ALU.add))
                u[0] += 1
                dve.wait_ge(s_v, u[0])
                v.tensor_tensor_scan(fl(num), fl(aa), fl(bv), 0.0, ALU.mult, ALU.add).then_inc(s_num, 1)
                dve.wait_ge(s_exp, 4 * n + 4)
                step(v.tensor_tensor(cur(bb), cur(e1), prev(den), ALU.mult))
                step(v.tensor_tensor(cur(bb), cur(bb), cur(e2), ALU.add))
                sm = (s0 + s1) // 2
                x, y, xy = bb[:, s0:sm, 1:], bb[:, sm:s1, 1:], mm[:, s0:sm, 1:]
                step(v.tensor_tensor(xy, x, y, ALU.mult))
                step(v.reciprocal(xy, xy))
                v.tensor_tensor(aa[:, s0:sm, 1:], xy, y, ALU.mult)
                step(v.tensor_tensor(aa[:, sm:s1, 1:], xy, x, ALU.mult))
                dve.wait_ge(s_nn, 3 * n + 3)
                v.tensor_tensor(yv[:, s0:s1, :], cur(nn), cur(aa), ALU.mult).then_inc(s_y, 1)
            for i0, i1 in ln_parts:
                for i in range(i0, i1):
                    dve.wait_ge(s_at, min(NT, i // 2 * 2 + 2))
                    v.tensor_tensor(h[:, i, :], h[:, i, :], ps[:, i // 2, 256 * (i % 2):256 * (i % 2) + C],
                                    ALU.add).then_inc(s_res, 1)
                    if i > i0:
                        dve.wait_ge(s_res, i)
                        tile_stats(2, i - 1)
                dve.wait_ge(s_res, i1)
                tile_stats(2, i1 - 1)
                aggregate(2, i0, i1)
            for j, (i0, i1) in enumerate(ln_parts):
                normalise(2, rstd2, j)
                for i in range(i0, i1):
                    dve.wait_ge(s_xhi, i + 1)
                    v.tensor_tensor(xr[:, i, 256:256 + C], xn[:, i, :], xr[:, i, 0:C], ALU.subtract).then_inc(s_xlo, 1)
            for j in (1, 3):
                dve.wait_ge(s_tp[1], 4 * (j // 2 + 1))
                transposed_out(v.tensor_copy, j).then_inc(s_xt2, 1)
            dve.wait_ge(s_shi, 1)
            split_lo(v, raw[:, 1, :], WS, FS, FSM * C)
            for u in range(2):
                last = split_lo_last(v, raw[:, 1, :], WS, FS, FSM * C, u)
            last.then_inc(s_slo, 1)

            def expert_lo(x, e, slot_, b):
                dve.wait_ge(s_hi[x], e + 1)
                if isinstance(e, int) and e == 1:
                    dve.wait_ge(s_lo[x], 1)
                if x == "R":
                    split_lo_last(v, raw[:, b, :], ring[:, slot_, :], F, FD, 0)
                    last = split_lo_last(v, raw[:, b, :], ring[:, slot_, :], F, FD, 1)
                else:
                    last = split_lo(v, raw[:, b, :], ring[:, slot_, :], F, FD, *parts[x])
                last.then_inc(s_lo[x], 1)

            r = [0]

            def rs(ins):
                r[0] += 1
                ins.then_inc(s_r, 1)
                dve.wait_ge(s_r, r[0])

            dve.wait_ge(s_es, 1)
            rs(v.tensor_scalar(sc, sc, 1.0, None, ALU.add))
            rs(v.reciprocal(sc, sc))

            dve.wait_ge(s_const, 5)
            v.memset(zc, 1.0)
            rs(v.tensor_copy(cands[:, 0, :], trial[:, 0, :]))

            def count(b):
                for c, to in enumerate((scr, gt, eq)):
                    last = v.tensor_scalar(to, sc, cands[:, b % 2, c + 1:c + 2].bitcast(fp32), None, ALU.is_ge, ALU.add,
                                           accum_out=cnt[:, c:c + 1])
                last.then_inc(s_cnt, 1)

            def decide(b):
                dve.wait_ge(s_tot, b + 1)
                rs(v.tensor_scalar(small[:, 4:7], ps[:, 7, 256:259], CAP - 0.5, None, ALU.is_ge, ALU.add,
                                   accum_out=small[:, 7:8]))
                rs(v.tensor_scalar(flip[:], small[:, 7:8], float(1 << (2 * (ROUNDS - 1 - b))), None, ALU.mult))
                rs(v.scalar_tensor_tensor(cands[:, (b + 1) % 2, :], trial[:, b + 1, :], flip[:, 0:1],
                                          cands[:, b % 2, 0:1].to_broadcast([128, 4]), ALU.bitwise_xor, ALU.bitwise_xor))

            def shared_up(c):
                n, m = c // FSM, c % FSM
                dve.wait_ge(s_ssg, c + 1)
                if n:
                    dve.wait_ge(s_sh, c + 1 - FSM)
                v.scalar_tensor_tensor(hsf[:, m, :], ps[:, 2 * (c % 2) + 1, 0:384], 1.0 / WSC, sgs[:, m, :],
                                       ALU.mult, ALU.mult).then_inc(s_hs, 1)

            def shared_out(i):
                dve.wait_ge(s_dn, i + 1)
                v.scalar_tensor_tensor(h[:, i, :], ps[:, 4 + i % 2, 0:C], 1.0 / (XSC * WSC), h[:, i, :],
                                       ALU.mult, ALU.add).then_inc(s_ysh, 1)

            def rank_above():
                thr = cands[:, ROUNDS % 2, 0:1].bitcast(fp32)
                v.tensor_scalar(gt, sc, thr, None, ALU.is_gt, ALU.add, accum_out=cnt[:, 0:1])
                v.tensor_scalar(eq, sc, thr, None, ALU.is_equal, ALU.add, accum_out=cnt[:, 1:2]).then_inc(s_cnt, 1)
                dve.wait_ge(s_cnt, ROUNDS + 1)
                rs(v.tensor_tensor_scan(cum, zc, eq, 0.0, ALU.mult, ALU.add))

            def rank_chosen():
                dve.wait_ge(s_rp, 1)
                v.tensor_scalar(small[:, 0:1], ps[:, 7, 260:261], -1.0, float(CAP), ALU.mult, ALU.add)
                rs(v.tensor_copy(small[:, 1:2], ps[:, 7, 261:262]))
                rs(v.tensor_scalar(cum, cum, small[:, 1:2], small[:, 0:1], ALU.add, ALU.is_le))
                rs(v.tensor_tensor(eq, eq, cum, ALU.mult))
                rs(v.tensor_tensor(gt, gt, eq, ALU.add))
                rs(v.tensor_tensor_scan(cum, zc, gt, 0.0, ALU.mult, ALU.add))
                v.tensor_copy(cnt[:, 0:1], cum[:, CAP - 1:CAP]).then_inc(s_cnt, 1)

            def place():
                dve.wait_ge(s_rp, 2)
                rs(v.tensor_copy(small[:, 2:3], ps[:, 7, 262:263]))
                rs(v.scalar_tensor_tensor(slt, cum, small[:, 2:3], gt, ALU.add, ALU.mult))
                rs(v.tensor_scalar(ai, slt, 1.0 / 18, -9.5 / 18, ALU.mult, ALU.add))
                rs(v.tensor_copy(af, ai))
                v.scalar_tensor_tensor(bf, af, -18.0, slt, ALU.mult, ALU.add).then_inc(s_cnt, 1)

            count(0)
            for b, (kind, i) in enumerate(shared_work):
                if b < ROUNDS:
                    decide(b)
                    if b + 1 < ROUNDS:
                        count(b + 1)
                if b == ROUNDS:
                    rank_above()
                    rank_chosen()
                if b == ROUNDS + 1:
                    place()
                if kind == "hidden":
                    shared_up(i)
                else:
                    shared_out(i)
                if b == 2:
                    dve.wait_ge(s_est, 1)
                    rs(v.tensor_scalar(scores, scores, 1.0, None, ALU.add))
                    v.reciprocal(scores, scores).then_inc(s_row, 1)
            dve.wait_ge(s_rp, 3)
            v.tensor_copy(abT.rearrange("p d h (s e) -> p (d h) s e", s=8),
                          ps[0:HC, 6, :].rearrange("p (x e s) -> p x s e", x=4, e=E)).then_inc(s_ab, 1)
            dve.wait_ge(s_ab, 1)
            digit = abT.rearrange("p d h (s e) -> p d (h s) e", s=8)
            for a_ in range(8):
                last = v.tensor_scalar(A0[:, :, E * a_:E * a_ + E], digit[:, 0], float(a_), None, ALU.is_equal)
            last.then_inc(s_a0, 1)
            dve.wait_ge(s_a0, 1)
            times_ids(v, 0)
            for hh in range(2):
                for b_ in range(18):
                    last = v.tensor_scalar(B1[:, 8 * hh:8 * hh + 8, E * b_:E * b_ + E], digit[:, 1, 8 * hh:8 * hh + 8],
                                           float(b_ + 1), None, ALU.is_equal)
                last.then_inc(s_b1, 1)
            dve.wait_ge(s_rp, 4)
            dve.wait_ge(s_mask, 1)
            rs(v.tensor_tensor(Ld.rearrange("p (b e) -> p b e", e=E), ps[:, 6, 0:E * 18].rearrange("p (b e) -> p b e", e=E),
                               emask[:].unsqueeze(1).to_broadcast([128, 18, E]), ALU.mult))
            rs(v.tensor_reduce(L1, Ld.rearrange("p (b e) -> p b e", e=E), AX.X, ALU.add))
            v.tensor_tensor(Lr.rearrange("p (a b) -> p a b", a=4), L1.unsqueeze(1).to_broadcast([128, 4, 18]),
                            amask[:].unsqueeze(2).to_broadcast([128, 4, 18]), ALU.mult).then_inc(s_cnt, 1)
            dve.wait_ge(s_rp, 5)
            v.tensor_copy(idx[:], ps[0:HC, 7, 320:320 + 2 * E]).then_inc(s_idx, 1)
            def outputs(g4, k):
                e = g4 * 4 + k
                dve.wait_ge(s_ed, e + 1)
                if not (isinstance(g4, int) and e < 2):
                    dve.wait_ge(s_add[0], (e - 1) * 16)
                    dve.wait_ge(s_add[1], (e - 1) * 16)
                for hh in range(2):
                    last = v.tensor_scalar(yo[:, k % 2, hh, :], ps[0:HC, 5 + k % 2, 256 * hh:256 * hh + C],
                                           xg[:, k, hh, 512:XH].bitcast(fp32)[:, ds(e, 1)], 1.0 / (XSC * WSC),
                                           ALU.mult, ALU.mult)
                last.then_inc(s_yo, 1)

            def hidden(g4, k):
                e = g4 * 4 + k
                ahead = not (isinstance(g4, int) and e + 1 >= E)
                nxt = (e + 1, (k + 1) % RING, (k + 1) % 2)
                if ahead:
                    expert_lo("R", *nxt)
                for q in range(2):
                    dve.wait_ge(s_sg, 2 * e + q + 1)
                    dve.wait_ge(s_eu, 2 * e + q + 1)
                    if not (isinstance(g4, int) and e == 0):
                        dve.wait_ge(s_h, 2 * e + q - 1)
                    v.scalar_tensor_tensor(hf[:, 3 * q:3 * q + 3, :], ps[:, 2 + q, 0:3 * CAP].rearrange("p (m t) -> p m t", m=3),
                                           1.0 / WSC, sg[:, 3 * q:3 * q + 3, :], ALU.mult, ALU.mult).then_inc(s_hf, 1)
                    if ahead:
                        expert_lo("GD"[q], *nxt)

            def group(g4):
                for k in range(4):
                    hidden(g4, k)
                    if not (isinstance(g4, int) and g4 == 0 and k == 0):
                        outputs(g4 if k else g4 - 1, (k + 3) % 4)
            group(0)
            with dve.Fori(1, E // 4 - 1) as g4:
                group(g4)
            group(E // 4 - 1)
            outputs(E // 4 - 1, 3)

        @block.tensor
        def _(pe):
            t = nc.tensor
            pe.wait_ge(s_kc, 16)
            pe.wait_ge(s_ones, 1)
            for j in range(NJ):
                pe.wait_ge(s_ws[j], 16)
                pe.wait_ge(s_xw[j], 16)
                pe.wait_ge(s_wc, j + 1)
                t.matmul(ps[:, 5, 0:C], ones[0:KC, :], Wc[:, j, 0:C], start=(j == 0), stop=(j == NJ - 1),
                         skip_group_check=True)
                for i in range(NT):
                    b, c = tokcol(i)
                    last = t.matmul(ps[:, b, c:c + C + 1], Xs[:, j, 128 * i:128 * i + 128], Wc[:, j, :],
                                    start=(j == 0 and c == 0), stop=(j == NJ - 1), skip_group_check=True)
            last.then_inc(s_tok, 1)
            pe.wait_ge(s_sq, NJ)
            for i in range(NT):
                last = t.matmul(ps[:, 6, i:i + 1], sqs[:, 128 * i:128 * i + 128], ones[0:KC, 0:1],
                                start=(i == 0), stop=(i == NT - 1), skip_group_check=True)
            last.then_inc(s_tok, 1)
            pe.wait_ge(s_lb, NJ)
            for s in range(5):
                t.matmul(ps[:, 7, 0:C], ones[0:KC, :], lbs[:, s, :], start=(s == 0), stop=False)
            pe.wait_ge(s_pb, 16)
            t.matmul(ps[:, 7, 0:C], ones[0:1, :], pbr[0:1, :], start=False, stop=True).then_inc(s_tok, 1)

            for i in range(NT):
                if i == 0:
                    pe.wait_ge(s_const, 1)
                pe.wait_ge(s_xn[0], i + 1)
                t.transpose(ps[:, i // 4, 128 * (i % 4):128 * (i % 4) + 128], xn[:, i, 0:128], ident[:])
                last = t.transpose(ps[0:64, 3 + i // 4, 128 * (i % 4):128 * (i % 4) + 128], xn[:, i, 128:C], ident[:])
                last.then_inc(s_tp[0], 1)
            pe.wait_ge(s_wa, 16)
            pe.wait_ge(s_xt[0], 2)
            for n in range(0, 18, 2):
                m, q = n // 6, n % 6
                if n >= 8:
                    pe.wait_ge(s_ev, n - 6)
                if m < 2:
                    pe.wait_ge(s_mix, 5 + 2 * (m + 1))
                else:
                    pe.wait_ge(s_mixr, 2)
                low, high = ps[:, n % 8, 0:288], ps[:, n % 8 + 1, 0:288]
                if q < 4:
                    hf = q // 2
                    for k, o_ in enumerate((low, high)):
                        c = 288 * (q + k)
                        t.matmul(o_, WA[:, m, 0:128], xm[m][:, c:c + 288], start=True, stop=False)
                    for k, o_ in enumerate((low, high)):
                        t.matmul(o_, WA[64 * hf:64 * hf + 64, 4 + m, 0:128],
                                 xm[m][64 * hf:64 * hf + 64, T + 288 * k:T + 288 * k + 288],
                                 start=False, stop=True).then_inc(s_proj, 1)
                else:
                    for k, o_ in enumerate((low, high)):
                        for hf in range(2):
                            c = HT * hf + 288 * k
                            t.matmul(o_[64 * hf:64 * hf + 64], WA[:, m, 128:C], xm[m][:, c:c + 288], start=True, stop=False)
                        for hf in range(2):
                            last = t.matmul(o_[64 * hf:64 * hf + 64], WA[64 * hf:64 * hf + 64, 4 + m, 128:C],
                                            xm[m][64 * hf:64 * hf + 64, T + 288 * k:T + 288 * k + 288],
                                            start=False, stop=True)
                        last.then_inc(s_proj, 1)
            pe.wait_ge(s_ev, 18)
            def main_channels(i, first):
                b, c = tokcol(i)
                return t.matmul(ps[:, b, c:c + C], yA[:, 128 * i:128 * i + 128], WA[:, 3, :],
                                start=(first and c == 0), stop=not first, skip_group_check=True)

            whole = HT // 128
            pe.wait_ge(s_y, 1)
            for i in range(whole):
                main_channels(i, True)
            pe.wait_ge(s_y, 2)
            for i in range(NT):
                b, c = tokcol(i)
                pieces = ([(0, 128, 0, 128 * i)] if i < 4 else [(0, 64, 0, 512), (64, 128, 64, 0)] if i == 4
                          else [(0, 128, 64, 128 * i - HT)])
                for p0, p1, k0, c0 in pieces:
                    last = t.matmul(ps[p0:p1, b, c:c + C], yB[k0:k0 + 64, c0:c0 + p1 - p0], WA[k0:k0 + 64, 7, :],
                                    start=(i >= whole and c == 0), stop=(i < whole), skip_group_check=True)
                if i < whole:
                    last.then_inc(s_at, 1)
            pe.wait_ge(s_y, 3)
            for i in range(whole, NT):
                main_channels(i, False).then_inc(s_at, 1)
            pe.wait_ge(s_const, 2)
            for i in range(NT):
                pe.wait_ge(s_xhi, i + 1)
                pe.wait_ge(s_xlo, i + 1)
                pe.wait_ge(s_xlo2, i + 1)
                for k in range(4):
                    c = 256 * (k % 2) + 64 * (i % 4)
                    to = ps[:, 2 * (i // 4) + k // 2, c:c + 64] if i < 8 else ps[:, 4, 64 * k:64 * k + 64]
                    last = t.transpose(to.bitcast(f16), xr[:, i, 128 * k:128 * k + 128], ident16[:])
                last.then_inc(s_tp[1], 1)
            pe.wait_ge(s_gz, 1)
            terms = ((0, 0), (1, 0), (0, 2), (2, 1), (2, 3))
            for s in range(8):
                pe.wait_ge(s_xt[1], (CAP * (s + 1) - 1) // 512 + 1)
                pe.wait_ge(s_xt2, min(2, (CAP * (s + 1) - 1) // 512 + 1))
                for x, (w, k) in enumerate(terms):
                    last = t.matmul(ps[:, 6, 0:CAP], GZ[:, w, s, :], xt2[:, k, CAP * s:CAP * s + CAP],
                                    start=(s == 0 and x == 0), stop=(s == 7 and x == 4))
            last.then_inc(s_sl, 1)
            for i in range(NT):
                for x, (w, k) in enumerate(terms):
                    last = t.matmul(ps[:, 7, E * i:E * i + E], xt2[:, k, 128 * i:128 * i + 128], WGh[:, w, :],
                                    start=(x == 0), stop=(x == 4))
            last.then_inc(s_st, 1)
            pe.wait_ge(s_est, 1)
            pe.wait_ge(s_slo, 1)

            def split_product(o_, W, f, d, w, m, x):
                n = 2 * f + d
                hi = f * w + 128 * m
                last_ch = 2 * n + f * w + 128 * m
                for y, (c, k) in enumerate(((hi, 0), (n + hi, 0), (hi, 2), (last_ch, 1), (last_ch, 3))):
                    last = t.matmul(o_, W[:, c:c + 128], x[k], start=(y == 0), stop=(y == 4))
                return last

            def total(b):
                pe.wait_ge(s_cnt, b + 1)
                t.matmul(ps[:, 7, 256:259], same[:], cnt[:, 0:3], start=True, stop=True).then_inc(s_tot, 1)

            def above():
                pe.wait_ge(s_cnt, ROUNDS + 1)
                t.matmul(ps[:, 7, 260:261], same[:], cnt[:, 0:1], start=True, stop=True)
                t.matmul(ps[:, 7, 261:262], before[:], cnt[:, 1:2], start=True, stop=True).then_inc(s_rp, 1)

            for b, (kind, i) in enumerate(shared_work):
                if b == ROUNDS:
                    above()
                if kind == "hidden":
                    n, m = i // FSM, i % FSM
                    if i >= 2:
                        pe.wait_ge(s_hs, i - 1)
                    for w in range(2):
                        last = split_product(ps[:, 2 * (i % 2) + w, 0:384], WS, FS, FSM * C, w, m,
                                             [xt2[:, k, 384 * n:384 * n + 384] for k in range(4)])
                    last.then_inc(s_gu, 1)
                else:
                    pe.wait_ge(s_sh, FSM * (i // 3 + 1))
                    if i >= 2:
                        pe.wait_ge(s_ysh, i - 1)
                    k = i % 3
                    for m in range(FSM):
                        for y, (x, w) in enumerate(((0, 0), (0, 1), (1, 0))):
                            c = (2 * FS + FSM * C) * w + 2 * FS + C * m
                            last = t.matmul(ps[:, 4 + i % 2, 0:C], hsT[:, x, m, 128 * k:128 * k + 128], WS[:, c:c + C],
                                            start=(m == 0 and y == 0), stop=(m == FSM - 1 and y == 2))
                    last.then_inc(s_dn, 1)
                if b < ROUNDS:
                    total(b)
                if b == ROUNDS:
                    pe.wait_ge(s_cnt, ROUNDS + 2)
                    t.matmul(ps[:, 7, 262:263], before[:], cnt[:, 0:1], start=True, stop=True).then_inc(s_rp, 1)
            pe.wait_ge(s_cnt, ROUNDS + 3)
            for d, x in enumerate((af, bf)):
                for hh in range(2):
                    last = t.transpose(ps[0:HC, 6, 256 * d + 128 * hh:256 * d + 128 * hh + 128],
                                       x[:, HC * hh:HC * hh + HC], ident[:])
            last.then_inc(s_rp, 1)
            pe.wait_ge(s_const, 3)
            for g_ in range(16):
                pe.wait_ge(s_a1[g_ // 4], 1)
                pe.wait_ge(s_b1, g_ // 8 + 1)
                last = t.matmul(ps[:, 6, 0:E * 18], A1[:, g_, :], B1[:, g_, :], start=(g_ == 0), stop=(g_ == 15))
            last.then_inc(s_rp, 1)
            pe.wait_ge(s_cnt, ROUNDS + 4)
            pe.wait_ge(s_mask, 1)
            t.matmul(ps[0:HC, 7, 320:320 + 2 * E], Lr, rmask[:].rearrange("p e h -> p (e h)"), start=True,
                     stop=True).then_inc(s_rp, 1)

            def xg_in(k):
                for hh in range(2):
                    for x in range(4):
                        o_ = ps[:, 4, HC * x + HC // 2 * hh:HC * x + HC // 2 * hh + HC // 2]
                        last = t.transpose(o_.bitcast(f16), xg[:, k, hh, 128 * x:128 * x + 128], ident16[0:HC, 0:HC])
                last.then_inc(s_xgt, 1)

            def up(g4, k):
                e = g4 * 4 + k
                b = k % 2
                pe.wait_ge(s_lo["G"], e + 1)
                pe.wait_ge(s_lo["R"], e + 1)
                pe.wait_ge(s_xgs, e + 1)
                for q in range(2):
                    if not (isinstance(g4, int) and e == 0):
                        pe.wait_ge(s_hf, 2 * e + q - 1)
                    for w in range(2):
                        for m in range(3 * q, 3 * q + 3):
                            o_ = ps[:, 2 * w + q, CAP * (m - 3 * q):CAP * (m - 3 * q) + CAP]
                            last = split_product(o_, ring[:, k, :], F, FD, w, m, [xgT[:, b, x, :] for x in range(4)])
                        last.then_inc(s_eg if w == 0 else s_eu, 1)
                if not (isinstance(g4, int) and e == E - 1):
                    pe.wait_ge(s_xg[(k + 1) % 4], g4 * 32 + 32 * ((k + 1) // 4 + 1))
                    xg_in((k + 1) % 4)

            def down(g4, k):
                e = g4 * 4 + k
                pe.wait_ge(s_h, 2 * e + 2)
                pe.wait_ge(s_lo["D"], e + 1)
                if not (isinstance(g4, int) and e < 2):
                    pe.wait_ge(s_yo, e - 1)
                for hh in range(2):
                    for m in range(FM):
                        for y, (x, w) in enumerate(((0, 0), (0, 1), (1, 0))):
                            c = (2 * F + FD) * w + 2 * F + C * m
                            last = t.matmul(ps[0:HC, 5 + k % 2, 256 * hh:256 * hh + C],
                                            hT[:, k % 2, x, m, HC * hh:HC * hh + HC], ring[:, k, c:c + C],
                                            start=(m == 0 and y == 0), stop=(m == FM - 1 and y == 2))
                last.then_inc(s_ed, 1)

            def group(g4):
                for k in range(4):
                    up(g4, k)
                    if not (isinstance(g4, int) and g4 == 0 and k == 0):
                        down(g4 if k else g4 - 1, (k + 3) % 4)

            pe.wait_ge(s_xg[0], 32)
            xg_in(0)
            group(0)
            with pe.Fori(1, E // 4 - 1) as g4:
                group(g4)
            group(E // 4 - 1)
            down(E // 4 - 1, 3)


def kernel(**inputs):
    import numpy as _np
    import concourse.bacc as _bacc
    from concourse import mybir as _mybir
    from concourse.bass_utils import run_bass_kernel_spmd as _run

    src = {k: _np.asarray(v) for k, v in inputs.items()}
    W2 = PATCH + 2
    pix = [(c, r, s) for c in range(CH) for r in range(W2) for s in range(W2)
           if not (r in (0, W2 - 1) and s in (0, W2 - 1))]
    pc, pr, pw = (_np.array([p[k] for p in pix]) for k in range(3))
    xp = _np.pad(src["x"], ((0, 0), (0, 0), (1, 1), (1, 1)))
    n = HW // PATCH
    rows = pr[None, :] + PATCH * _np.arange(n)[:, None]
    cols = pw[None, :] + PATCH * _np.arange(n)[:, None]
    win = xp[:, pc[None, None, :], rows[:, None, :], cols[None, :, :]]
    xwin = win.reshape(T, NJ, KC).transpose(2, 1, 0)
    places = ((1, 1), (1, 0), (1, 2), (0, 1), (2, 1))

    def in_window(a):
        w = a.reshape(PATCH, PATCH, 5, CH, -1)
        full = _np.zeros((5, CH, W2, W2, w.shape[-1]), a.dtype)
        for s, (r, c) in enumerate(places):
            full[s, :, r:r + PATCH, c:c + PATCH] = w[:, :, s].transpose(2, 0, 1, 3)
        return full[:, pc, pr, pw].reshape(5, NJ, KC, -1).transpose(2, 1, 0, 3)

    wshift = in_window(src["L0_tok_proj_weight"].T)
    lnw = in_window(src["L0_tok_ln_weight"])[..., 0]
    lnb = in_window(src["L0_tok_ln_bias"])[..., 0]
    times = _np.zeros((CH, W2, W2), _np.float32)
    for r, c in places:
        times[:, r:r + PATCH, c:c + PATCH] += 1
    times = times[pc, pr, pw].reshape(NJ, KC).T[:, :, None]
    kconst = _np.concatenate([lnw, lnb, times], axis=2)
    chan = _np.stack([src["L0_attn_" + k] for k in ("mix_k", "mix_v", "mix_r", "time_decay", "time_first")], axis=1)
    chan = _np.stack([chan[:128], _np.concatenate([chan[128:]] * 2)], axis=1)
    wt = [src["L0_attn_W" + k].T for k in "kvro"]
    wattn = _np.stack([w[:128] for w in wt] + [_np.concatenate([w[128:]] * 2) for w in wt], axis=1)
    gt = src["L0_ffn_gate_weight"].T
    gate_t = _np.stack([gt[:128], _np.concatenate([gt[128:]] * 2)], axis=1)

    def ffn(g, u, d):
        g, u, d = (_np.swapaxes(x, -1, -2) for x in (g, u, d))
        d = d.reshape(d.shape[:-2] + (-1, 128, C))
        d = _np.swapaxes(d, -3, -2).reshape(d.shape[:-3] + (128, -1))
        low = _np.concatenate([g[..., 128:, :], u[..., 128:, :]], axis=-2)
        return _np.concatenate([g[..., :128, :], u[..., :128, :], d, low], axis=-1)

    wshared = ffn(*(src["L0_ffn_Ws_" + k] for k in "gud"))
    wexp = ffn(*(src["L0_ffn_W" + k] for k in "gud"))
    given = {"xwin": xwin, "wshift": wshift, "kconst": kconst, "proj_b": src["L0_tok_proj_bias"][None, :],
             "chan": chan, "wattn": wattn, "gate_t": gate_t, "wshared": wshared,
             "wexp_gu": wexp[..., :2 * F], "wexp_d": wexp[..., 2 * F:-F], "wexp_last": wexp[..., -F:]}
    nc = _bacc.Bacc("TRN2", target_bir_lowering=False, num_devices=1)
    arrays, args = {}, []
    for name, a in given.items():
        a = _np.ascontiguousarray(a)
        arrays[f"in_{name}"] = a
        args.append(nc.dram_tensor(f"in_{name}", a.shape, _mybir.dt.from_np(a.dtype), kind="ExternalInput").ap())
    args.append(nc.dram_tensor("out_h", (T, C), _mybir.dt.float32, kind="ExternalOutput").ap())
    vit_tower_kernel(nc, *args)
    r = _run(nc, [arrays], core_ids=[0])
    return r.results[0]["out_h"].reshape(B, SEG, C)
```
